# Optimizing a Trainium2 kernel written in Bass

```python
import numpy as np
import jax
import jax.numpy as jnp

def _softmax(x, axis=-1):
    return jax.nn.softmax(x, axis=axis)

def _gelu(x):
    return jax.nn.gelu(x, approximate=True)

def _silu(x):
    return jax.nn.silu(x)

def _sigmoid(x):
    return jax.nn.sigmoid(x)

def _layernorm(x, axis=-1, eps=1e-05):
    m = jnp.mean(x, axis=axis, keepdims=True)
    v = jnp.var(x, axis=axis, keepdims=True)
    return (x - m) / jnp.sqrt(v + eps)

def _scatter_add(tgt, idx, src, axis=0):
    return tgt.at[idx].add(src)

def _segment_sum(src, seg, n):
    return jax.ops.segment_sum(src, seg, n)
kernel_name = 'mk_adj_ffn_d2_adj_r2_6bbaa2'

def setup_inputs(seed: int=0):
    np.random.seed(seed)
    _w = jnp.asarray

    def _rec_inputs():
        import jax
        import jax.numpy as jnp
        _gk = jax.random.key(seed)
        x = -0.0005207 + 1.001 * jax.random.normal(jax.random.fold_in(_gk, 1), (128, 128, 128), jnp.float32)
        _w = (1.0 + jnp.arange(128, dtype=jnp.float32)) ** (-0.5)
        _w = _w / _w.mean()
        _pij = jnp.clip(0.125 * _w[:, None] * _w[None, :], 0.0, 1.0)
        _a = jax.random.uniform(jax.random.fold_in(_gk, 2), (128, 128, 128)) < _pij
        adj = _a.astype(jnp.int32)
        return (x, adj)
    x, adj = _rec_inputs()

    def _L0_gnn_setup():
        import jax, jax.numpy as jnp
        import numpy as np
        B, N, F_IN, F_OUT = (1, 4096, 128, 128)
        ALPHA = 0.2
        NEG_INF = -9000000000000000.0
        key = jax.random.key(seed)
        ks = jax.random.split(key, 8)
        feat = jax.random.normal(ks[0], (B, N, F_IN), dtype=jnp.float32)
        adj = jax.random.randint(ks[1], (B, N, N), 0, 2, dtype=jnp.int32)
        s = 1.414 * (6.0 / (F_IN + F_OUT)) ** 0.5
        W = jax.random.uniform(ks[2], (F_IN, F_OUT), minval=-s, maxval=s, dtype=jnp.float32)
        a_1 = jax.random.normal(ks[3], (F_OUT, 1), dtype=jnp.float32) * 0.1
        a_2 = jax.random.normal(ks[4], (F_OUT, 1), dtype=jnp.float32) * 0.1
        a_12 = jax.random.normal(ks[5], (F_OUT, F_OUT), dtype=jnp.float32) * (1.0 / F_OUT ** 0.5)
        W_1 = jax.random.uniform(ks[6], (F_IN, F_OUT), minval=-s, maxval=s, dtype=jnp.float32)
        W_2 = jax.random.uniform(ks[7], (F_IN, F_OUT), minval=-s, maxval=s, dtype=jnp.float32)
        return {'feat': feat, 'adj': adj, 'W': W, 'a_1': a_1, 'a_2': a_2, 'a_12': a_12, 'W_1': W_1, 'W_2': W_2}
    _L0_gnn_all = _L0_gnn_setup()
    _L0_gnn_in = {k: v for k, v in _L0_gnn_all.items() if k in ('W', 'a_1', 'a_2', 'a_12', 'W_1', 'W_2')}
    del _L0_gnn_all

    def _L0_ffn_setup():
        import jax, jax.numpy as jnp
        import numpy as np
        IN_CH = 128
        OUT_CH = 128
        key = jax.random.key(seed)
        kx, kw, kb = jax.random.split(key, 3)
        x = jax.random.normal(kx, (8, 2048, IN_CH), dtype=jnp.float32)
        bound = 1.0 / np.sqrt(IN_CH)
        weight = jax.random.uniform(kw, (OUT_CH, IN_CH), dtype=jnp.float32, minval=-bound, maxval=bound)
        bias = jax.random.uniform(kb, (OUT_CH,), dtype=jnp.float32, minval=-bound, maxval=bound)
        return {'x': x, 'weight': weight, 'bias': bias}
    _L0_ffn_all = _L0_ffn_setup()
    _L0_ffn_in = {k: v for k, v in _L0_ffn_all.items() if k in ('weight', 'bias')}
    del _L0_ffn_all

    def _L1_gnn_setup():
        import jax, jax.numpy as jnp
        import numpy as np
        NEG_BIG = -9000000000000000.0
        key = jax.random.key(seed)
        k1, k2, k3, k4 = jax.random.split(key, 4)
        B, N, F_in, F_out = (4, 2048, 128, 128)
        h = jax.random.normal(k1, (B, N, F_in), dtype=jnp.float32)
        adj = jax.random.randint(k2, (B, N, N), 0, 2, dtype=jnp.int32)
        bW = 1.414 * np.sqrt(6.0 / (F_in + F_out))
        W = jax.random.uniform(k3, (F_in, F_out), minval=-bW, maxval=bW, dtype=jnp.float32)
        ba = 1.414 * np.sqrt(6.0 / (2 * F_out + 1))
        a = jax.random.uniform(k4, (2 * F_out, 1), minval=-ba, maxval=ba, dtype=jnp.float32)
        return {'h': h, 'adj': adj, 'W': W, 'a': a}
    _L1_gnn_all = _L1_gnn_setup()
    _L1_gnn_in = {k: v for k, v in _L1_gnn_all.items() if k in ('W', 'a')}
    del _L1_gnn_all

    def _L1_ffn_setup():
        import math
        import jax, jax.numpy as jnp
        import numpy as np
        CAPACITY_FACTOR = 1.25
        TOP_K = 2
        LN_EPS = 1e-05

        def _layer_norm(x, gamma, beta):
            mu = jnp.mean(x, axis=-1, keepdims=True)
            var = jnp.var(x, axis=-1, keepdims=True)
            return (x - mu) * jax.lax.rsqrt(var + LN_EPS) * gamma + beta
        key = jax.random.key(seed)
        ks = jax.random.split(key, 4)
        B, S, D, F, E = (8, 2048, 128, 256, 8)
        x = jax.random.normal(ks[0], (B, S, D), dtype=jnp.float32)
        Wr = jax.random.normal(ks[1], (D, E), dtype=jnp.float32) / np.sqrt(D)
        br = jnp.zeros((E,), jnp.float32)
        W1 = jax.random.normal(ks[2], (E, D, F), dtype=jnp.float32) / np.sqrt(D)
        b1 = jnp.zeros((E, F), jnp.float32)
        W2 = jax.random.normal(ks[3], (E, F, D), dtype=jnp.float32) / np.sqrt(F)
        b2 = jnp.zeros((E, D), jnp.float32)
        gamma = jnp.ones((D,), jnp.float32)
        beta = jnp.zeros((D,), jnp.float32)
        return {'x': x, 'Wr': Wr, 'br': br, 'W1': W1, 'b1': b1, 'W2': W2, 'b2': b2, 'gamma': gamma, 'beta': beta}
    _L1_ffn_all = _L1_ffn_setup()
    _L1_ffn_in = {k: v for k, v in _L1_ffn_all.items() if k in ('Wr', 'br', 'W1', 'b1', 'W2', 'b2', 'gamma', 'beta')}
    del _L1_ffn_all
    return {'x': x, 'adj': adj, 'L0_gnn_W': _L0_gnn_in['W'], 'L0_gnn_a_1': _L0_gnn_in['a_1'], 'L0_gnn_a_2': _L0_gnn_in['a_2'], 'L0_gnn_a_12': _L0_gnn_in['a_12'], 'L0_gnn_W_1': _L0_gnn_in['W_1'], 'L0_gnn_W_2': _L0_gnn_in['W_2'], 'L0_ffn_weight': _L0_ffn_in['weight'], 'L0_ffn_bias': _L0_ffn_in['bias'], 'L1_gnn_W': _L1_gnn_in['W'], 'L1_gnn_a': _L1_gnn_in['a'], 'L1_ffn_Wr': _L1_ffn_in['Wr'], 'L1_ffn_br': _L1_ffn_in['br'], 'L1_ffn_W1': _L1_ffn_in['W1'], 'L1_ffn_b1': _L1_ffn_in['b1'], 'L1_ffn_W2': _L1_ffn_in['W2'], 'L1_ffn_b2': _L1_ffn_in['b2'], 'L1_ffn_gamma': _L1_ffn_in['gamma'], 'L1_ffn_beta': _L1_ffn_in['beta']}

def reference(x, adj, L0_gnn_W, L0_gnn_a_1, L0_gnn_a_2, L0_gnn_a_12, L0_gnn_W_1, L0_gnn_W_2, L0_ffn_weight, L0_ffn_bias, L1_gnn_W, L1_gnn_a, L1_ffn_Wr, L1_ffn_br, L1_ffn_W1, L1_ffn_b1, L1_ffn_W2, L1_ffn_b2, L1_ffn_gamma, L1_ffn_beta):
    import jax
    import jax.numpy as jnp

    def _L0_gnn_ref(feat, adj, W, a_1, a_2, a_12, W_1, W_2):
        import jax, jax.numpy as jnp
        import numpy as np
        B, N, F_IN, F_OUT = (1, 4096, 128, 128)
        ALPHA = 0.2
        NEG_INF = -9000000000000000.0
        h = jnp.matmul(feat, W)
        Ax = jnp.matmul(h, a_1)
        Ay = jnp.matmul(h, a_2)
        A_xy = jnp.matmul(jnp.matmul(h, a_12), jnp.swapaxes(h, 1, 2))
        logits = jnp.swapaxes(Ax, 1, 2) + Ay + A_xy
        e = jax.nn.leaky_relu(logits, negative_slope=ALPHA)
        e = jnp.where(adj > 0, e, NEG_INF)
        attention = jax.nn.softmax(e, axis=-1)
        h_prime = jnp.matmul(attention, feat)
        h_out = jnp.matmul(feat, W_1) + jnp.matmul(h_prime, W_2)
        return jax.nn.elu(h_out)

    def _L0_ffn_ref(x, weight, bias):
        import jax, jax.numpy as jnp
        import numpy as np
        IN_CH = 128
        OUT_CH = 128
        return jnp.einsum('bsi,oi->bso', x, weight) + bias

    def _L1_gnn_ref(h, adj, W, a):
        import jax, jax.numpy as jnp
        import numpy as np
        NEG_BIG = -9000000000000000.0
        F_out = W.shape[1]
        Wh = jnp.einsum('bnf,fo->bno', h, W)
        src = Wh @ a[:F_out, 0]
        dst = Wh @ a[F_out:, 0]
        e = jax.nn.leaky_relu(src[:, :, None] + dst[:, None, :], negative_slope=0.2)
        scores = jnp.where(adj > 0, e, jnp.float32(NEG_BIG))
        attention = jax.nn.softmax(scores, axis=2)
        h_prime = jnp.einsum('bij,bjo->bio', attention, Wh)
        return jax.nn.relu(h_prime)

    def _L1_ffn_ref(x, Wr, br, W1, b1, W2, b2, gamma, beta):
        import math
        import jax, jax.numpy as jnp
        import numpy as np
        CAPACITY_FACTOR = 1.25
        TOP_K = 2
        LN_EPS = 1e-05

        def _layer_norm(x, gamma, beta):
            mu = jnp.mean(x, axis=-1, keepdims=True)
            var = jnp.var(x, axis=-1, keepdims=True)
            return (x - mu) * jax.lax.rsqrt(var + LN_EPS) * gamma + beta
        B, S, D = x.shape
        E = Wr.shape[1]
        N = B * S
        K = TOP_K
        logits = jnp.mean(x, axis=1) @ Wr + br
        routing_weights = jax.nn.softmax(logits, axis=-1)
        capacity = float(math.ceil(N * CAPACITY_FACTOR / E))
        expected_loads = routing_weights.sum(axis=0) * (N / B)
        scale = jnp.where(expected_loads > capacity, capacity / expected_loads, 1.0)
        routing_weights = jax.nn.softmax(routing_weights * scale, axis=-1)
        rw_tok = jnp.broadcast_to(routing_weights[:, None, :], (B, S, E)).reshape(N, E)
        top_w, top_i = jax.lax.top_k(rw_tok, K)
        top_w = jax.nn.softmax(top_w, axis=-1)
        xf = x.reshape(N, D)
        h = jax.nn.gelu(jnp.einsum('nd,edf->enf', xf, W1) + b1[:, None, :], approximate=False)
        y = jnp.einsum('enf,efd->end', h, W2) + b2[:, None, :]
        w_dense = jnp.zeros((N, E), x.dtype).at[jnp.arange(N)[:, None], top_i].add(top_w)
        out = jnp.einsum('ne,end->nd', w_dense, y).reshape(B, S, D)
        out = _layer_norm(out + x, gamma, beta)
        return out
    x = x + _L0_gnn_ref(_layernorm(x, axis=-1), adj, L0_gnn_W, L0_gnn_a_1, L0_gnn_a_2, L0_gnn_a_12, L0_gnn_W_1, L0_gnn_W_2)
    x = x + _L0_ffn_ref(_layernorm(x, axis=-1), L0_ffn_weight, L0_ffn_bias)
    x = x + _L1_gnn_ref(_layernorm(x, axis=-1), adj, L1_gnn_W, L1_gnn_a)
    x = x + _L1_ffn_ref(_layernorm(x, axis=-1), L1_ffn_Wr, L1_ffn_br, L1_ffn_W1, L1_ffn_b1, L1_ffn_W2, L1_ffn_b2, L1_ffn_gamma, L1_ffn_beta)
    return x

_drawn_inputs = setup_inputs


def setup_inputs(seed=0):
    import zlib

    import numpy as np

    out = dict(_drawn_inputs(seed))
    spreads = {'L1_ffn_br': (0.0, 0.1),
     'L1_ffn_b1': (0.0, 0.503),
     'L1_ffn_b2': (0.0, 0.354),
     'L1_ffn_gamma': (1.0, 0.2),
     'L1_ffn_beta': (0.0, 0.1)}
    factors = {'L0_gnn_a_2': 8.0}
    for name, (base, spread) in spreads.items():
        noise = np.random.default_rng([zlib.crc32(name.encode()), seed]).standard_normal(out[name].shape)
        drawn = base * np.exp(spread * noise) if base else spread * noise
        out[name] = jnp.asarray(drawn.astype(out[name].dtype))
    for name, factor in factors.items():
        out[name] = (out[name] * factor).astype(out[name].dtype)
    return out
```

```python
from contextlib import ExitStack

import concourse.bass as bass
from concourse import mybir

F32 = mybir.dt.float32
BF16 = mybir.dt.bfloat16
I32 = mybir.dt.int32
ALU = mybir.AluOpType
ACT = mybir.ActivationFunctionType
AX = mybir.AxisListType

GRAPHS, P, D = 128, 128, 128
GRP = 4
W = GRP * D
NG = GRAPHS // GRP
UN = 4
EXPERTS, FF, TOPK = 8, 256, 2
EPS = 1e-5
MASKED = 4.5e16
SLOPE = 0.2
CAPACITY = float(-(-(GRAPHS * P * 5 // 4) // EXPERTS))
RSQRT_SEED = float(0x5F375A86)
RSTD_STEPS = 13


class Memory:
    pass


class Frames:

    def __init__(self, it, k, count, body):
        self.it, self.k, self.count, self.body = it, k, count, body

    def live(self, lag):
        return self.body or 0 <= self.it * UN + self.k - lag < self.count

    def group(self, lag=0):
        return self.it * UN + (self.k - lag)

    def pair(self, lag=0):
        return self.it * (UN // 2) + (self.k - lag) // 2

    def past(self, lag, n):
        return self.body or self.it * UN + self.k - lag >= n

    def slot(self, lag, n):
        return (self.k - lag) % n


def run_frames(eng, step, last_lag, history):
    first = -(-(last_lag + history) // UN)
    assert first < NG // UN
    for t in range(first * UN):
        step(Frames(t // UN, t % UN, NG, False))
    with eng.Fori(first, NG // UN) as it:
        for k in range(UN):
            step(Frames(it, k, NG, True))
    for t in range(NG, NG + last_lag):
        step(Frames(t // UN, t % UN, NG, False))


def grp(t, s):
    return t[:, bass.ds(s * W, W)]


def by_graph(ap):
    return ap.rearrange("p (g d) -> p g d", g=GRP)


def each(v):
    return v.to_broadcast([P, GRP, D])


def hold(eng, m):
    eng.sem_inc(m.held[eng], 1)


class Rstd:

    STEPS = 14

    def __init__(self, nc, m, done):
        self.nc, self.m, self.done = nc, m, done

    def step(self, n, pair, rstd, shift):
        v, m, done = self.nc.vector, self.m, self.done
        mean, squares = m.stats[:, :, 1], m.stats[:, :, 2]
        if n:
            v.wait_ge(done, pair * self.STEPS + n)
        if n == 0:
            i = v.tensor_scalar(m.var[:, :], squares, 1.0 / D, EPS, ALU.mult, ALU.add)
        elif n == 1:
            i = v.tensor_scalar(m.nhv[:, :], squares, -0.5 / D, -0.5 * EPS, ALU.mult, ALU.add)
        elif n == 2:
            i = v.tensor_scalar(m.seed[:, :], m.var[:, :].bitcast(I32), -0.5, RSQRT_SEED, ALU.mult, ALU.add)
        elif n < 12:
            y = [m.seed[:, :].bitcast(F32), m.ra[:, :], m.rb[:, :], rstd]
            a, b = y[n // 3 - 1], y[n // 3]
            if n % 3 == 0:
                i = v.tensor_tensor(m.rt[:, :], a, a, ALU.mult)
            elif n % 3 == 1:
                i = v.tensor_tensor(m.rt[:, :], m.rt[:, :], m.nhv[:, :], ALU.mult)
            else:
                i = v.scalar_tensor_tensor(b, m.rt[:, :], 1.5, a, ALU.add, ALU.mult)
        elif n == 12:
            i = v.tensor_tensor(m.rt[:, :], mean, rstd, ALU.mult)
        else:
            i = v.tensor_scalar(shift, m.rt[:, :], -1.0, 1.0, ALU.mult, ALU.add)
        i.then_inc(done, 1)


def make_weights(nc, m, a):
    with ExitStack() as ctx:
        s_in = ctx.enter_context(nc.semaphore("w_in"))
        s_pe = ctx.enter_context(nc.semaphore("w_product"))
        s_dve = ctx.enter_context(nc.semaphore("w_copied"))
        block = ctx.enter_context(nc.Block())
        bk = m.banks
        raw = m.raw
        wcT, a12T, b_s, a2b, a1b, asb, adb, wfT = (m.h_s[:, 0, 0:D], m.h_s[:, 0, D:2 * D], m.h_s[:, 0, 2 * D:3 * D],
                                                   m.h_s[:, 0, 3 * D:], m.h_s[:, 1, 0:D], m.h_s[:, 1, D:2 * D],
                                                   m.h_s[:, 1, 2 * D:3 * D], m.h_s[:, 1, 3 * D:])
        zero = m.e_s[:, 0, 0:D]
        wc1T = m.e_s[:, 0, D:2 * D]
        w1_raw = m.w1_raw
        wr_in = m.e_s[:, 0, 2 * D:2 * D + EXPERTS]
        bias_row = m.e_s[0:1, 0, 3 * D:4 * D]
        b1_all = m.b1_all
        vecs = m.e_s[:, 1, 0:8]

        LOADS = [(m.consts[:, :], a["consts"]), (m.one_row[:, :], a["one_row"]),
                 (raw[0], a["L0_gnn_W"]), (raw[1], a["L0_gnn_W_1"]), (raw[2], a["L0_gnn_W_2"]),
                 (raw[3], a["L0_gnn_a_12"]), (raw[4], a["L0_ffn_weight"]), (raw[5], a["L1_gnn_W"]),
                 (vecs[:, 0:1], a["L0_gnn_a_1"]), (vecs[:, 1:2], a["L0_gnn_a_2"]),
                 (vecs[:, 2:3], a["L1_gnn_a"][0:D, :]), (vecs[:, 3:4], a["L1_gnn_a"][D:2 * D, :]),
                 (bias_row, a["L0_ffn_bias"].rearrange("(a d) -> a d", a=1)),
                 (wr_in, a["L1_ffn_Wr"]), (m.br_row[:, :], a["L1_ffn_br"].rearrange("(a e) -> a e", a=1)),
                 (m.b2_rows[:, :], a["L1_ffn_b2"]),
                 (b1_all, a["L1_ffn_b1"].rearrange("(a e) f -> a (e f)", a=1)),
                 (m.gamma[:, :], a["L1_ffn_gamma"].partition_broadcast(P)),
                 (m.beta[:, :], a["L1_ffn_beta"].partition_broadcast(P)),
                 (w1_raw.rearrange("p (e f) -> p e f", e=EXPERTS), a["L1_ffn_W1"].rearrange("e d f -> d e f")),
                 (m.w2x[:, :, :, :], a["L1_ffn_W2"].rearrange("e (c p) d -> p e c d", p=P))]
        N_IN = 16 * len(LOADS)

        @block.sync
        def _(sp):
            for to, of in LOADS:
                sp.dma_start(to, of).then_inc(s_in, 16)

        def bank(i, n):
            return bk[:, i, 0:n]

        @block.tensor
        def _(pe):
            pe.wait_ge(s_in, N_IN)
            pe.matmul(bank(0, D), raw[0], m.centre, start=True, stop=True)
            pe.transpose(bank(1, D), raw[3], m.ident)
            pe.transpose(bank(2, D), raw[4], m.ident)
            pe.matmul(bank(3, D), raw[5], m.centre, start=True, stop=True)
            pe.matmul(bk[:, 4, 0:2 * D], m.centre, m.w12_in, start=True, stop=True)
            pe.matmul(bank(5, D), m.centre, raw[5], start=True, stop=True)
            pe.matmul(bank(6, EXPERTS), m.centre, wr_in, start=True, stop=True).then_inc(s_pe, 1)
            pe.wait_ge(s_dve, 1)
            pe.matmul(bank(0, D), a12T, wcT, start=True, stop=True)
            pe.matmul(bank(1, D), m.centre, wfT, start=True, stop=False)
            pe.matmul(bank(1, D), m.one_row[:, 0:D], m.bias_less[:, :], start=False, stop=True)
            pe.matmul(bank(2, D), wc1T, asb, start=True, stop=True)
            pe.matmul(bank(3, D), wc1T, adb, start=True, stop=True).then_inc(s_pe, 1)
            pe.wait_ge(s_dve, 2)
            pe.matmul(bank(0, D), wcT, b_s, start=True, stop=False)
            pe.matmul(bank(0, D), a1b, wcT, start=False, stop=True).then_inc(s_pe, 1)
            for e in range(EXPERTS):
                if e >= 4:
                    pe.wait_ge(s_dve, e - 1)
                pe.matmul(bank(4 + e % 4, FF), m.centre, w1_raw[:, e * FF:(e + 1) * FF], start=True, stop=False)
                pe.matmul(bank(4 + e % 4, FF), m.one_row[:, 0:D], b1_all[:, e * FF:(e + 1) * FF],
                          start=False, stop=True).then_inc(s_pe, 1)

        @block.vector
        def _(v):
            chain = m.small
            n = [0]

            def after(i):
                n[0] += 1
                i.then_inc(chain, 1)
                v.wait_ge(chain, n[0])

            v.wait_ge(s_in, N_IN)
            after(v.memset(zero, 0.0))
            for to, j, scale in ((a1b, 0, 1.0 / D), (a2b, 1, 1.0 / D), (asb, 2, -1.0), (adb, 3, -1.0)):
                after(v.tensor_scalar(to, zero, vecs[:, j:j + 1], scale, ALU.add, ALU.mult))
            after(v.tensor_scalar(m.bias_less[:, :], bias_row, 1.0, None, ALU.subtract))
            after(v.memset(m.xv[:, :, :, 2 * D:], 1.0))
            after(v.memset(m.ones[:, :], 1.0))
            v.wait_ge(s_pe, 1)
            after(v.tensor_copy(wcT, bank(0, D)))
            after(v.tensor_copy(a12T, bank(1, D)))
            after(v.tensor_copy(wfT, bank(2, D)))
            after(v.tensor_copy(wc1T, bank(3, D)))
            after(v.tensor_copy(m.w12[:, :], bk[:, 4, 0:2 * D]))
            after(v.tensor_copy(m.wc[:, :], bank(5, D)))
            after(v.tensor_scalar(m.wr[:, :], bank(6, EXPERTS), 1.0 / P, None, ALU.mult))
            v.sem_inc(s_dve, 1)
            v.wait_ge(s_pe, 2)
            after(v.tensor_tensor(b_s, bank(0, D), a2b, ALU.add))
            after(v.tensor_copy(m.wf[:, :], bank(1, D)))
            after(v.tensor_copy(m.src_w[:, :], bank(2, D)))
            after(v.tensor_copy(m.dst_w[:, :], bank(3, D)))
            v.sem_inc(s_dve, 1)
            v.wait_ge(s_pe, 3)
            after(v.tensor_scalar(m.m_w[:, :], bank(0, D), -1.0, None, ALU.mult))
            for e in range(EXPERTS):
                v.wait_ge(s_pe, 4 + e)
                v.tensor_copy(m.w1x[:, e, :], bank(4 + e % 4, FF)).then_inc(s_dve, 1)


def statistics(v, stats, x, first, u, done):
    for j in range(0, GRP, 2):
        v.bn_stats(stats[:, GRP * u + j:GRP * u + j + 2, :].rearrange("p a b -> p (a b)"),
                   x[:, bass.ds(first + j * D, 2 * D)].rearrange("p (g d) -> p d g", g=2)).then_inc(done, 1)


def transpose_graphs(pe, to, of, ident, done):
    for j in range(GRP):
        i = pe.transpose(to[:, j * D:(j + 1) * D], of[:, j * D:(j + 1) * D], ident)
    i.then_inc(done, 1)


def make_z(pool, m, s, q, rstd, shift, z_mul, z_ready):
    zq = by_graph(m.z[:, q, :])
    pool.tensor_tensor(zq, by_graph(grp(m.X, s)), each(rstd), ALU.mult).then_inc(z_mul, 1)
    pool.wait_ge(z_mul, s + 1)
    pool.tensor_tensor(zq, zq, each(shift), ALU.add).then_inc(z_ready, 1)


def softmax_rows(act, m, q, done):
    for j in range(GRP):
        i = act.activation(m.p_s[:, q, j * D:(j + 1) * D], m.l_s[:, q, j * D:(j + 1) * D], ACT.Exp,
                           bias=m.nmax[:, q, j:j + 1], scale=-1.0)
    i.then_inc(done, 1)


def layer0(nc, m, a):
    with ExitStack() as ctx:
        def sem(name):
            return ctx.enter_context(nc.semaphore("a_" + name))

        x_in = [sem(f"x_in{i}") for i in range(4)]
        adj_in = [sem(f"adj_in{i}") for i in range(4)]
        mask_kept = [sem(f"mask_kept{i}") for i in range(4)]
        masked, stats_done, rstd_done = sem("masked"), sem("stats_done"), sem("rstd_done")
        z_mul, z_ready = sem("z_mul"), sem("z_ready")
        t_done, zT_copied = sem("t_done"), sem("zT_copied")
        u_done, uT_copied = sem("u_done"), sem("uT_copied")
        xv_done, xv_copied = sem("xv_done"), sem("xv_copied")
        s_done, s_read = sem("s_done"), sem("s_read")
        max_ready, l_ready = sem("max_ready"), sem("l_ready")
        p_ready = sem("p_ready")
        pt_done, pT_copied = sem("pt_done"), sem("pT_copied")
        o_done, rden_done, h_done = sem("o_done"), sem("rden_done"), sem("h_done")
        e_done, ex_done, x_done = sem("e_done"), sem("ex_done"), sem("x_done")
        rstd = Rstd(nc, m, rstd_done)
        bk = m.banks
        T_B, PT_B, U_B, S_B, XV_B, O_B = 0, 1, 2, 3, 4, 6
        block = ctx.enter_context(nc.Block())

        @block.sync
        def _(sp):
            def step(f):
                if f.live(0):
                    s, k = f.group(), f.slot(0, 4)
                    if f.past(0, 4):
                        sp.wait_ge(stats_done, 2 * (s - 3))
                    sp.dma_start(by_graph(grp(m.X, s)),
                                 a["x"][bass.ds(s * GRP, GRP), :, :].rearrange("g n d -> n g d")).then_inc(x_in[k], 16)
                if f.live(4):
                    s, k = f.group(4), f.slot(4, 4)
                    if f.past(4, 4):
                        sp.wait_ge(masked, s - 3)
                    sp.dma_start(by_graph(m.adj_in[:, k, :]),
                                 a["adj"][bass.ds(s * GRP, GRP), :, :].rearrange("g n d -> n g d")).then_inc(adj_in[k], 16)
                if f.live(8):
                    s, k = f.group(8), f.slot(8, 4)
                    sp.wait_ge(masked, s + 1)
                    sp.dma_start(grp(m.MASK, s), m.mask[:, k, :]).then_inc(mask_kept[k], 16)

            run_frames(sp, step, 8, 4)
            for k in range(4):
                sp.wait_ge(mask_kept[k], 16 * (NG // 4))

        @block.gpsimd
        def _(pool):
            def step(f):
                s, q = f.group(), f.slot(0, 2)
                p, r = f.pair(f.k % 2), (f.k // 2) % 2
                pool.wait_ge(rstd_done, (p + 1) * Rstd.STEPS)
                if f.past(0, 2):
                    pool.wait_ge(t_done, s - 1)
                half = slice(GRP * (f.k % 2), GRP * (f.k % 2) + GRP)
                make_z(pool, m, s, q, m.rstd[:, r, half], m.shift[:, r, half], z_mul, z_ready)

            run_frames(pool, step, 0, 2)

        @block.tensor
        def _(pe):
            def step(f):
                if f.live(0):
                    s, q = f.group(), f.slot(0, 2)
                    pe.wait_ge(z_ready, s + 1)
                    if f.past(0, 1):
                        pe.wait_ge(zT_copied, s)
                    transpose_graphs(pe, bk[:, T_B, :], m.z[:, q, :], m.ident, t_done)
                if f.live(3):
                    s, q = f.group(3), f.slot(3, 2)
                    pe.wait_ge(p_ready, s + 1)
                    if f.past(3, 1):
                        pe.wait_ge(pT_copied, s)
                    transpose_graphs(pe, bk[:, PT_B, :], m.p_s[:, q, :], m.ident, pt_done)
                if f.live(1):
                    s, q = f.group(1), f.slot(1, 2)
                    pe.wait_ge(zT_copied, s + 1)
                    if f.past(1, 1):
                        pe.wait_ge(uT_copied, s)
                    pe.matmul(bk[:, U_B, :], m.m_w[:, :], m.zT[:, q, :], start=True, stop=True).then_inc(u_done, 1)
                    if f.past(1, 1):
                        pe.wait_ge(xv_copied, s)
                    for j in range(GRP):
                        i = pe.matmul(bk[:, XV_B + j // 2, (j % 2) * 2 * D:(j % 2 + 1) * 2 * D],
                                      m.zT[:, q, j * D:(j + 1) * D], m.w12[:, :], start=True, stop=True)
                    i.then_inc(xv_done, 1)
                if f.live(1):
                    s, q = f.group(1), f.slot(1, 2)
                    pe.wait_ge(uT_copied, s + 1)
                    if f.past(1, 1):
                        pe.wait_ge(s_read, GRP * s)
                    for j in range(GRP):
                        c = slice(j * D, (j + 1) * D)
                        i = pe.matmul(bk[:, S_B, c], m.uT[:, q, c], m.zT[:, q, c], start=True, stop=True)
                    i.then_inc(s_done, 1)
                if f.live(3):
                    s, q, k = f.group(3), f.slot(3, 2), f.slot(3, 4)
                    pe.wait_ge(pT_copied, s + 1)
                    if f.past(3, 1):
                        pe.wait_ge(h_done, s)
                    for j in range(GRP):
                        i = pe.matmul(bk[:, O_B + j // 2, (j % 2) * (D + 1):(j % 2 + 1) * (D + 1)],
                                      m.pT[:, q, j * D:(j + 1) * D], m.xv[:, k, j, D:], start=True, stop=True)
                    i.then_inc(o_done, 1)

            run_frames(pe, step, 3, 1)

        @block.scalar
        def _(act):
            def step(f):
                if f.live(0):
                    s, q = f.group(), f.slot(0, 2)
                    act.wait_ge(t_done, s + 1)
                    if f.past(0, 2):
                        act.wait_ge(s_done, s - 1)
                    act.copy(m.zT[:, q, :], bk[:, T_B, :]).then_inc(zT_copied, 1)
                if f.live(3):
                    s, q = f.group(3), f.slot(3, 2)
                    act.wait_ge(pt_done, s + 1)
                    if f.past(3, 2):
                        act.wait_ge(o_done, s - 1)
                    act.copy(m.pT[:, q, :], bk[:, PT_B, :]).then_inc(pT_copied, 1)
                if f.live(1):
                    s, q = f.group(1), f.slot(1, 2)
                    act.wait_ge(u_done, s + 1)
                    if f.past(1, 2):
                        act.wait_ge(s_done, s - 1)
                    act.copy(m.uT[:, q, :], bk[:, U_B, :]).then_inc(uT_copied, 1)
                if f.live(2):
                    s, q = f.group(2), f.slot(2, 2)
                    act.wait_ge(l_ready, s + 1)
                    if f.past(2, 2):
                        act.wait_ge(pt_done, s - 1)
                    softmax_rows(act, m, q, p_ready)
                if f.live(1):
                    s, k = f.group(1), f.slot(1, 4)
                    act.wait_ge(xv_done, s + 1)
                    if f.past(1, 4):
                        act.wait_ge(h_done, s - 3)
                    act.copy(m.xv[:, k, :, 0:2 * D].rearrange("p (b j) n -> p b j n", b=2),
                             bk[:, XV_B:XV_B + 2, :].rearrange("p b (j n) -> p b j n", j=2)).then_inc(xv_copied, 1)
                if f.live(4):
                    s, q = f.group(4), f.slot(4, 2)
                    act.wait_ge(h_done, s + 1)
                    if f.past(4, 2):
                        act.wait_ge(x_done, s - 1)
                    act.activation(m.e_s[:, q, :], m.h_s[:, q, :], ACT.Exp).then_inc(e_done, 1)

            run_frames(act, step, 4, 4)

        @block.vector
        def _(v):
            def step(f):
                def chain(*ns):
                    if f.live(f.k % 2):
                        r = (f.k // 2) % 2
                        for n in ns:
                            rstd.step(n, f.pair(f.k % 2), m.rstd[:, r, :], m.shift[:, r, :])

                if f.k % 2 == 0 and f.live(0):
                    p = f.pair()
                    for u in range(2):
                        s, k = f.group() + u, f.slot(-u, 4)
                        v.wait_ge(x_in[k], 16 * (f.it + 1))
                        if u == 0 and f.past(0, 2):
                            v.wait_ge(rstd_done, p * Rstd.STEPS)
                        statistics(v, m.stats, m.X, s * W, u, stats_done)
                    if f.past(0, 4):
                        v.wait_ge(z_ready, 2 * p - 2)
                    v.wait_ge(stats_done, 4 * (p + 1))
                    chain(0, 1)
                first = 2 if f.k % 2 == 0 else 8
                if f.live(5):
                    s, q, k = f.group(5), f.slot(5, 2), f.slot(5, 4)
                    v.wait_ge(s_done, s + 1)
                    v.wait_ge(masked, s + 1)
                    if f.past(5, 2):
                        v.wait_ge(l_ready, s - 1)
                    hold(v, m)
                    for j in range(GRP):
                        c = slice(j * D, (j + 1) * D)
                        v.tensor_tensor_reduce(m.t_s[:, q, c], bk[:, S_B, c], m.mask[:, k, c], 1.0, 3.0e38,
                                               ALU.add, ALU.min, m.nmin[:, q, j:j + 1]).then_inc(s_read, 1)
                        chain(first + j)
                    v.wait_ge(s_read, GRP * (s + 1))
                    if f.past(5, 2):
                        v.wait_ge(p_ready, s - 1)
                    v.scalar_tensor_tensor(m.nmax[:, q, :], m.nmin[:, q, :], SLOPE, m.nmin[:, q, :], ALU.mult, ALU.min)\
                     .then_inc(max_ready, 1)
                    v.scalar_tensor_tensor(m.l_s[:, q, :], m.t_s[:, q, :], SLOPE, m.t_s[:, q, :], ALU.mult, ALU.min)\
                     .then_inc(l_ready, 1)
                else:
                    chain(*range(first, first + 4))
                if f.live(4):
                    s, k = f.group(4), f.slot(4, 4)
                    v.wait_ge(adj_in[k], 16 * f.it)
                    if f.past(4, 4):
                        v.wait_ge(mask_kept[k], 16 * (f.it - 1))
                        v.wait_ge(s_read, GRP * (s - 3))
                    v.tensor_scalar(m.mask[:, k, :], m.adj_in[:, k, :], 0, MASKED, ALU.is_le, ALU.mult)\
                     .then_inc(masked, 1)
                chain(first + 4)
                if f.live(7):
                    s, q, k = f.group(7), f.slot(7, 2), f.slot(7, 4)
                    v.wait_ge(o_done, s + 1)
                    if f.past(7, 1):
                        v.wait_ge(h_done, s)
                    v.reciprocal(m.rden[:, q, :].rearrange("p (b j) -> p b j", b=2),
                                 bk[:, O_B:O_B + 2, D:2 * (D + 1):D + 1]).then_inc(rden_done, 1)
                    chain(first + 5)
                    v.wait_ge(rden_done, s + 1)
                    if f.past(7, 2):
                        v.wait_ge(x_done, s - 1)
                    for j in range(GRP):
                        o = (j % 2) * (D + 1)
                        i = v.scalar_tensor_tensor(m.h_s[:, q, j * D:(j + 1) * D], bk[:, O_B + j // 2, o:o + D],
                                                   m.rden[:, q, j:j + 1], m.xv[:, k, j, 0:D], ALU.mult, ALU.add)
                    i.then_inc(h_done, 1)
                else:
                    chain(first + 5)
                if f.live(8):
                    s, q = f.group(8), f.slot(8, 2)
                    v.wait_ge(e_done, s + 1)
                    v.scalar_tensor_tensor(m.e_s[:, q, :], m.e_s[:, q, :], 1.0, grp(m.X, s), ALU.min, ALU.add)\
                     .then_inc(ex_done, 1)
                    v.wait_ge(ex_done, s + 1)
                    v.scalar_tensor_tensor(grp(m.X, s), m.h_s[:, q, :], 0.0, m.e_s[:, q, :], ALU.max, ALU.add)\
                     .then_inc(x_done, 1)

            run_frames(v, step, 8, 2)


def linear(nc, m):
    with ExitStack() as ctx:
        def sem(name):
            return ctx.enter_context(nc.semaphore("f_" + name))

        stats_done, rstd_done = sem("stats_done"), sem("rstd_done")
        z_mul, z_ready = sem("z_mul"), sem("z_ready")
        t_done, zT_copied = sem("t_done"), sem("zT_copied")
        y_done, x_done = sem("y_done"), sem("x_done")
        rstd = Rstd(nc, m, rstd_done)
        bk = m.banks
        T_B, Y_B = 0, 2
        block = ctx.enter_context(nc.Block())

        @block.gpsimd
        def _(pool):
            def step(f):
                s, q = f.group(), f.slot(0, 2)
                p, r = f.pair(f.k % 2), (f.k // 2) % 2
                pool.wait_ge(rstd_done, (p + 1) * Rstd.STEPS)
                if f.past(0, 2):
                    pool.wait_ge(t_done, s - 1)
                half = slice(GRP * (f.k % 2), GRP * (f.k % 2) + GRP)
                make_z(pool, m, s, q, m.rstd[:, r, half], m.shift[:, r, half], z_mul, z_ready)

            run_frames(pool, step, 0, 2)

        @block.tensor
        def _(pe):
            def step(f):
                if f.live(0):
                    s, q = f.group(), f.slot(0, 2)
                    pe.wait_ge(z_ready, s + 1)
                    if f.past(0, 2):
                        pe.wait_ge(zT_copied, s - 1)
                    transpose_graphs(pe, bk[:, T_B + q, :], m.z[:, q, :], m.ident, t_done)
                if f.live(1):
                    s, q = f.group(1), f.slot(1, 2)
                    pe.wait_ge(zT_copied, s + 1)
                    if f.past(1, 2):
                        pe.wait_ge(x_done, s - 1)
                    for j in range(GRP):
                        c = slice(j * D, (j + 1) * D)
                        i = pe.matmul(bk[:, Y_B + q, c], m.zT[:, q, c], m.wf[:, :], start=True, stop=True)
                    i.then_inc(y_done, 1)

            run_frames(pe, step, 1, 2)

        @block.scalar
        def _(act):
            def step(f):
                s, q = f.group(), f.slot(0, 2)
                act.wait_ge(t_done, s + 1)
                if f.past(0, 2):
                    act.wait_ge(y_done, s - 1)
                act.copy(m.zT[:, q, :], bk[:, T_B + q, :]).then_inc(zT_copied, 1)

            run_frames(act, step, 0, 2)

        @block.vector
        def _(v):
            def step(f):
                def chain(*ns):
                    if f.live(f.k % 2):
                        r = (f.k // 2) % 2
                        for n in ns:
                            rstd.step(n, f.pair(f.k % 2), m.rstd[:, r, :], m.shift[:, r, :])

                if f.k % 2 == 0 and f.live(0):
                    p = f.pair()
                    if f.past(0, 2):
                        v.wait_ge(rstd_done, p * Rstd.STEPS)
                    statistics(v, m.stats, m.X, f.group() * W, 0, stats_done)
                    statistics(v, m.stats, m.X, f.group() * W + W, 1, stats_done)
                    if f.past(0, 4):
                        v.wait_ge(z_ready, 2 * p - 2)
                    v.wait_ge(stats_done, 4 * (p + 1))
                chain(*range(7 * (f.k % 2), 7 * (f.k % 2) + 7))
                if f.live(4):
                    s, q = f.group(4), f.slot(4, 2)
                    v.wait_ge(y_done, s + 1)
                    v.tensor_tensor(grp(m.X, s), grp(m.X, s), bk[:, Y_B + q, :], ALU.add).then_inc(x_done, 1)

            run_frames(v, step, 4, 2)


def layer1(nc, m):
    with ExitStack() as ctx:
        def sem(name):
            return ctx.enter_context(nc.semaphore("b_" + name))

        mask_in = [sem(f"mask_in{i}") for i in range(4)]
        x_copied = [sem(f"x_copied{i}") for i in range(4)]
        stats_done, rstd_done = sem("stats_done"), sem("rstd_done")
        stats3_done, rstd3_done = sem("stats3_done"), sem("rstd3_done")
        z_mul, z_ready = sem("z_mul"), sem("z_ready")
        t_done, zT_copied = sem("t_done"), sem("zT_copied")
        wh_done, wh_copied = sem("wh_done"), sem("wh_copied")
        s_done, s_read = sem("s_done"), sem("s_read")
        max_ready, l_ready = sem("max_ready"), sem("l_ready")
        p_ready = sem("p_ready")
        pt_done, pT_copied = sem("pt_done"), sem("pT_copied")
        o_done, rden_done, h_done = sem("o_done"), sem("rden_done"), sem("h_done")
        x_done, mean_done = sem("x_done"), sem("mean_done")
        mean_copied = sem("mean_copied")
        rstd = Rstd(nc, m, rstd_done)
        rstd3 = Rstd(nc, m.for_rstd3, rstd3_done)
        bk = m.banks
        T_B, PT_B, WH_B, S_B, MEAN_B, O_B = 0, 1, 2, 3, 4, 6
        block = ctx.enter_context(nc.Block())

        @block.sync
        def _(sp):
            def step(f):
                if f.live(0):
                    s, k = f.group(), f.slot(0, 4)
                    if f.past(0, 4):
                        sp.wait_ge(s_read, GRP * (s - 3))
                    sp.dma_start(m.mask[:, k, :], grp(m.MASK, s)).then_inc(mask_in[k], 16)
                if f.live(8):
                    s, k = f.group(8), f.slot(8, 4)
                    sp.wait_ge(x_done, s + 1)
                    hold(sp, m)
                    if f.past(8, 4):
                        sp.wait_ge(mean_done, s - 3)
                    sp.dma_start(m.x_copy[:, k, :], grp(m.X, s)).then_inc(x_copied[k], 16)

            run_frames(sp, step, 8, 4)

        @block.gpsimd
        def _(pool):
            def step(f):
                s, q = f.group(), f.slot(0, 2)
                p, r = f.pair(f.k % 2), (f.k // 2) % 2
                pool.wait_ge(rstd_done, (p + 1) * Rstd.STEPS)
                if f.past(0, 2):
                    pool.wait_ge(t_done, s - 1)
                half = slice(GRP * (f.k % 2), GRP * (f.k % 2) + GRP)
                make_z(pool, m, s, q, m.rstd[:, r, half], m.shift[:, r, half], z_mul, z_ready)

            run_frames(pool, step, 0, 2)

        @block.tensor
        def _(pe):
            def step(f):
                if f.live(0):
                    s, q = f.group(), f.slot(0, 2)
                    pe.wait_ge(z_ready, s + 1)
                    if f.past(0, 1):
                        pe.wait_ge(zT_copied, s)
                    transpose_graphs(pe, bk[:, T_B, :], m.z[:, q, :], m.ident, t_done)
                if f.live(3):
                    s, q = f.group(3), f.slot(3, 2)
                    pe.wait_ge(p_ready, s + 1)
                    if f.past(3, 1):
                        pe.wait_ge(pT_copied, s)
                    transpose_graphs(pe, bk[:, PT_B, :], m.p_s[:, q, :], m.ident, pt_done)
                if f.live(1):
                    s, q = f.group(1), f.slot(1, 2)
                    pe.wait_ge(zT_copied, s + 1)
                    if f.past(1, 1):
                        pe.wait_ge(s_read, GRP * s)
                    pe.matmul(bk[:, S_B, :], m.dst_w[:, :], m.zT[:, q, :], start=True, stop=False)
                    for j in range(GRP):
                        c = slice(j * D, (j + 1) * D)
                        i = pe.matmul(bk[:, S_B, c], m.zT[:, q, c], m.src_w[:, :], start=False, stop=j == GRP - 1)
                    i.then_inc(s_done, 1)
                    if f.past(1, 1):
                        pe.wait_ge(wh_copied, s)
                    for j in range(GRP):
                        c = slice(j * D, (j + 1) * D)
                        i = pe.matmul(bk[:, WH_B, c], m.zT[:, q, c], m.wc[:, :], start=True, stop=True)
                    i.then_inc(wh_done, 1)
                if f.live(3):
                    s, q, k = f.group(3), f.slot(3, 2), f.slot(3, 4)
                    pe.wait_ge(pT_copied, s + 1)
                    if f.past(3, 1):
                        pe.wait_ge(h_done, s)
                    for j in range(GRP):
                        i = pe.matmul(bk[:, O_B + j // 2, (j % 2) * (D + 1):(j % 2 + 1) * (D + 1)],
                                      m.pT[:, q, j * D:(j + 1) * D], m.xv[:, k, j, D:], start=True, stop=True)
                    i.then_inc(o_done, 1)
                if f.live(8):
                    s, k = f.group(8), f.slot(8, 4)
                    pe.wait_ge(x_copied[k], 16 * (f.it - 1))
                    pe.wait_ge(rstd3_done, (f.pair(8 + f.k % 2) + 1) * Rstd.STEPS)
                    for j in range(GRP):
                        i = pe.matmul(bk[:, MEAN_B, bass.ds(s * GRP + j, 1)], m.x_copy[:, k, j * D:(j + 1) * D],
                                      m.rstd3[:, bass.ds(s * GRP + j, 1)], start=True, stop=True)
                    i.then_inc(mean_done, 1)

            run_frames(pe, step, 8, 1)

        @block.scalar
        def _(act):
            def step(f):
                if f.live(0):
                    s, q = f.group(), f.slot(0, 2)
                    act.wait_ge(t_done, s + 1)
                    if f.past(0, 2):
                        act.wait_ge(wh_done, s - 1)
                    act.copy(m.zT[:, q, :], bk[:, T_B, :]).then_inc(zT_copied, 1)
                if f.live(3):
                    s, q = f.group(3), f.slot(3, 2)
                    act.wait_ge(pt_done, s + 1)
                    if f.past(3, 2):
                        act.wait_ge(o_done, s - 1)
                    act.copy(m.pT[:, q, :], bk[:, PT_B, :]).then_inc(pT_copied, 1)
                if f.live(2):
                    s, q = f.group(2), f.slot(2, 2)
                    act.wait_ge(l_ready, s + 1)
                    if f.past(2, 2):
                        act.wait_ge(pt_done, s - 1)
                    softmax_rows(act, m, q, p_ready)
                if f.live(1):
                    s, k = f.group(1), f.slot(1, 4)
                    act.wait_ge(wh_done, s + 1)
                    if f.past(1, 4):
                        act.wait_ge(o_done, s - 3)
                    act.copy(m.xv[:, k, :, D:2 * D], by_graph(bk[:, WH_B, :])).then_inc(wh_copied, 1)
                if f.live(4):
                    s, q = f.group(4), f.slot(4, 2)
                    act.wait_ge(rden_done, s + 1)
                    if f.past(4, 2):
                        act.wait_ge(x_done, s - 1)
                    for j in range(GRP):
                        o = (j % 2) * (D + 1)
                        i = act.activation(m.h_s[:, q, j * D:(j + 1) * D], bk[:, O_B + j // 2, o:o + D], ACT.Relu,
                                           scale=m.rden[:, q, j:j + 1])
                    i.then_inc(h_done, 1)

            run_frames(act, step, 4, 4)

        @block.vector
        def _(v):
            def step(f):
                def chain(*ns):
                    if f.live(f.k % 2):
                        r = (f.k // 2) % 2
                        for n in ns:
                            rstd.step(n, f.pair(f.k % 2), m.rstd[:, r, :], m.shift[:, r, :])

                def chain3(*ns):
                    if f.live(10 + f.k % 2):
                        p = f.pair(10 + f.k % 2)
                        for n in ns:
                            rstd3.step(n, p, m.rstd3[:, bass.ds(p * 2 * GRP, 2 * GRP)],
                                       m.shift3[:, bass.ds(p * 2 * GRP, 2 * GRP)])

                if f.k % 2 == 0 and f.live(0):
                    p = f.pair()
                    if f.past(0, 2):
                        v.wait_ge(rstd_done, p * Rstd.STEPS)
                    statistics(v, m.stats, m.X, f.group() * W, 0, stats_done)
                    statistics(v, m.stats, m.X, f.group() * W + W, 1, stats_done)
                    if f.past(0, 4):
                        v.wait_ge(z_ready, 2 * p - 2)
                    v.wait_ge(stats_done, 4 * (p + 1))
                if f.k % 2 == 0 and f.live(10):
                    p = f.pair(10)
                    if f.past(10, 2):
                        v.wait_ge(rstd3_done, p * Rstd.STEPS)
                    v.wait_ge(x_done, 2 * (p + 1))
                    hold(v, m)
                    statistics(v, m.for_rstd3.stats, m.X, f.group(10) * W, 0, stats3_done)
                    statistics(v, m.for_rstd3.stats, m.X, f.group(10) * W + W, 1, stats3_done)
                    v.wait_ge(stats3_done, 4 * (p + 1))
                first = 7 * (f.k % 2)
                chain(first)
                chain3(first)
                if f.live(5):
                    s, q, k = f.group(5), f.slot(5, 2), f.slot(5, 4)
                    v.wait_ge(s_done, s + 1)
                    if f.past(5, 2):
                        v.wait_ge(l_ready, s - 1)
                    v.wait_ge(mask_in[k], 16 * (f.it - (f.k == 0)))
                    hold(v, m)
                    for j in range(GRP):
                        c = slice(j * D, (j + 1) * D)
                        v.tensor_tensor_reduce(m.t_s[:, q, c], bk[:, S_B, c], m.mask[:, k, c], 1.0, 3.0e38,
                                               ALU.add, ALU.min, m.nmin[:, q, j:j + 1]).then_inc(s_read, 1)
                        chain(first + 1 + j)
                        chain3(first + 1 + j)
                    v.wait_ge(s_read, GRP * (s + 1))
                    if f.past(5, 2):
                        v.wait_ge(p_ready, s - 1)
                    v.scalar_tensor_tensor(m.nmax[:, q, :], m.nmin[:, q, :], SLOPE, m.nmin[:, q, :], ALU.mult, ALU.min)\
                     .then_inc(max_ready, 1)
                    v.scalar_tensor_tensor(m.l_s[:, q, :], m.t_s[:, q, :], SLOPE, m.t_s[:, q, :], ALU.mult, ALU.min)\
                     .then_inc(l_ready, 1)
                else:
                    chain(*range(first + 1, first + 5))
                    chain3(*range(first + 1, first + 5))
                chain(first + 5)
                chain3(first + 5)
                if f.live(7):
                    s, q, k = f.group(7), f.slot(7, 2), f.slot(7, 4)
                    v.wait_ge(o_done, s + 1)
                    if f.past(7, 2):
                        v.wait_ge(h_done, s - 1)
                    v.reciprocal(m.rden[:, q, :].rearrange("p (b j) -> p b j", b=2),
                                 bk[:, O_B:O_B + 2, D:2 * (D + 1):D + 1]).then_inc(rden_done, 1)
                if f.live(8):
                    s, q = f.group(8), f.slot(8, 2)
                    v.wait_ge(h_done, s + 1)
                    v.tensor_tensor(grp(m.X, s), grp(m.X, s), m.h_s[:, q, :], ALU.add).then_inc(x_done, 1)
                chain(first + 6)
                chain3(first + 6)

            run_frames(v, step, 11, 4)
            v.wait_ge(mean_done, NG)
            v.tensor_copy(m.node_sums[:, :], bk[:, MEAN_B, 0:GRAPHS]).then_inc(mean_copied, 1)
            v.wait_ge(mean_copied, 1)


def route(nc, m):
    with ExitStack() as ctx:
        s_pe = ctx.enter_context(nc.semaphore("r_product"))
        s_v = ctx.enter_context(nc.semaphore("r_vector"))
        s_act = ctx.enter_context(nc.semaphore("r_exp"))
        kept = ctx.enter_context(nc.semaphore("r_kept"))
        back = ctx.enter_context(nc.semaphore("r_back"))
        block = ctx.enter_context(nc.Block())
        bk = m.banks
        LG, LOAD, WT, B2 = bk[:, 0, 0:EXPERTS], bk[:, 1, 0:EXPERTS], bk[0:EXPERTS, 2, 0:D], bk[:, 3, 0:D]
        rows = m.l_s[:, 0, :].rearrange("p (r e) -> p r e", e=EXPERTS)
        ex, rw, scale, rw2, eq, first, second, rest, dense, tmp = (rows[:, i, :] for i in range(10))
        cols = m.l_s[:, 1, :]
        nmax, total, rtotal, top1, top2, i1, i2, diff, e2, w_sum = (cols[:, i:i + 1] for i in range(10))
        w12 = cols[:, 16:18]
        idx = cols[:, 20:22]
        idx_int = cols[:, 24:26].bitcast(I32)
        dense_T = m.t_s[0:EXPERTS, 0, 0:D]
        b2_mix = m.t_s[:, 1, 0:D]

        @block.tensor
        def _(pe):
            pe.matmul(LG, m.node_sums[:, :], m.wr[:, :], start=True, stop=False)
            pe.matmul(LG, m.one_row[:, D:2 * D], m.br_row[:, :], start=False, stop=True).then_inc(s_pe, 1)
            pe.wait_ge(s_v, 3)
            pe.matmul(LOAD, m.ones[:, :], rw, start=True, stop=True).then_inc(s_pe, 1)
            pe.wait_ge(s_v, 34)
            pe.transpose(WT, dense, m.ident).then_inc(s_pe, 1)
            pe.wait_ge(s_v, 35)
            pe.matmul(B2, dense_T, m.b2_rows[:, :], start=True, stop=True).then_inc(s_pe, 1)

        @block.scalar
        def _(act):
            act.wait_ge(s_v, 1)
            act.activation(ex, LG, ACT.Exp, bias=nmax, accum_out=total).then_inc(s_act, 1)
            act.wait_ge(s_v, 8)
            act.activation(ex, rw2, ACT.Exp, bias=nmax, accum_out=total).then_inc(s_act, 1)
            act.wait_ge(s_v, 27)
            act.activation(e2, diff, ACT.Exp).then_inc(s_act, 1)

        @block.vector
        def _(v):
            n = [0]

            def done(i):
                n[0] += 1
                i.then_inc(s_v, 1)
                v.wait_ge(s_v, n[0])

            v.wait_ge(s_pe, 1)
            done(v.tensor_reduce(nmax, LG, AX.X, ALU.max, negate=True))
            v.wait_ge(s_act, 1)
            done(v.reciprocal(rtotal, total))
            done(v.tensor_scalar(rw, ex, rtotal, None, ALU.mult))
            v.wait_ge(s_pe, 2)
            done(v.tensor_scalar(scale, LOAD, float(P), None, ALU.mult))
            done(v.reciprocal(tmp, scale))
            done(v.tensor_scalar(scale, tmp, CAPACITY, 1.0, ALU.mult, ALU.min))
            done(v.tensor_tensor(rw2, rw, scale, ALU.mult))
            done(v.tensor_reduce(nmax, rw2, AX.X, ALU.max, negate=True))
            v.wait_ge(s_act, 2)
            done(v.reciprocal(rtotal, total))
            done(v.tensor_scalar(rw, ex, rtotal, None, ALU.mult))
            done(v.tensor_copy(rest, rw))
            for top, i, hot in ((top1, i1, first), (top2, i2, second)):
                done(v.tensor_reduce(top, rest, AX.X, ALU.max))
                done(v.tensor_scalar(eq, rest, top, None, ALU.is_equal))
                done(v.tensor_scalar(tmp, m.iota, float(EXPERTS), None, ALU.subtract))
                done(v.tensor_tensor(tmp, tmp, eq, ALU.mult))
                done(v.tensor_reduce(i, tmp, AX.X, ALU.min))
                done(v.tensor_scalar(i, i, float(EXPERTS), None, ALU.add))
                done(v.tensor_scalar(hot, m.iota, i, None, ALU.is_equal))
                if hot is first:
                    done(v.scalar_tensor_tensor(rest, first, -4.0, rw, ALU.mult, ALU.add))
            done(v.tensor_tensor(diff, top2, top1, ALU.subtract))
            assert n[0] == 27
            v.wait_ge(s_act, 3)
            done(v.tensor_scalar(w_sum, e2, 1.0, None, ALU.add))
            done(v.reciprocal(w12[:, 0:1], w_sum))
            done(v.tensor_tensor(w12[:, 1:2], e2, w12[:, 0:1], ALU.mult))
            done(v.tensor_copy(idx_int[:, 0:1], i1))
            done(v.tensor_copy(idx_int[:, 1:2], i2))
            done(v.tensor_scalar(tmp, first, w12[:, 0:1], None, ALU.mult))
            done(v.scalar_tensor_tensor(dense, second, w12[:, 1:2], tmp, ALU.mult, ALU.add))
            assert n[0] == 34
            v.wait_ge(s_pe, 3)
            done(v.tensor_copy(dense_T, WT))
            v.wait_ge(s_pe, 4)
            done(v.tensor_copy(b2_mix, B2))
            done(v.tensor_tensor(m.shift_beta[:, :], m.beta[:, :], m.gamma[:, :], ALU.subtract))

        @block.sync
        def _(sp):
            sp.wait_ge(s_v, 32)
            sp.dma_start(m.d_expert, idx_int).then_inc(kept, 16)
            sp.dma_start(m.d_weight, w12).then_inc(kept, 16)
            sp.wait_ge(s_v, 36)
            sp.dma_start(m.d_b2, b2_mix).then_inc(kept, 16)
            sp.wait_ge(kept, 48)
            sp.dma_start(m.expert[:, :], m.d_expert.rearrange("g r -> (g r)").rearrange("(a n) -> a n", a=1))\
              .then_inc(back, 16)
            sp.dma_start(m.weight[:, :], m.d_weight.rearrange("g r -> (g r)").partition_broadcast(P)).then_inc(back, 16)
            sp.wait_ge(back, 32)


def experts(nc, m, out):
    with ExitStack() as ctx:
        def sem(name):
            return ctx.enter_context(nc.semaphore("e_" + name))

        w1_in = [sem(f"w1_in{i}") for i in range(2)]
        b2_in = [sem(f"b2_in{i}") for i in range(2)]
        stored = [sem(f"stored{i}") for i in range(4)]
        z_mul, z_ready, r_ready, xb_ready = sem("z_mul"), sem("z_ready"), sem("r_ready"), sem("xb_ready")
        t_done, zT_copied = sem("t_done"), sem("zT_copied")
        h_done, g_ready = sem("h_done"), sem("g_ready")
        y_done, y_first, y_used = sem("y_done"), sem("y_first"), sem("y_used")
        stats_done, rstd_done = sem("stats_done"), sem("rstd_done")
        f_ready, fg_mul, out_ready = sem("f_ready"), sem("fg_mul"), sem("out_ready")
        rstd = Rstd(nc, m, rstd_done)
        bk = m.banks
        T_B, H_B, Y_B = 0, 1, 3
        w2 = m.w2x[:, :, :, :].rearrange("p e c d -> p (e c d)")
        w1 = m.w1x[:, :, :].rearrange("p e f -> p (e f)")
        CH = FF // P
        block = ctx.enter_context(nc.Block())

        @block.sync
        def _(sp):
            def step(f):
                if f.live(0):
                    s, q = f.group(), f.slot(0, 2)
                    if f.past(0, 2):
                        sp.wait_ge(h_done, GRP * (s - 1))
                        hold(sp, m)
                    for n in range(GRP * TOPK):
                        e = sp.value_load(m.expert[0:1, bass.ds(s * (GRP * TOPK) + n, 1)], min_val=0, max_val=EXPERTS - 1)
                        sp.dma_start(m.w1_top[:, q, n, :], w1[:, bass.ds(e * FF, FF)]).then_inc(w1_in[q], 16)
                    if f.past(0, 2):
                        sp.wait_ge(r_ready, s - 1)
                    sp.dma_start(m.b2_all[:, q, :], m.d_b2[bass.ds(s * GRP, GRP), :].rearrange("g d -> (g d)")
                                 .partition_broadcast(P)).then_inc(b2_in[q], 16)
                if f.live(8):
                    s, k = f.group(8), f.slot(8, 4)
                    sp.wait_ge(out_ready, s + 1)
                    hold(sp, m)
                    sp.dma_start(out[bass.ds(s * GRP, GRP), :, :].rearrange("g n d -> n g d"),
                                 by_graph(m.out_s[:, k, :])).then_inc(stored[k], 16)

            run_frames(sp, step, 8, 2)
            for k in range(4):
                sp.wait_ge(stored[k], 16 * (NG // 4))

        @block.gpsimd
        def _(pool):
            def step(f):
                if f.live(0):
                    s, q = f.group(), f.slot(0, 2)
                    if f.past(0, 2):
                        pool.wait_ge(t_done, s - 1)
                        pool.wait_ge(r_ready, s - 1)
                    make_z(pool, m, s, q, m.rstd3[:, bass.ds(s * GRP, GRP)], m.shift3[:, bass.ds(s * GRP, GRP)],
                           z_mul, z_ready)
                    pool.wait_ge(z_ready, s + 1)
                    pool.wait_ge(b2_in[q], 16 * (2 * f.it + f.k // 2 + 1))
                    if f.past(0, 2):
                        pool.wait_ge(y_used, GRP * (s - 1))
                    pool.tensor_tensor(m.r_s[:, q, :], m.z[:, q, :], m.b2_all[:, q, :], ALU.add).then_inc(r_ready, 1)
                if f.live(5):
                    s, k = f.group(5), f.slot(5, 4)
                    if f.past(5, 4):
                        pool.wait_ge(out_ready, s - 3)
                    pool.tensor_tensor(by_graph(m.xb_s[:, k, :]), by_graph(grp(m.X, s)),
                                       m.shift_beta[:, :].unsqueeze(1).to_broadcast([P, GRP, D]), ALU.add)\
                        .then_inc(xb_ready, 1)

            run_frames(pool, step, 5, 4)

        @block.tensor
        def _(pe):
            def hidden(f, j):
                s, q = f.group(1), f.slot(1, 2)
                if j == 0:
                    pe.wait_ge(zT_copied, s + 1)
                    pe.wait_ge(w1_in[q], 16 * GRP * TOPK * (2 * f.it + (f.k - 1) // 2 + 1))
                if j >= 2 or f.past(1, 1):
                    pe.wait_ge(g_ready, GRP * s + j - 1)
                for n in range(TOPK * CH):
                    i = pe.matmul(bk[:, H_B + j % 2, n * P:(n + 1) * P],
                                  m.w1_top[:, q, TOPK * j + n // CH, (n % CH) * P:(n % CH + 1) * P],
                                  m.zT[:, q, j * D:(j + 1) * D], start=True, stop=True)
                i.then_inc(h_done, 1)

            def outputs(f, j):
                s = f.group(1)
                e = [pe.value_load(m.expert[0:1, bass.ds(s * (GRP * TOPK) + TOPK * j + n, 1)],
                                   min_val=0, max_val=EXPERTS - 1) for n in range(TOPK)]
                pe.wait_ge(g_ready, GRP * s + j + 1)
                if f.past(1, 1):
                    pe.wait_ge(y_used, GRP * (s - 1) + j + 1)
                for n in range(TOPK):
                    for c in range(CH):
                        i = pe.matmul(bk[:, Y_B + j, n * D:(n + 1) * D],
                                      m.g_s[:, j % 2, (n * CH + c) * P:(n * CH + c + 1) * P],
                                      w2[:, bass.ds(e[n] * FF + c * D, D)], start=c == 0, stop=c == CH - 1)
                i.then_inc(y_done, 1)

            def step(f):
                if f.live(1):
                    hidden(f, 0)
                    hidden(f, 1)
                    outputs(f, 0)
                    hidden(f, 2)
                    outputs(f, 1)
                    hidden(f, 3)
                    outputs(f, 2)
                if f.live(0):
                    s, q = f.group(), f.slot(0, 2)
                    pe.wait_ge(z_ready, s + 1)
                    if f.past(0, 1):
                        pe.wait_ge(zT_copied, s)
                    transpose_graphs(pe, bk[:, T_B, :], m.z[:, q, :], m.ident, t_done)
                if f.live(1):
                    outputs(f, 3)

            run_frames(pe, step, 1, 2)

        @block.scalar
        def _(act):
            def step(f):
                if f.live(5):
                    s, k, q = f.group(5), f.slot(5, 4), f.slot(5, 2)
                    p, r, odd = f.pair(6 - f.k % 2), k // 2, k % 2
                    act.wait_ge(rstd_done, (p + 1) * Rstd.STEPS)
                    if f.past(5, 2):
                        act.wait_ge(out_ready, s - 1)
                    for j in range(GRP):
                        c = slice(j * D, (j + 1) * D)
                        i = act.activation(m.f_s[:, q, c], m.o_s[:, k, c], ACT.Identity,
                                           bias=m.shift[:, r, GRP * odd + j:GRP * odd + j + 1],
                                           scale=m.rstd[:, r, GRP * odd + j:GRP * odd + j + 1])
                    i.then_inc(f_ready, 1)
                if f.live(1):
                    s = f.group(1)
                    for j in range(GRP):
                        act.wait_ge(h_done, GRP * s + j + 1)
                        if j >= 2 or f.past(1, 1):
                            act.wait_ge(y_done, GRP * s + j - 1)
                        act.activation(m.g_s[:, j % 2, :], bk[:, H_B + j % 2, :], ACT.Gelu).then_inc(g_ready, 1)
                if f.live(0):
                    s, q = f.group(), f.slot(0, 2)
                    act.wait_ge(t_done, s + 1)
                    if f.past(0, 2):
                        act.wait_ge(h_done, GRP * (s - 1))
                    act.copy(m.zT[:, q, :], bk[:, T_B, :]).then_inc(zT_copied, 1)

            run_frames(act, step, 5, 2)

        @block.vector
        def _(v):
            def step(f):
                def chain(*ns):
                    lag = 2 + f.k % 2
                    if f.live(lag):
                        r = ((f.k - lag) // 2) % 2
                        for n in ns:
                            rstd.step(n, f.pair(lag), m.rstd[:, r, :], m.shift[:, r, :])

                if f.k % 2 == 0 and f.live(2):
                    p = f.pair(2)
                    if f.past(2, 2):
                        v.wait_ge(rstd_done, p * Rstd.STEPS)
                    v.wait_ge(y_used, 2 * GRP * (p + 1))
                    hold(v, m)
                    for u in range(2):
                        statistics(v, m.stats, m.o_s[:, f.slot(2 - u, 4), :], 0, u, stats_done)
                    if f.past(2, 4):
                        v.wait_ge(f_ready, 2 * p - 2)
                    v.wait_ge(stats_done, 4 * (p + 1))
                first = 7 * (f.k % 2)
                chain(first)
                if f.live(0):
                    s, k, q = f.group(), f.slot(0, 4), f.slot(0, 2)
                    v.wait_ge(r_ready, s + 1)
                    if f.past(0, 4):
                        v.wait_ge(f_ready, s - 3)

                    def second(j):
                        c = slice(j * D, (j + 1) * D)
                        v.wait_ge(y_first, GRP * s + j + 1)
                        v.scalar_tensor_tensor(m.o_s[:, k, c], bk[:, Y_B + j, D:2 * D],
                                               m.weight[:, bass.ds(s * (GRP * TOPK) + TOPK * j + 1, 1)], m.y_s[:, j, :],
                                               ALU.mult, ALU.add).then_inc(y_used, 1)

                    for j in range(GRP):
                        c = slice(j * D, (j + 1) * D)
                        v.wait_ge(y_done, GRP * s + j + 1)
                        if f.past(0, 1):
                            v.wait_ge(y_used, GRP * (s - 1) + j + 1)
                        v.scalar_tensor_tensor(m.y_s[:, j, :], bk[:, Y_B + j, 0:D],
                                               m.weight[:, bass.ds(s * (GRP * TOPK) + TOPK * j, 1)], m.r_s[:, q, c],
                                               ALU.mult, ALU.add).then_inc(y_first, 1)
                        chain(first + 1 + j)
                        if j:
                            second(j - 1)
                    second(GRP - 1)
                else:
                    chain(*range(first + 1, first + 5))
                chain(first + 5)
                if f.live(5):
                    s, q, k = f.group(5), f.slot(5, 2), f.slot(5, 4)
                    v.wait_ge(f_ready, s + 1)
                    v.wait_ge(xb_ready, s + 1)
                    v.tensor_tensor(by_graph(m.f_s[:, q, :]), by_graph(m.f_s[:, q, :]),
                                    m.gamma[:, :].unsqueeze(1).to_broadcast([P, GRP, D]), ALU.mult).then_inc(fg_mul, 1)
                    chain(first + 6)
                    v.wait_ge(fg_mul, s + 1)
                    if f.past(5, 4):
                        v.wait_ge(stored[k], 16 * (f.it - 1 - (f.k < 1)))
                    v.tensor_tensor(m.out_s[:, k, :], m.f_s[:, q, :], m.xb_s[:, k, :], ALU.add)\
                     .then_inc(out_ready, 1)
                else:
                    chain(first + 6)

            run_frames(v, step, 5, 4)


def kernel_program(nc, a, out):
    with ExitStack() as ctx:
        def sb(name, shape, dt=F32):
            return ctx.enter_context(nc.sbuf_tensor("sb_" + name, shape, dt))

        m = Memory()
        m.X = sb("X", [P, GRAPHS * D])
        m.MASK = sb("MASK", [P, GRAPHS * D], BF16)
        m.adj_in = sb("adj_in", [P, 4, W], I32)
        m.mask = sb("mask", [P, 4, W], BF16)
        m.z, m.zT, m.uT = (sb(name, [P, 2, W]) for name in ("z", "zT", "uT"))
        m.t_s = sb("t_s", [P, 2, W])
        m.l_s = sb("l_s", [P, 2, W])
        m.p_s = sb("p_s", [P, 2, W])
        m.pT = sb("pT", [P, 2, W])
        m.h_s, m.e_s = (sb(name, [P, 2, W]) for name in ("h_s", "e_s"))
        m.xv = sb("xv", [P, 4, GRP, 2 * D + 1])
        m.stats = sb("stats", [P, 8, 3])
        m.var, m.nhv, m.ra, m.rb, m.rt = (sb(name, [P, 8]) for name in ("var", "nhv", "ra", "rb", "rt"))
        m.seed = sb("seed", [P, 8], I32)
        m.rstd = sb("rstd", [P, 2, 8])
        m.shift = sb("shift", [P, 2, 8])
        m.rstd3 = sb("rstd3", [P, GRAPHS])
        m.shift3 = sb("shift3", [P, GRAPHS])
        m.nmin, m.nmax, m.rden = (sb(name, [P, 2, GRP]) for name in ("nmin", "nmax", "rden"))
        m.consts = sb("consts", [P, 2 * D + EXPERTS])
        m.ident, m.centre, m.iota = m.consts[:, 0:D], m.consts[:, D:2 * D], m.consts[:, 2 * D:]
        m.ones = sb("ones", [P, D])
        m.one_row = sb("one_row", [1, 2 * D])
        m.m_w = sb("m_w", [P, D])
        m.wf, m.wc = sb("wf", [P, D]), sb("wc", [P, D])
        m.src_w, m.dst_w = sb("src_w", [P, D]), sb("dst_w", [P, D])
        m.gamma, m.beta = sb("gamma", [P, D]), sb("beta", [P, D])
        m.w12 = sb("w12", [P, 2 * D])
        m.wr = sb("wr", [P, EXPERTS])
        m.br_row = sb("br_row", [1, EXPERTS])
        m.bias_less = sb("bias_less", [1, D])
        m.b2_rows = sb("b2_rows", [EXPERTS, D])
        m.w1x = sb("w1x", [P, EXPERTS, FF])
        m.w2x = sb("w2x", [P, EXPERTS, FF // P, D])
        floats = m.MASK[:, :].bitcast(F32)
        m.w1_raw = floats[:, 0:EXPERTS * FF]
        m.b1_all = floats[0:1, EXPERTS * FF:2 * EXPERTS * FF]
        m.raw = [floats[:, 2 * EXPERTS * FF + i * D:2 * EXPERTS * FF + (i + 1) * D] for i in range(6)]
        m.w12_in = floats[:, 2 * EXPERTS * FF + D:2 * EXPERTS * FF + 3 * D]
        m.banks = ctx.enter_context(nc.psum_tensor("banks", [P, 8, W], F32))
        m.node_sums = sb("node_sums", [P, GRAPHS])
        m.x_copy = sb("x_copy", [P, 4, W])
        m.for_rstd3 = Memory()
        m3 = m.for_rstd3
        m3.var, m3.nhv, m3.ra, m3.rb, m3.rt = (sb(name + "3", [P, 8]) for name in ("var", "nhv", "ra", "rb", "rt"))
        m3.stats, m3.seed = sb("stats3", [P, 8, 3]), sb("seed3", [P, 8], I32)
        m.held = {eng: ctx.enter_context(nc.semaphore(f"held{i}")) for i, eng in enumerate((nc.vector, nc.sync))}
        m.shift_beta = sb("shift_beta", [P, D])
        m.expert = sb("expert", [1, GRAPHS * TOPK], I32)
        m.weight = sb("weight", [P, GRAPHS * TOPK])
        m.d_expert = nc.dram_tensor("d_expert", (GRAPHS, TOPK), I32, kind="Internal").ap()
        m.d_weight = nc.dram_tensor("d_weight", (GRAPHS, TOPK), F32, kind="Internal").ap()
        m.d_b2 = nc.dram_tensor("d_b2", (GRAPHS, D), F32, kind="Internal").ap()
        m.w1_top = floats[:, 0:2 * GRP * TOPK * FF].rearrange("p (q n f) -> p q n f", q=2, n=GRP * TOPK)
        m.g_s, m.f_s, m.r_s, m.b2_all = m.uT, m.p_s, m.h_s, m.e_s
        m.y_s = m.t_s[:, 0, :].rearrange("p (j d) -> p j d", j=GRP)
        m.o_s = m.xv[:, :, :, :].rearrange("p a g n -> p (a g n)")[:, 0:4 * W].rearrange("p (k w) -> p k w", k=4)
        m.xb_s = m.x_copy
        m.out_s = m.adj_in[:, :, :].bitcast(F32)
        m.small = ctx.enter_context(nc.semaphore("small"))
        make_weights(nc, m, a)
        layer0(nc, m, a)
        linear(nc, m)
        layer1(nc, m)
        route(nc, m)
        experts(nc, m, out)


def kernel(**inputs):
    import numpy as np
    import concourse.bacc as bacc
    from concourse.bass_utils import run_bass_kernel_spmd

    arrays = {name: np.ascontiguousarray(v) for name, v in inputs.items()}
    arrays["consts"] = np.concatenate([np.eye(D), np.eye(D) - 1 / D, np.tile(np.arange(EXPERTS), (P, 1))], 1)\
        .astype(np.float32)
    arrays["one_row"] = np.concatenate([np.full((1, D), 1 / D), np.ones((1, D))], 1).astype(np.float32)
    nc = bacc.Bacc("TRN2", target_bir_lowering=False, num_devices=1)
    a = {name: nc.dram_tensor(f"in_{name}", v.shape, mybir.dt.from_np(v.dtype), kind="ExternalInput").ap()
         for name, v in arrays.items()}
    out = nc.dram_tensor("out_x", (GRAPHS, P, D), F32, kind="ExternalOutput").ap()
    kernel_program(nc, a, out)
    r = run_bass_kernel_spmd(nc, [{f"in_{name}": v for name, v in arrays.items()}], core_ids=[0])
    return r.results[0]["out_x"]
```

```python
from contextlib import ExitStack

import concourse.bass as bass
from concourse import mybir

F32 = mybir.dt.float32
BF16 = mybir.dt.bfloat16
I32 = mybir.dt.int32
ALU = mybir.AluOpType
ACT = mybir.ActivationFunctionType
AX = mybir.AxisListType

GRAPHS, P, D = 128, 128, 128
GRP = 4
W = GRP * D
NG = GRAPHS // GRP
UN = 4
EXPERTS, FF, TOPK = 8, 256, 2
EPS = 1e-5
MASKED = 4.5e16
SLOPE = 0.2
CAPACITY = float(-(-(GRAPHS * P * 5 // 4) // EXPERTS))
RSQRT_SEED = float(0x5F375A86)
RSTD_STEPS = 13


class Memory:
    pass


class Frames:

    def __init__(self, it, k, count, body):
        self.it, self.k, self.count, self.body = it, k, count, body

    def live(self, lag):
        return self.body or 0 <= self.it * UN + self.k - lag < self.count

    def group(self, lag=0):
        return self.it * UN + (self.k - lag)

    def pair(self, lag=0):
        return self.it * (UN // 2) + (self.k - lag) // 2

    def past(self, lag, n):
        return self.body or self.it * UN + self.k - lag >= n

    def slot(self, lag, n):
        return (self.k - lag) % n


def run_frames(eng, step, last_lag, history, ahead=0):
    first = -(-(last_lag + history) // UN)
    last = NG // UN - ahead
    assert first < last
    for t in range(first * UN):
        step(Frames(t // UN, t % UN, NG, False))
    with eng.Fori(first, last) as it:
        for k in range(UN):
            step(Frames(it, k, NG, True))
    for t in range(last * UN, NG + last_lag):
        step(Frames(t // UN, t % UN, NG, False))


def grp(t, s):
    return t[:, bass.ds(s * W, W)]


def by_graph(ap):
    return ap.rearrange("p (g d) -> p g d", g=GRP)


def each(v):
    return v.to_broadcast([P, GRP, D])


def hold(eng, m):
    eng.sem_inc(m.held[eng], 1)


class Rstd:

    STEPS = 14

    def __init__(self, nc, m, done):
        self.nc, self.m, self.done = nc, m, done

    def step(self, n, pair, rstd, shift, stats=None):
        v, m, done = self.nc.vector, self.m, self.done
        stats = m.stats if stats is None else stats
        mean, squares = stats[:, :, 1], stats[:, :, 2]
        if n:
            v.wait_ge(done, pair * self.STEPS + n)
        if n == 0:
            i = v.tensor_scalar(m.var[:, :], squares, 1.0 / D, EPS, ALU.mult, ALU.add)
        elif n == 1:
            i = v.tensor_scalar(m.nhv[:, :], squares, -0.5 / D, -0.5 * EPS, ALU.mult, ALU.add)
        elif n == 2:
            i = v.tensor_scalar(m.seed[:, :], m.var[:, :].bitcast(I32), -0.5, RSQRT_SEED, ALU.mult, ALU.add)
        elif n < 12:
            y = [m.seed[:, :].bitcast(F32), m.ra[:, :], m.rb[:, :], rstd]
            a, b = y[n // 3 - 1], y[n // 3]
            if n % 3 == 0:
                i = v.tensor_tensor(m.rt[:, :], a, a, ALU.mult)
            elif n % 3 == 1:
                i = v.tensor_tensor(m.rt[:, :], m.rt[:, :], m.nhv[:, :], ALU.mult)
            else:
                i = v.scalar_tensor_tensor(b, m.rt[:, :], 1.5, a, ALU.add, ALU.mult)
        elif n == 12:
            i = v.tensor_tensor(m.rt[:, :], mean, rstd, ALU.mult)
        else:
            i = v.tensor_scalar(shift, m.rt[:, :], -1.0, 1.0, ALU.mult, ALU.add)
        i.then_inc(done, 1)


def load_group(sp, m, a, s, k):
    sp.dma_start(by_graph(grp(m.X, s)),
                 a["x"][bass.ds(s * GRP, GRP), :, :].rearrange("g n d -> n g d")).then_inc(m.x_in[k], 16)


def make_weights(nc, m, a):
    with ExitStack() as ctx:
        s_in = ctx.enter_context(nc.semaphore("w_in"))
        s_pe = ctx.enter_context(nc.semaphore("w_product"))
        s_dve = ctx.enter_context(nc.semaphore("w_copied"))
        block = ctx.enter_context(nc.Block())
        bk = m.banks
        raw = m.raw
        wcT, a12T, b_s, a2b, a1b, asb, adb, wfT = (m.h_s[:, 0, 0:D], m.h_s[:, 0, D:2 * D], m.h_s[:, 0, 2 * D:3 * D],
                                                   m.h_s[:, 0, 3 * D:], m.h_s[:, 1, 0:D], m.h_s[:, 1, D:2 * D],
                                                   m.h_s[:, 1, 2 * D:3 * D], m.h_s[:, 1, 3 * D:])
        zero = m.e_s[:, 0, 0:D]
        wc1T = m.e_s[:, 0, D:2 * D]
        wr_in = m.e_s[:, 0, 2 * D:2 * D + EXPERTS]
        bias_row = m.e_s[0:1, 0, 3 * D:4 * D]
        vecs = m.e_s[:, 1, 0:8]

        LOADS = [(m.consts[:, :], a["consts"]), (m.one_row[:, :], a["one_row"]),
                 (raw[0], a["L0_gnn_W"]), (raw[1], a["L0_gnn_W_1"]), (raw[2], a["L0_gnn_W_2"]),
                 (raw[3], a["L0_gnn_a_12"]), (raw[4], a["L0_ffn_weight"]), (raw[5], a["L1_gnn_W"]),
                 (vecs[:, 0:1], a["L0_gnn_a_1"]), (vecs[:, 1:2], a["L0_gnn_a_2"]),
                 (vecs[:, 2:3], a["L1_gnn_a"][0:D, :]), (vecs[:, 3:4], a["L1_gnn_a"][D:2 * D, :]),
                 (bias_row, a["L0_ffn_bias"].rearrange("(a d) -> a d", a=1)),
                 (wr_in, a["L1_ffn_Wr"]), (m.br_row[:, :], a["L1_ffn_br"].rearrange("(a e) -> a e", a=1)),
                 (m.b2_rows[:, :], a["L1_ffn_b2"]),
                 (m.gamma[:, :], a["L1_ffn_gamma"].partition_broadcast(P)),
                 (m.beta[:, :], a["L1_ffn_beta"].partition_broadcast(P))]
        N_IN = 16 * len(LOADS)

        @block.sync
        def _(sp):
            for to, of in LOADS[0::2]:
                sp.dma_start(to, of).then_inc(s_in, 16)
            for s in range(4):
                load_group(sp, m, a, s, s)
            sp.dma_start(m.w1x[:, :, :], a["L1_ffn_W1"].rearrange("e d f -> d e f")).then_inc(m.experts_in, 16)
            sp.dma_start(m.b1, a["L1_ffn_b1"].rearrange("e f -> (e f)").partition_broadcast(P)).then_inc(m.experts_in, 16)

        @block.scalar
        def _(act):
            for to, of in LOADS[1::2]:
                act.dma_start(to, of).then_inc(s_in, 16)

        def bank(i, n):
            return bk[:, i, 0:n]

        @block.tensor
        def _(pe):
            pe.wait_ge(s_in, N_IN)
            pe.matmul(bank(0, D), raw[0], m.centre, start=True, stop=True)
            pe.transpose(bank(1, D), raw[3], m.ident)
            pe.transpose(bank(2, D), raw[4], m.ident)
            pe.matmul(bank(3, D), raw[5], m.centre, start=True, stop=True)
            pe.matmul(bk[:, 4, 0:2 * D], m.centre, m.w12_in, start=True, stop=True)
            pe.matmul(bank(5, D), m.centre, raw[5], start=True, stop=True)
            pe.matmul(bank(6, EXPERTS), m.centre, wr_in, start=True, stop=True).then_inc(s_pe, 1)
            pe.wait_ge(s_dve, 1)
            pe.matmul(bank(0, D), a12T, wcT, start=True, stop=True)
            pe.matmul(bank(1, D), m.centre, wfT, start=True, stop=False)
            pe.matmul(bank(1, D), m.one_row[:, 0:D], m.bias_less[:, :], start=False, stop=True)
            pe.matmul(bank(2, D), wc1T, asb, start=True, stop=True)
            pe.matmul(bank(3, D), wc1T, adb, start=True, stop=True).then_inc(s_pe, 1)
            pe.wait_ge(s_dve, 2)
            pe.matmul(bank(0, D), wcT, b_s, start=True, stop=False)
            pe.matmul(bank(0, D), a1b, wcT, start=False, stop=True).then_inc(s_pe, 1)

        @block.vector
        def _(v):
            chain = m.small
            n = [0]

            def after(i):
                n[0] += 1
                i.then_inc(chain, 1)
                v.wait_ge(chain, n[0])

            v.wait_ge(s_in, N_IN)
            after(v.memset(zero, 0.0))
            for to, j, scale in ((a1b, 0, 1.0 / D), (a2b, 1, 1.0 / D), (asb, 2, -1.0), (adb, 3, -1.0)):
                after(v.tensor_scalar(to, zero, vecs[:, j:j + 1], scale, ALU.add, ALU.mult))
            after(v.tensor_scalar(m.bias_less[:, :], bias_row, 1.0, None, ALU.subtract))
            after(v.memset(m.xv[:, :, :, 2 * D:], 1.0))
            after(v.memset(m.ones[:, :], 1.0))
            v.wait_ge(s_pe, 1)
            after(v.tensor_copy(wcT, bank(0, D)))
            after(v.tensor_copy(a12T, bank(1, D)))
            after(v.tensor_copy(wfT, bank(2, D)))
            after(v.tensor_copy(wc1T, bank(3, D)))
            after(v.tensor_copy(m.w12[:, :], bk[:, 4, 0:2 * D]))
            after(v.tensor_copy(m.wc[:, :], bank(5, D)))
            after(v.tensor_scalar(m.wr[:, :], bank(6, EXPERTS), 1.0 / P, None, ALU.mult))
            v.sem_inc(s_dve, 1)
            v.wait_ge(s_pe, 2)
            after(v.tensor_tensor(b_s, bank(0, D), a2b, ALU.add))
            after(v.tensor_copy(m.wf[:, :], bank(1, D)))
            after(v.tensor_copy(m.src_w[:, :], bank(2, D)))
            after(v.tensor_copy(m.dst_w[:, :], bank(3, D)))
            v.sem_inc(s_dve, 1)
            v.wait_ge(s_pe, 3)
            after(v.tensor_scalar(m.m_w[:, :], bank(0, D), -1.0, None, ALU.mult))


def two_statistics(v, stats, x, first, u, j, done):
    v.bn_stats(stats[:, GRP * u + j:GRP * u + j + 2, :].rearrange("p a b -> p (a b)"),
               x[:, bass.ds(first + j * D, 2 * D)].rearrange("p (g d) -> p d g", g=2)).then_inc(done, 1)


def statistics(v, stats, x, first, u, done):
    for j in range(0, GRP, 2):
        two_statistics(v, stats, x, first, u, j, done)


def transpose_graphs(pe, to, of, ident, done):
    for j in range(GRP):
        i = pe.transpose(to[:, j * D:(j + 1) * D], of[:, j * D:(j + 1) * D], ident)
    i.then_inc(done, 1)


def make_z(pool, m, s, z, rstd, shift, z_mul, z_ready, before=None):
    zq = by_graph(z)
    pool.tensor_tensor(zq, by_graph(grp(m.X, s)), each(rstd), ALU.mult).then_inc(z_mul, 1)
    pool.wait_ge(z_mul, (s if before is None else before) + 1)
    pool.tensor_tensor(zq, zq, each(shift), ALU.add).then_inc(z_ready, 1)


def softmax_rows(act, m, q, done, sums=None):
    for j in range(GRP):
        i = act.activation(m.p_s[:, q, j * D:(j + 1) * D], m.l_s[:, q, j * D:(j + 1) * D], ACT.Exp,
                           bias=m.nmax[:, q, j:j + 1], scale=-1.0,
                           accum_out=None if sums is None else sums[:, q, j:j + 1])
    i.then_inc(done, 1)


CHAIN = (0, 1, 2, 3), (4, 5, 6, 7), (8, 9, 10), (11, 12, 13)


def of_group(t, s):
    return t[:, bass.ds(s * GRP, GRP)]


def statistics_of(v, m, s, j, done):
    v.bn_stats(m.all_stats[:, bass.ds(s * GRP + j, 2), :].rearrange("p a b -> p (a b)"),
               m.X[:, bass.ds(s * W + j * D, 2 * D)].rearrange("p (g d) -> p d g", g=2)).then_inc(done, 1)


def rstd_of_body(v, m, rstd, done, f, ns):
    b = f.it - 1
    for n in ns:
        if n == 0 and f.past(4, UN):
            v.wait_ge(done, b * Rstd.STEPS)
        here = bass.ds(b * (UN * GRP), UN * GRP)
        rstd.step(n, b, m.rstd3[:, here], m.shift3[:, here], m.all_stats[:, here, :])


EARLY = 2 * UN


def early_statistics(v, m, rstd, t):
    f = Frames(t // UN, t % UN, NG, False)
    if t == UN:
        v.wait_ge(m.f_stats_done, 2 * UN)
    if f.live(UN):
        rstd_of_body(v, m, rstd, m.f_rstd_done, f, CHAIN[f.k])
    for j in range(0, GRP, 2):
        statistics_of(v, m, t, j, m.f_stats_done)


def layer0(nc, m, a):
    with ExitStack() as ctx:
        def sem(name):
            return ctx.enter_context(nc.semaphore("a_" + name))

        adj_in = [sem(f"adj_in{i}") for i in range(4)]
        mask_kept = [sem(f"mask_kept{i}") for i in range(4)]
        masked, stats_done, rstd_done = sem("masked"), sem("stats_done"), sem("rstd_done")
        z_mul, z_ready = sem("z_mul"), sem("z_ready")
        t_done, zT_copied = sem("t_done"), sem("zT_copied")
        u_done, uT_copied = sem("u_done"), sem("uT_copied")
        xv_done, xv_copied = sem("xv_done"), sem("xv_copied")
        s_done, s_read = sem("s_done"), sem("s_read")
        max_ready, l_ready = sem("max_ready"), sem("l_ready")
        p_ready = sem("p_ready")
        pt_done, pT_copied = sem("pt_done"), sem("pT_copied")
        o_done, rden_done, h_done = sem("o_done"), sem("rden_done"), sem("h_done")
        e_done, ex_done, x_done = sem("e_done"), sem("ex_done"), sem("x_done")
        w1_done, w1_copied = sem("w1_done"), sem("w1_copied")
        rstd = Rstd(nc, m.four, rstd_done)
        linear_rstd = Rstd(nc, m.four, m.f_rstd_done)
        bk = m.banks
        T_B, PT_B, U_B, S_B, XV_B, O_B = 0, 1, 2, 3, 4, 6
        block = ctx.enter_context(nc.Block())

        @block.sync
        def _(sp):
            def step(f):
                if f.live(0) and f.past(0, 4):
                    s, k = f.group(), f.slot(0, 4)
                    sp.wait_ge(stats_done, 2 * (s - 3))
                    load_group(sp, m, a, s, k)
                if f.live(8):
                    s, k = f.group(8), f.slot(8, 4)
                    if f.past(8, 4):
                        sp.wait_ge(masked, s - 3)
                    sp.dma_start(by_graph(m.adj_in[:, k, :]),
                                 a["adj"][bass.ds(s * GRP, GRP), :, :].rearrange("g n d -> n g d")).then_inc(adj_in[k], 16)
                if f.live(12):
                    s, k = f.group(12), f.slot(12, 4)
                    sp.wait_ge(masked, s + 1)
                    sp.dma_start(grp(m.MASK, s), m.mask[:, k, :]).then_inc(mask_kept[k], 16)

            run_frames(sp, step, 12, 4)
            sp.dma_start(m.w2x[:, :, :, :], a["L1_ffn_W2"].rearrange("e (c p) d -> p e c d", p=P))\
              .then_inc(m.experts_in, 16)
            sp.wait_ge(m.experts_in, 48)
            for k in range(4):
                sp.wait_ge(mask_kept[k], 16 * (NG // 4))

        @block.gpsimd
        def _(pool):
            def step(f):
                s, q = f.group(), f.slot(0, 2)
                pool.wait_ge(rstd_done, (f.it + 1) * Rstd.STEPS)
                if f.past(0, 2):
                    pool.wait_ge(t_done, s - 1)
                make_z(pool, m, s, m.z[:, q, :], of_group(m.rstd3, s), of_group(m.shift3, s), z_mul, z_ready)

            run_frames(pool, step, 0, 2)

        @block.tensor
        def _(pe):
            def step(f):
                if f.live(0):
                    s, q = f.group(), f.slot(0, 2)
                    pe.wait_ge(z_ready, s + 1)
                    if f.past(0, 1):
                        pe.wait_ge(zT_copied, s)
                    transpose_graphs(pe, bk[:, T_B, :], m.z[:, q, :], m.ident, t_done)
                if f.live(3):
                    s, q = f.group(3), f.slot(3, 2)
                    pe.wait_ge(p_ready, s + 1)
                    if f.past(3, 1):
                        pe.wait_ge(pT_copied, s)
                    transpose_graphs(pe, bk[:, PT_B, :], m.p_s[:, q, :], m.ident, pt_done)
                if f.live(1):
                    s, q = f.group(1), f.slot(1, 2)
                    pe.wait_ge(zT_copied, s + 1)
                    if f.past(1, 1):
                        pe.wait_ge(uT_copied, s)
                    pe.matmul(bk[:, U_B, :], m.m_w[:, :], m.zT[:, q, :], start=True, stop=True).then_inc(u_done, 1)
                    if f.past(1, 1):
                        pe.wait_ge(xv_copied, s)
                    for j in range(GRP):
                        i = pe.matmul(bk[:, XV_B + j // 2, (j % 2) * 2 * D:(j % 2 + 1) * 2 * D],
                                      m.zT[:, q, j * D:(j + 1) * D], m.w12[:, :], start=True, stop=True)
                    i.then_inc(xv_done, 1)
                if f.live(1):
                    s, q = f.group(1), f.slot(1, 2)
                    pe.wait_ge(uT_copied, s + 1)
                    if f.past(1, 1):
                        pe.wait_ge(s_read, GRP * s)
                    for j in range(GRP):
                        c = slice(j * D, (j + 1) * D)
                        i = pe.matmul(bk[:, S_B, c], m.uT[:, q, c], m.zT[:, q, c], start=True, stop=True)
                    i.then_inc(s_done, 1)
                if f.live(3):
                    s, q, k = f.group(3), f.slot(3, 2), f.slot(3, 4)
                    pe.wait_ge(pT_copied, s + 1)
                    if f.past(3, 1):
                        pe.wait_ge(h_done, s)
                    for j in range(GRP):
                        i = pe.matmul(bk[:, O_B + j // 2, (j % 2) * (D + 1):(j % 2 + 1) * (D + 1)],
                                      m.pT[:, q, j * D:(j + 1) * D], m.xv[:, k, j, D:], start=True, stop=True)
                    i.then_inc(o_done, 1)

            pe.wait_ge(m.experts_in, 32)
            for e in range(EXPERTS):
                pe.matmul(bk[:, e, 0:FF], m.centre, m.w1x[:, e, :], start=True, stop=True).then_inc(w1_done, 1)
            pe.wait_ge(w1_copied, EXPERTS)
            run_frames(pe, step, 3, 1)

        @block.scalar
        def _(act):
            def step(f):
                if f.live(0):
                    s, q = f.group(), f.slot(0, 2)
                    act.wait_ge(t_done, s + 1)
                    if f.past(0, 2):
                        act.wait_ge(s_done, s - 1)
                    act.copy(m.zT[:, q, :], bk[:, T_B, :]).then_inc(zT_copied, 1)
                if f.live(3):
                    s, q = f.group(3), f.slot(3, 2)
                    act.wait_ge(pt_done, s + 1)
                    if f.past(3, 2):
                        act.wait_ge(o_done, s - 1)
                    act.copy(m.pT[:, q, :], bk[:, PT_B, :]).then_inc(pT_copied, 1)
                if f.live(1):
                    s, q = f.group(1), f.slot(1, 2)
                    act.wait_ge(u_done, s + 1)
                    if f.past(1, 2):
                        act.wait_ge(s_done, s - 1)
                    act.copy(m.uT[:, q, :], bk[:, U_B, :]).then_inc(uT_copied, 1)
                if f.live(2):
                    s, q = f.group(2), f.slot(2, 2)
                    act.wait_ge(l_ready, s + 1)
                    if f.past(2, 2):
                        act.wait_ge(pt_done, s - 1)
                    softmax_rows(act, m, q, p_ready)
                if f.live(1):
                    s, k = f.group(1), f.slot(1, 4)
                    act.wait_ge(xv_done, s + 1)
                    if f.past(1, 4):
                        act.wait_ge(h_done, s - 3)
                    act.copy(m.xv[:, k, :, 0:2 * D].rearrange("p (b j) n -> p b j n", b=2),
                             bk[:, XV_B:XV_B + 2, :].rearrange("p b (j n) -> p b j n", j=2)).then_inc(xv_copied, 1)
                if f.live(4):
                    s, q = f.group(4), f.slot(4, 2)
                    act.wait_ge(h_done, s + 1)
                    if f.past(4, 2):
                        act.wait_ge(x_done, s - 1)
                    act.activation(m.e_s[:, q, :], m.h_s[:, q, :], ACT.Exp).then_inc(e_done, 1)

            run_frames(act, step, 4, 4)

        @block.vector
        def _(v):
            def step(f):
                def chain(*ns):
                    if f.live(4):
                        rstd_of_body(v, m, rstd, rstd_done, f, ns)

                def measure(j):
                    if f.live(0):
                        if j == 0:
                            v.wait_ge(m.x_in[f.k], 16 * (f.it + 1))
                            hold(v, m)
                        statistics_of(v, m, f.group(), j, stats_done)

                if not f.body and f.it * UN + f.k < EXPERTS:
                    e = f.it * UN + f.k
                    v.wait_ge(w1_done, e + 1)
                    v.scalar_tensor_tensor(m.w1x[:, e, :], m.b1[:, e * FF:(e + 1) * FF], 1.0 / P, bk[:, e, 0:FF],
                                           ALU.mult, ALU.add).then_inc(w1_copied, 1)
                ns = CHAIN[f.k]
                if f.k == 0 and f.live(4):
                    v.wait_ge(stats_done, 2 * UN * f.it)
                if f.live(11):
                    s, q, k = f.group(11), f.slot(11, 2), f.slot(11, 4)
                    v.wait_ge(s_done, s + 1)
                    v.wait_ge(masked, s + 1)
                    if f.past(11, 2):
                        v.wait_ge(l_ready, s - 1)
                    hold(v, m)
                    for j in range(GRP):
                        c = slice(j * D, (j + 1) * D)
                        v.tensor_tensor_reduce(m.t_s[:, q, c], bk[:, S_B, c], m.mask[:, k, c], 1.0, 3.0e38,
                                               ALU.add, ALU.min, m.nmin[:, q, j:j + 1]).then_inc(s_read, 1)
                        chain(*ns[j:j + 1])
                    v.wait_ge(s_read, GRP * (s + 1))
                    if f.past(11, 2):
                        v.wait_ge(p_ready, s - 1)
                    v.scalar_tensor_tensor(m.nmax[:, q, :], m.nmin[:, q, :], SLOPE, m.nmin[:, q, :], ALU.mult, ALU.min)\
                     .then_inc(max_ready, 1)
                    v.scalar_tensor_tensor(m.l_s[:, q, :], m.t_s[:, q, :], SLOPE, m.t_s[:, q, :], ALU.mult, ALU.min)\
                     .then_inc(l_ready, 1)
                else:
                    chain(*ns)
                if f.live(8):
                    s, k = f.group(8), f.slot(8, 4)
                    v.wait_ge(adj_in[k], 16 * (f.it - 1))
                    if f.past(8, 4):
                        v.wait_ge(mask_kept[k], 16 * (f.it - 2))
                        v.wait_ge(s_read, GRP * (s - 3))
                    v.tensor_scalar(m.mask[:, k, :], m.adj_in[:, k, :], 0, MASKED, ALU.is_le, ALU.mult)\
                     .then_inc(masked, 1)
                measure(0)
                if f.live(13):
                    s, q, k = f.group(13), f.slot(13, 2), f.slot(13, 4)
                    v.wait_ge(o_done, s + 1)
                    if f.past(13, 1):
                        v.wait_ge(h_done, s)
                    v.reciprocal(m.rden[:, q, :].rearrange("p (b j) -> p b j", b=2),
                                 bk[:, O_B:O_B + 2, D:2 * (D + 1):D + 1]).then_inc(rden_done, 1)
                    measure(2)
                    v.wait_ge(rden_done, s + 1)
                    if f.past(13, 2):
                        v.wait_ge(x_done, s - 1)
                    for j in range(GRP):
                        o = (j % 2) * (D + 1)
                        i = v.scalar_tensor_tensor(m.h_s[:, q, j * D:(j + 1) * D], bk[:, O_B + j // 2, o:o + D],
                                                   m.rden[:, q, j:j + 1], m.xv[:, k, j, 0:D], ALU.mult, ALU.add)
                    i.then_inc(h_done, 1)
                else:
                    measure(2)
                if f.live(14):
                    s, q = f.group(14), f.slot(14, 2)
                    v.wait_ge(e_done, s + 1)
                    v.scalar_tensor_tensor(m.e_s[:, q, :], m.e_s[:, q, :], 1.0, grp(m.X, s), ALU.min, ALU.add)\
                     .then_inc(ex_done, 1)
                    v.wait_ge(ex_done, s + 1)
                    v.scalar_tensor_tensor(grp(m.X, s), m.h_s[:, q, :], 0.0, m.e_s[:, q, :], ALU.max, ALU.add)\
                     .then_inc(x_done, 1)

                t = 0 if f.body else f.it * UN + f.k - NG
                if not f.body and 0 <= t < EARLY:
                    if t == 0:
                        v.wait_ge(z_ready, EARLY)
                    if t == UN:
                        v.wait_ge(rstd_done, NG // UN * Rstd.STEPS)
                    v.wait_ge(x_done, EARLY)
                    early_statistics(v, m, linear_rstd, t)

            run_frames(v, step, 14, 2)


def linear(nc, m):
    with ExitStack() as ctx:
        def sem(name):
            return ctx.enter_context(nc.semaphore("f_" + name))

        stats_done, rstd_done = m.f_stats_done, m.f_rstd_done
        z_act_ready, z_mul, z_pool_ready = sem("z_act_ready"), sem("z_mul"), sem("z_pool_ready")
        t_done, zT_copied = sem("t_done"), sem("zT_copied")
        y_done, x_done = sem("y_done"), sem("x_done")
        rstd = Rstd(nc, m.four, rstd_done)
        layer1_rstd = Rstd(nc, m, m.b_rstd_done)
        bk = m.banks
        z, zT = m.z_lin, m.zT_lin
        T_B, Y_B = 0, 2
        LAG = 12
        block = ctx.enter_context(nc.Block())

        @block.gpsimd
        def _(pool):
            def step(f):
                if f.k == UN - 1:
                    s = f.group()
                    pool.wait_ge(rstd_done, (f.it + 1) * Rstd.STEPS)
                    if f.past(0, 4):
                        pool.wait_ge(t_done, s - 3)
                    make_z(pool, m, s, z[:, f.k, :], of_group(m.rstd3, s), of_group(m.shift3, s), z_mul, z_pool_ready, f.it)

            run_frames(pool, step, 0, 4)

        @block.tensor
        def _(pe):
            def step(f):
                if f.live(0):
                    s, q, k = f.group(), f.slot(0, 2), f.slot(0, 4)
                    if f.k == UN - 1:
                        pe.wait_ge(z_pool_ready, f.it + 1)
                    else:
                        pe.wait_ge(z_act_ready, (UN - 1) * f.it + f.k + 1)
                    if f.past(0, 2):
                        pe.wait_ge(zT_copied, s - 1)
                    transpose_graphs(pe, bk[:, T_B + q, :], z[:, k, :], m.ident, t_done)
                if f.live(1):
                    s, k = f.group(1), f.slot(1, 4)
                    pe.wait_ge(zT_copied, s + 1)
                    if f.past(1, 4):
                        pe.wait_ge(x_done, s - 3)
                    for j in range(GRP):
                        c = slice(j * D, (j + 1) * D)
                        i = pe.matmul(bk[:, Y_B + k, c], zT[k][:, c], m.wf[:, :], start=True, stop=True)
                    i.then_inc(y_done, 1)

            run_frames(pe, step, 1, 4)

        @block.scalar
        def _(act):
            def step(f):
                if f.k < UN - 1 and f.live(0):
                    s, k = f.group(), f.slot(0, 4)
                    act.wait_ge(rstd_done, (f.it + 1) * Rstd.STEPS)
                    if f.past(0, 4):
                        act.wait_ge(t_done, s - 3)
                    for j in range(GRP):
                        n = s * GRP + j
                        i = act.activation(z[:, k, j * D:(j + 1) * D], m.X[:, bass.ds(s * W + j * D, D)], ACT.Identity,
                                           bias=m.shift3[:, bass.ds(n, 1)], scale=m.rstd3[:, bass.ds(n, 1)])
                    i.then_inc(z_act_ready, 1)
                if f.live(1):
                    s, q, k = f.group(1), f.slot(1, 2), f.slot(1, 4)
                    act.wait_ge(t_done, s + 1)
                    if f.past(1, 4):
                        act.wait_ge(y_done, s - 3)
                    act.copy(zT[k], bk[:, T_B + q, :]).then_inc(zT_copied, 1)

            run_frames(act, step, 1, 4)

        @block.vector
        def _(v):
            def step(f):
                def chain(*ns):
                    if f.live(4) and f.past(0, EARLY):
                        rstd_of_body(v, m, rstd, rstd_done, f, ns)

                def add(half):
                    if f.live(LAG):
                        s, k = f.group(LAG), f.slot(LAG, 4)
                        if half == 0:
                            v.wait_ge(y_done, s + 1)
                        x = m.X[:, bass.ds(s * W + half * 2 * D, 2 * D)]
                        i = v.tensor_tensor(x, x, bk[:, Y_B + k, half * 2 * D:(half + 1) * 2 * D], ALU.add)
                        if half:
                            i.then_inc(x_done, 1)

                ns = CHAIN[f.k]
                if f.k == 0 and f.live(4) and f.past(0, EARLY):
                    v.wait_ge(stats_done, 2 * UN * f.it)
                chain(ns[0])
                if f.live(0) and f.past(0, EARLY):
                    statistics_of(v, m, f.group(), 0, stats_done)
                chain(ns[1])
                add(0)
                chain(ns[2])
                if f.live(0) and f.past(0, EARLY):
                    statistics_of(v, m, f.group(), 2, stats_done)
                chain(*ns[3:])
                add(1)

                t = 0 if f.body else f.it * UN + f.k - NG
                if t == 1:
                    v.wait_ge(x_done, 2)
                    for u in range(2):
                        statistics(v, m.stats, m.X, u * W, u, m.b_stats_done)
                    v.wait_ge(m.b_stats_done, 4)
                if 1 <= t <= Rstd.STEPS // 2:
                    for n in (2 * t - 2, 2 * t - 1):
                        layer1_rstd.step(n, 0, m.rstd[:, 0, :], m.shift[:, 0, :])

            run_frames(v, step, LAG, 4)


def layer1(nc, m):
    with ExitStack() as ctx:
        def sem(name):
            return ctx.enter_context(nc.semaphore("b_" + name))

        mask_in = [sem(f"mask_in{i}") for i in range(4)]
        x_copied = [sem(f"x_copied{i}") for i in range(4)]
        stats_done, rstd_done = m.b_stats_done, m.b_rstd_done
        stats3_done, rstd3_done = sem("stats3_done"), sem("rstd3_done")
        z_mul, z_ready = sem("z_mul"), sem("z_ready")
        t_done, zT_copied = sem("t_done"), sem("zT_copied")
        wh_done, wh_copied = sem("wh_done"), sem("wh_copied")
        s_done, s_read = sem("s_done"), sem("s_read")
        max_ready, l_ready = sem("max_ready"), sem("l_ready")
        p_ready = sem("p_ready")
        pt_done, pT_copied = sem("pt_done"), sem("pT_copied")
        o_done, rden_done, h_done = sem("o_done"), sem("rden_done"), sem("h_done")
        x_done, mean_done = sem("x_done"), sem("mean_done")
        mean_copied = sem("mean_copied")
        rstd = Rstd(nc, m, rstd_done)
        rstd3 = Rstd(nc, m.for_rstd3, rstd3_done)
        bk = m.banks
        T_B, PT_B, WH_B, S_B, MEAN_B, O_B = 0, 1, 2, 3, 5, 6
        block = ctx.enter_context(nc.Block())

        @block.sync
        def _(sp):
            def step(f):
                if f.live(0):
                    s, k = f.group(), f.slot(0, 4)
                    if f.past(0, 4):
                        sp.wait_ge(s_read, GRP * (s - 3))
                    sp.dma_start(m.mask[:, k, :], grp(m.MASK, s)).then_inc(mask_in[k], 16)
                if f.live(8):
                    s, k = f.group(8), f.slot(8, 4)
                    sp.wait_ge(x_done, s + 1)
                    hold(sp, m)
                    if f.past(8, 4):
                        sp.wait_ge(mean_done, s - 3)
                    sp.dma_start(m.x_copy[:, k, :], grp(m.X, s)).then_inc(x_copied[k], 16)

            run_frames(sp, step, 8, 4)

        @block.gpsimd
        def _(pool):
            def step(f):
                s, q = f.group(), f.slot(0, 2)
                p, r = f.pair(f.k % 2), (f.k // 2) % 2
                pool.wait_ge(rstd_done, (p + 1) * Rstd.STEPS)
                if f.past(0, 2):
                    pool.wait_ge(t_done, s - 1)
                half = slice(GRP * (f.k % 2), GRP * (f.k % 2) + GRP)
                make_z(pool, m, s, m.z[:, q, :], m.rstd[:, r, half], m.shift[:, r, half], z_mul, z_ready)

            run_frames(pool, step, 0, 2)

        @block.tensor
        def _(pe):
            def step(f):
                if f.live(0):
                    s, q = f.group(), f.slot(0, 2)
                    pe.wait_ge(z_ready, s + 1)
                    if f.past(0, 1):
                        pe.wait_ge(zT_copied, s)
                    transpose_graphs(pe, bk[:, T_B, :], m.z[:, q, :], m.ident, t_done)
                if f.live(3):
                    s, q = f.group(3), f.slot(3, 2)
                    pe.wait_ge(p_ready, s + 1)
                    if f.past(3, 1):
                        pe.wait_ge(pT_copied, s)
                    transpose_graphs(pe, bk[:, PT_B, :], m.p_s[:, q, :], m.ident, pt_done)
                if f.live(1):
                    s, q = f.group(1), f.slot(1, 2)
                    pe.wait_ge(zT_copied, s + 1)
                    if f.past(1, 2):
                        pe.wait_ge(s_read, GRP * (s - 1))
                    pe.matmul(bk[:, S_B + q, :], m.dst_w[:, :], m.zT[:, q, :], start=True, stop=False)
                    for j in range(GRP):
                        c = slice(j * D, (j + 1) * D)
                        i = pe.matmul(bk[:, S_B + q, c], m.zT[:, q, c], m.src_w[:, :], start=False, stop=j == GRP - 1)
                    i.then_inc(s_done, 1)
                    if f.past(1, 1):
                        pe.wait_ge(wh_copied, s)
                    for j in range(GRP):
                        c = slice(j * D, (j + 1) * D)
                        i = pe.matmul(bk[:, WH_B, c], m.zT[:, q, c], m.wc[:, :], start=True, stop=True)
                    i.then_inc(wh_done, 1)
                if f.live(3):
                    s, q, k = f.group(3), f.slot(3, 2), f.slot(3, 4)
                    pe.wait_ge(pT_copied, s + 1)
                    if f.past(3, 2):
                        pe.wait_ge(h_done, s - 1)
                    for j in range(GRP):
                        c = slice(j * D, (j + 1) * D)
                        i = pe.matmul(bk[:, O_B + q, c], m.pT[:, q, c], m.xv[:, k, j, D:2 * D],
                                      start=True, stop=True)
                    i.then_inc(o_done, 1)
                if f.live(8):
                    s, k = f.group(8), f.slot(8, 4)
                    pe.wait_ge(x_copied[k], 16 * (f.it - 1))
                    pe.wait_ge(rstd3_done, (f.pair(8 + f.k % 2) + 1) * Rstd.STEPS)
                    for j in range(GRP):
                        i = pe.matmul(bk[:, MEAN_B, bass.ds(s * GRP + j, 1)], m.x_copy[:, k, j * D:(j + 1) * D],
                                      m.rstd3[:, bass.ds(s * GRP + j, 1)], start=True, stop=True)
                    i.then_inc(mean_done, 1)

            run_frames(pe, step, 8, 1)

        @block.scalar
        def _(act):
            def step(f):
                if f.live(0):
                    s, q = f.group(), f.slot(0, 2)
                    act.wait_ge(t_done, s + 1)
                    if f.past(0, 2):
                        act.wait_ge(wh_done, s - 1)
                    act.copy(m.zT[:, q, :], bk[:, T_B, :]).then_inc(zT_copied, 1)
                if f.live(4):
                    s, q = f.group(4), f.slot(4, 2)
                    act.wait_ge(o_done, s + 1)
                    act.wait_ge(rden_done, s + 1)
                    if f.past(4, 2):
                        act.wait_ge(x_done, s - 1)
                    for j in range(GRP):
                        c = slice(j * D, (j + 1) * D)
                        i = act.activation(m.h_s[:, q, c], bk[:, O_B + q, c], ACT.Relu,
                                           scale=m.rden[:, q, j:j + 1])
                    i.then_inc(h_done, 1)
                if f.live(3):
                    s, q = f.group(3), f.slot(3, 2)
                    act.wait_ge(pt_done, s + 1)
                    if f.past(3, 2):
                        act.wait_ge(o_done, s - 1)
                    act.copy(m.pT[:, q, :], bk[:, PT_B, :]).then_inc(pT_copied, 1)
                if f.live(2):
                    s, q = f.group(2), f.slot(2, 2)
                    act.wait_ge(l_ready, s + 1)
                    if f.past(2, 2):
                        act.wait_ge(pt_done, s - 1)
                    if f.past(2, 2):
                        act.wait_ge(rden_done, s - 1)
                    softmax_rows(act, m, q, p_ready, m.sums)
                if f.live(1):
                    s, k = f.group(1), f.slot(1, 4)
                    act.wait_ge(wh_done, s + 1)
                    if f.past(1, 4):
                        act.wait_ge(o_done, s - 3)
                    act.copy(m.xv[:, k, :, D:2 * D], by_graph(bk[:, WH_B, :])).then_inc(wh_copied, 1)

            run_frames(act, step, 4, 4)

        @block.vector
        def _(v):
            def step(f):
                def chain(*ns):
                    if f.live(f.k % 2) and f.past(f.k % 2, 2):
                        r = (f.k // 2) % 2
                        for n in ns:
                            rstd.step(n, f.pair(f.k % 2), m.rstd[:, r, :], m.shift[:, r, :])

                def chain3(*ns):
                    if f.live(10 + f.k % 2):
                        p = f.pair(10 + f.k % 2)
                        for n in ns:
                            rstd3.step(n, p, m.rstd3[:, bass.ds(p * 2 * GRP, 2 * GRP)],
                                       m.shift3[:, bass.ds(p * 2 * GRP, 2 * GRP)])

                if f.k % 2 == 0 and f.live(0) and f.past(0, 2):
                    p = f.pair()
                    v.wait_ge(rstd_done, p * Rstd.STEPS)
                    statistics(v, m.stats, m.X, f.group() * W, 0, stats_done)
                    statistics(v, m.stats, m.X, f.group() * W + W, 1, stats_done)
                    if f.past(0, 4):
                        v.wait_ge(z_ready, 2 * p - 2)
                    v.wait_ge(stats_done, 4 * (p + 1))
                if f.live(7):
                    s, q = f.group(7), f.slot(7, 2)
                    v.wait_ge(p_ready, s + 1)
                    if f.past(7, 2):
                        v.wait_ge(h_done, s - 1)
                    v.reciprocal(m.rden[:, q, :], m.sums[:, q, :]).then_inc(rden_done, 1)
                if f.k % 2 == 0 and f.live(10):
                    p = f.pair(10)
                    if f.past(10, 2):
                        v.wait_ge(rstd3_done, p * Rstd.STEPS)
                    v.wait_ge(x_done, 2 * (p + 1))
                    hold(v, m)
                    statistics(v, m.for_rstd3.stats, m.X, f.group(10) * W, 0, stats3_done)
                    statistics(v, m.for_rstd3.stats, m.X, f.group(10) * W + W, 1, stats3_done)
                    v.wait_ge(stats3_done, 4 * (p + 1))
                first = 7 * (f.k % 2)
                chain(first)
                chain3(first)
                if f.live(5):
                    s, q, k = f.group(5), f.slot(5, 2), f.slot(5, 4)
                    v.wait_ge(s_done, s + 1)
                    if f.past(5, 2):
                        v.wait_ge(l_ready, s - 1)
                    v.wait_ge(mask_in[k], 16 * (f.it - (f.k == 0)))
                    hold(v, m)
                    for j in range(GRP):
                        c = slice(j * D, (j + 1) * D)
                        v.tensor_tensor_reduce(m.t_s[:, q, c], bk[:, S_B + q, c], m.mask[:, k, c], 1.0, 3.0e38,
                                               ALU.add, ALU.min, m.nmin[:, q, j:j + 1]).then_inc(s_read, 1)
                        chain(first + 1 + j)
                        chain3(first + 1 + j)
                    v.wait_ge(s_read, GRP * (s + 1))
                    if f.past(5, 2):
                        v.wait_ge(p_ready, s - 1)
                    v.scalar_tensor_tensor(m.nmax[:, q, :], m.nmin[:, q, :], SLOPE, m.nmin[:, q, :], ALU.mult, ALU.min)\
                     .then_inc(max_ready, 1)
                    v.scalar_tensor_tensor(m.l_s[:, q, :], m.t_s[:, q, :], SLOPE, m.t_s[:, q, :], ALU.mult, ALU.min)\
                     .then_inc(l_ready, 1)
                else:
                    chain(*range(first + 1, first + 5))
                    chain3(*range(first + 1, first + 5))
                chain(first + 5)
                chain3(first + 5)
                if f.live(8):
                    s, q = f.group(8), f.slot(8, 2)
                    v.wait_ge(h_done, s + 1)
                    v.tensor_tensor(grp(m.X, s), grp(m.X, s), m.h_s[:, q, :], ALU.add).then_inc(x_done, 1)
                chain(first + 6)
                chain3(first + 6)

            run_frames(v, step, 11, 4)
            v.wait_ge(mean_done, NG)
            v.tensor_copy(m.node_sums[:, :], bk[:, MEAN_B, 0:GRAPHS]).then_inc(mean_copied, 1)
            v.wait_ge(mean_copied, 1)


def route(nc, m):
    with ExitStack() as ctx:
        s_pe = ctx.enter_context(nc.semaphore("r_product"))
        s_v = ctx.enter_context(nc.semaphore("r_vector"))
        s_act = ctx.enter_context(nc.semaphore("r_exp"))
        kept = ctx.enter_context(nc.semaphore("r_kept"))
        back = ctx.enter_context(nc.semaphore("r_back"))
        block = ctx.enter_context(nc.Block())
        bk = m.banks
        LG, LOAD, WT, B2 = bk[:, 0, 0:EXPERTS], bk[:, 1, 0:EXPERTS], bk[0:EXPERTS, 2, 0:D], bk[:, 3, 0:D]
        rows = m.l_s[:, 0, :].rearrange("p (r e) -> p r e", e=EXPERTS)
        ex, rw, scale, rw2, eq, first, second, rest, dense, tmp = (rows[:, i, :] for i in range(10))
        cols = m.l_s[:, 1, :]
        nmax, total, rtotal, top1, top2, i1, i2, diff, e2, w_sum = (cols[:, i:i + 1] for i in range(10))
        w12 = cols[:, 16:18]
        idx = cols[:, 20:22]
        idx_int = cols[:, 24:26].bitcast(I32)
        dense_T = m.t_s[0:EXPERTS, 0, 0:D]
        b2_mix = m.t_s[:, 1, 0:D]

        @block.tensor
        def _(pe):
            pe.matmul(LG, m.node_sums[:, :], m.wr[:, :], start=True, stop=False)
            pe.matmul(LG, m.one_row[:, D:2 * D], m.br_row[:, :], start=False, stop=True).then_inc(s_pe, 1)
            pe.wait_ge(s_v, 3)
            pe.matmul(LOAD, m.ones[:, :], rw, start=True, stop=True).then_inc(s_pe, 1)
            pe.wait_ge(s_v, 36)
            pe.transpose(WT, dense, m.ident).then_inc(s_pe, 1)
            pe.wait_ge(s_v, 37)
            pe.matmul(B2, dense_T, m.b2_rows[:, :], start=True, stop=True).then_inc(s_pe, 1)

        @block.scalar
        def _(act):
            act.wait_ge(s_v, 1)
            act.activation(ex, LG, ACT.Exp, bias=nmax, accum_out=total).then_inc(s_act, 1)
            act.wait_ge(s_v, 8)
            act.activation(ex, rw2, ACT.Exp, bias=nmax, accum_out=total).then_inc(s_act, 1)
            act.wait_ge(s_v, 29)
            act.activation(e2, diff, ACT.Exp).then_inc(s_act, 1)

        @block.vector
        def _(v):
            n = [0]

            def done(i):
                n[0] += 1
                i.then_inc(s_v, 1)
                v.wait_ge(s_v, n[0])

            v.wait_ge(s_pe, 1)
            done(v.tensor_reduce(nmax, LG, AX.X, ALU.max, negate=True))
            v.wait_ge(s_act, 1)
            done(v.reciprocal(rtotal, total))
            done(v.tensor_scalar(rw, ex, rtotal, None, ALU.mult))
            v.wait_ge(s_pe, 2)
            done(v.tensor_scalar(scale, LOAD, float(P), None, ALU.mult))
            done(v.reciprocal(tmp, scale))
            done(v.tensor_scalar(scale, tmp, CAPACITY, 1.0, ALU.mult, ALU.min))
            done(v.tensor_tensor(rw2, rw, scale, ALU.mult))
            done(v.tensor_reduce(nmax, rw2, AX.X, ALU.max, negate=True))
            v.wait_ge(s_act, 2)
            done(v.reciprocal(rtotal, total))
            done(v.tensor_scalar(rw, ex, rtotal, None, ALU.mult))
            done(v.tensor_copy(rest, rw))
            for top, i, hot in ((top1, i1, first), (top2, i2, second)):
                done(v.tensor_reduce(top, rest, AX.X, ALU.max))
                done(v.tensor_scalar(eq, rest, top, None, ALU.is_equal))
                done(v.tensor_scalar(tmp, m.iota, float(EXPERTS), None, ALU.subtract))
                done(v.tensor_tensor(tmp, tmp, eq, ALU.mult))
                done(v.tensor_reduce(i, tmp, AX.X, ALU.min))
                done(v.tensor_scalar(i, i, float(EXPERTS), None, ALU.add))
                done(v.tensor_scalar(hot, m.iota, i, None, ALU.is_equal))
                done(v.tensor_scalar(i, i, EXPERTS - 1.0, float(FF), ALU.min, ALU.mult))
                if hot is first:
                    done(v.scalar_tensor_tensor(rest, first, -4.0, rw, ALU.mult, ALU.add))
            done(v.tensor_tensor(diff, top2, top1, ALU.subtract))
            assert n[0] == 29
            v.wait_ge(s_act, 3)
            done(v.tensor_scalar(w_sum, e2, 1.0, None, ALU.add))
            done(v.reciprocal(w12[:, 0:1], w_sum))
            done(v.tensor_tensor(w12[:, 1:2], e2, w12[:, 0:1], ALU.mult))
            done(v.tensor_copy(idx_int[:, 0:1], i1))
            done(v.tensor_copy(idx_int[:, 1:2], i2))
            done(v.tensor_scalar(tmp, first, w12[:, 0:1], None, ALU.mult))
            done(v.scalar_tensor_tensor(dense, second, w12[:, 1:2], tmp, ALU.mult, ALU.add))
            assert n[0] == 36
            v.wait_ge(s_pe, 3)
            done(v.tensor_copy(dense_T, WT))
            v.wait_ge(s_pe, 4)
            done(v.tensor_copy(b2_mix, B2))
            done(v.tensor_tensor(m.shift_beta[:, :], m.beta[:, :], m.gamma[:, :], ALU.subtract))

        @block.sync
        def _(sp):
            sp.wait_ge(s_v, 34)
            sp.dma_start(m.d_expert, idx_int).then_inc(kept, 16)
            sp.dma_start(m.d_weight, w12).then_inc(kept, 16)
            sp.wait_ge(kept, 32)
            sp.dma_start(m.expert[:, :], m.d_expert.rearrange("g r -> (g r)").rearrange("(a n) -> a n", a=1))\
              .then_inc(back, 16)
            sp.dma_start(m.weight[:, :], m.d_weight.rearrange("g r -> (g r)").partition_broadcast(P)).then_inc(back, 16)
            sp.wait_ge(s_v, 38)
            sp.dma_start(m.d_b2, b2_mix).then_inc(kept, 16)
            sp.wait_ge(back, 32)
            sp.wait_ge(kept, 48)


def expert_columns(nc, m, eng, first, count):
    _, values = nc.values_load_multi_w_load_instructions(
        m.expert[0:1, bass.ds(first, count)], engines=[eng.engine], min_val=0, max_val=(EXPERTS - 1) * FF,
        skip_runtime_bounds_check_because="route() clamps the numbers of the experts")
    return values


def experts(nc, m, out):
    with ExitStack() as ctx:
        def sem(name):
            return ctx.enter_context(nc.semaphore("e_" + name))

        w1_in = [sem(f"w1_in{i}") for i in range(2)]
        b2_in = [sem(f"b2_in{i}") for i in range(2)]
        stored = [sem(f"stored{i}") for i in range(4)]
        z_mul, z_ready, r_ready, xb_ready = sem("z_mul"), sem("z_ready"), sem("r_ready"), sem("xb_ready")
        t_done, zT_copied, w1_copied = sem("t_done"), sem("zT_copied"), sem("w1_copied")
        h_done, g_ready = sem("h_done"), sem("g_ready")
        y_done, y_first, y_used = sem("y_done"), sem("y_first"), sem("y_used")
        stats_done, rstd_done = sem("stats_done"), sem("rstd_done")
        f_ready, fg_mul, out_ready = sem("f_ready"), sem("fg_mul"), sem("out_ready")
        rstd = Rstd(nc, m, rstd_done)
        bk = m.banks
        T_B, H_B, Y_B = 0, 1, 3
        w2 = m.w2x[:, :, :, :].rearrange("p e c d -> p (e c d)")
        w1 = m.w1x[:, :, :].rearrange("p e f -> p (e f)")
        CH = FF // P
        block = ctx.enter_context(nc.Block())

        @block.sync
        def _(sp):
            def step(f):
                if f.live(0):
                    s, q = f.group(), f.slot(0, 2)
                    if f.past(0, 2):
                        sp.wait_ge(h_done, GRP * (s - 1))
                        hold(sp, m)
                    e = expert_columns(nc, m, sp, s * (GRP * TOPK), GRP * TOPK)
                    for n in range(1, GRP * TOPK, TOPK):
                        sp.dma_start(m.w1_top[:, q, n, :], w1[:, bass.ds(e[n], FF)]).then_inc(w1_in[q], 16)
                    if f.past(0, 2):
                        sp.wait_ge(r_ready, s - 1)
                    sp.dma_start(m.b2_all[:, q, :], m.d_b2[bass.ds(s * GRP, GRP), :].rearrange("g d -> (g d)")
                                 .partition_broadcast(P)).then_inc(b2_in[q], 16)
                if f.live(8):
                    s, k = f.group(8), f.slot(8, 4)
                    sp.wait_ge(out_ready, s + 1)
                    hold(sp, m)
                    sp.dma_start(out[bass.ds(s * GRP, GRP), :, :].rearrange("g n d -> n g d"),
                                 by_graph(m.out_s[:, k, :])).then_inc(stored[k], 16)

            run_frames(sp, step, 8, 2)
            for k in range(4):
                sp.wait_ge(stored[k], 16 * (NG // 4))

        @block.gpsimd
        def _(pool):
            def step(f):
                if f.live(0):
                    s, q = f.group(), f.slot(0, 2)
                    if f.past(0, 2):
                        pool.wait_ge(t_done, s - 1)
                        pool.wait_ge(r_ready, s - 1)
                    make_z(pool, m, s, m.z[:, q, :], m.rstd3[:, bass.ds(s * GRP, GRP)], m.shift3[:, bass.ds(s * GRP, GRP)],
                           z_mul, z_ready)
                    pool.wait_ge(z_ready, s + 1)
                    pool.wait_ge(b2_in[q], 16 * (2 * f.it + f.k // 2 + 1))
                    if f.past(0, 4):
                        pool.wait_ge(y_used, GRP * (s - 3))
                    pool.tensor_tensor(m.r_s[:, f.slot(0, 4), :], m.z[:, q, :], m.b2_all[:, q, :], ALU.add).then_inc(r_ready, 1)
                if f.live(5):
                    s, k = f.group(5), f.slot(5, 4)
                    if f.past(5, 4):
                        pool.wait_ge(out_ready, s - 3)
                    pool.tensor_tensor(by_graph(m.xb_s[:, k, :]), by_graph(grp(m.X, s)),
                                       m.shift_beta[:, :].unsqueeze(1).to_broadcast([P, GRP, D]), ALU.add)\
                        .then_inc(xb_ready, 1)

            run_frames(pool, step, 5, 4)

        @block.tensor
        def _(pe):
            def hidden(f, j):
                s, q = f.group(1), f.slot(1, 2)
                if j == 0:
                    pe.wait_ge(zT_copied, s + 1)
                    pe.wait_ge(w1_in[q], 16 * GRP * (2 * f.it + (f.k - 1) // 2 + 1))
                    pe.wait_ge(w1_copied, s + 1)
                if j >= 2 or f.past(1, 1):
                    pe.wait_ge(g_ready, GRP * s + j - 1)
                for n in range(TOPK * CH):
                    i = pe.matmul(bk[:, H_B + j % 2, n * P:(n + 1) * P],
                                  m.w1_top[:, q, TOPK * j + n // CH, (n % CH) * P:(n % CH + 1) * P],
                                  m.zT[:, q, j * D:(j + 1) * D], start=True, stop=True)
                i.then_inc(h_done, 1)

            def outputs(f, lag, j):
                s = f.group(lag)
                e = expert_columns(nc, m, pe, s * (GRP * TOPK) + TOPK * j, TOPK)
                pe.wait_ge(g_ready, GRP * s + j + 1)
                if f.past(lag, 1):
                    pe.wait_ge(y_used, GRP * (s - 1) + j + 1)
                for n in range(TOPK):
                    for c in range(CH):
                        i = pe.matmul(bk[:, Y_B + j, n * D:(n + 1) * D],
                                      m.g_s[:, j % 2, (n * CH + c) * P:(n * CH + c + 1) * P],
                                      w2[:, bass.ds(e[n] + c * D, D)], start=c == 0, stop=c == CH - 1)
                i.then_inc(y_done, 1)

            def step(f):
                if f.live(1):
                    hidden(f, 0)
                if f.live(2):
                    outputs(f, 2, 3)
                if f.live(1):
                    hidden(f, 1)
                    outputs(f, 1, 0)
                    hidden(f, 2)
                    outputs(f, 1, 1)
                if f.live(0):
                    s, q = f.group(), f.slot(0, 2)
                    pe.wait_ge(z_ready, s + 1)
                    if f.past(0, 1):
                        pe.wait_ge(zT_copied, s)
                    transpose_graphs(pe, bk[:, T_B, :], m.z[:, q, :], m.ident, t_done)
                if f.live(1):
                    hidden(f, 3)
                    outputs(f, 1, 2)

            run_frames(pe, step, 2, 2)

        @block.scalar
        def _(act):
            def step(f):
                def normalise(j):
                    if f.live(5):
                        s, k = f.group(5), f.slot(5, 4)
                        p, r, odd = f.pair(6 - f.k % 2), k // 2, k % 2
                        if j == 0:
                            act.wait_ge(rstd_done, (p + 1) * Rstd.STEPS)
                            if f.past(5, 4):
                                act.wait_ge(out_ready, s - 3)
                        c = slice(j * D, (j + 1) * D)
                        act.activation(m.f_s[:, k, c], m.o_s[:, k, c], ACT.Identity,
                                       bias=m.shift[:, r, GRP * odd + j:GRP * odd + j + 1],
                                       scale=m.rstd[:, r, GRP * odd + j:GRP * odd + j + 1]).then_inc(f_ready, 1)

                def copy_zT():
                    if f.live(0):
                        s, q = f.group(), f.slot(0, 2)
                        act.wait_ge(t_done, s + 1)
                        if f.past(0, 2):
                            act.wait_ge(h_done, GRP * (s - 1))
                        act.copy(m.zT[:, q, :], bk[:, T_B, :]).then_inc(zT_copied, 1)

                for j in range(GRP):
                    if j == GRP - 1:
                        copy_zT()
                    if f.live(1):
                        s = f.group(1)
                        act.wait_ge(h_done, GRP * s + j + 1)
                        if j >= 2 or f.past(1, 1):
                            act.wait_ge(y_done, GRP * s + j - 1)
                        act.activation(m.g_s[:, j % 2, :], bk[:, H_B + j % 2, :], ACT.Gelu).then_inc(g_ready, 1)
                    if j:
                        normalise(j - 1)
                    if j == GRP - 1:
                        normalise(j)

            run_frames(act, step, 5, 4)

        @block.vector
        def _(v):
            def first_experts(s, q, past):
                e = expert_columns(nc, m, v, s * (GRP * TOPK), GRP * TOPK)
                if past:
                    v.wait_ge(h_done, GRP * (s - 1))
                    hold(v, m)
                for j in range(GRP):
                    i = v.tensor_copy(m.w1_top[:, q, TOPK * j, :], w1[:, bass.ds(e[TOPK * j], FF)])
                i.then_inc(w1_copied, 1)

            def step(f):
                def chain(*ns):
                    lag = 2 + f.k % 2
                    if f.live(lag):
                        r = ((f.k - lag) // 2) % 2
                        for n in ns:
                            rstd.step(n, f.pair(lag), m.rstd[:, r, :], m.shift[:, r, :])

                if f.live(-1):
                    first_experts(f.group(-1), f.slot(-1, 2), f.past(-1, 2))
                if f.k % 2 == 0 and f.live(2):
                    p = f.pair(2)
                    if f.past(2, 2):
                        v.wait_ge(rstd_done, p * Rstd.STEPS)
                    v.wait_ge(y_used, 2 * GRP * (p + 1))
                    hold(v, m)
                    for u in range(2):
                        statistics(v, m.stats, m.o_s[:, f.slot(2 - u, 4), :], 0, u, stats_done)
                    v.wait_ge(stats_done, 4 * (p + 1))
                if f.k % 2 and f.past(3, 4):
                    v.wait_ge(f_ready, GRP * (2 * f.pair(3) - 2))
                first = 7 * (f.k % 2)
                chain(first)
                if f.live(0):
                    s, k = f.group(), f.slot(0, 4)
                    v.wait_ge(r_ready, s + 1)

                    def second(j):
                        c = slice(j * D, (j + 1) * D)
                        v.wait_ge(y_first, GRP * s + j + 1)
                        if f.past(0, 4):
                            v.wait_ge(f_ready, GRP * (s - 4) + j + 1)
                        v.scalar_tensor_tensor(m.o_s[:, k, c], bk[:, Y_B + j, D:2 * D],
                                               m.weight[:, bass.ds(s * (GRP * TOPK) + TOPK * j + 1, 1)], m.y_s[:, j, :],
                                               ALU.mult, ALU.add).then_inc(y_used, 1)

                    for j in range(GRP):
                        c = slice(j * D, (j + 1) * D)
                        v.wait_ge(y_done, GRP * s + j + 1)
                        if f.past(0, 1):
                            v.wait_ge(y_used, GRP * (s - 1) + j + 1)
                        v.scalar_tensor_tensor(m.y_s[:, j, :], bk[:, Y_B + j, 0:D],
                                               m.weight[:, bass.ds(s * (GRP * TOPK) + TOPK * j, 1)], m.r_s[:, k, c],
                                               ALU.mult, ALU.add).then_inc(y_first, 1)
                        chain(first + 1 + j)
                        if j:
                            second(j - 1)
                    second(GRP - 1)
                else:
                    chain(*range(first + 1, first + 5))
                chain(first + 5)
                if f.live(6):
                    s, q, k = f.group(6), f.slot(6, 4), f.slot(6, 4)
                    v.wait_ge(f_ready, GRP * (s + 1))
                    v.wait_ge(xb_ready, s + 1)
                    v.tensor_tensor(by_graph(m.f_s[:, q, :]), by_graph(m.f_s[:, q, :]),
                                    m.gamma[:, :].unsqueeze(1).to_broadcast([P, GRP, D]), ALU.mult).then_inc(fg_mul, 1)
                    chain(first + 6)
                    v.wait_ge(fg_mul, s + 1)
                    if f.past(6, 4):
                        v.wait_ge(stored[k], 16 * (f.it - 1 - (f.k < 2)))
                    v.tensor_tensor(m.out_s[:, k, :], m.f_s[:, q, :], m.xb_s[:, k, :], ALU.add)\
                     .then_inc(out_ready, 1)
                else:
                    chain(first + 6)

            first_experts(0, 0, False)
            run_frames(v, step, 6, 4, ahead=1)


def kernel_program(nc, a, out):
    with ExitStack() as ctx:
        def sb(name, shape, dt=F32):
            return ctx.enter_context(nc.sbuf_tensor("sb_" + name, shape, dt))

        m = Memory()
        m.X = sb("X", [P, GRAPHS * D])
        m.MASK = sb("MASK", [P, GRAPHS * D], BF16)
        m.adj_in = sb("adj_in", [P, 4, W], I32)
        m.mask = sb("mask", [P, 4, W], BF16)
        m.z, m.zT, m.uT = (sb(name, [P, 2, W]) for name in ("z", "zT", "uT"))
        m.t_s = sb("t_s", [P, 2, W])
        m.l_s = sb("l_s", [P, 2, W])
        m.p_s = sb("p_s", [P, 2, W])
        m.pT = sb("pT", [P, 2, W])
        m.h_s, m.e_s = (sb(name, [P, 2, W]) for name in ("h_s", "e_s"))
        m.xv = sb("xv", [P, 4, GRP, 2 * D + 1])
        m.stats = sb("stats", [P, 8, 3])
        m.var, m.nhv, m.ra, m.rb, m.rt = (sb(name, [P, 8]) for name in ("var", "nhv", "ra", "rb", "rt"))
        m.seed = sb("seed", [P, 8], I32)
        m.rstd = sb("rstd", [P, 2, 8])
        m.shift = sb("shift", [P, 2, 8])
        m.rstd3 = sb("rstd3", [P, GRAPHS])
        m.shift3 = sb("shift3", [P, GRAPHS])
        m.nmin, m.nmax, m.sums, m.rden = (sb(name, [P, 2, GRP]) for name in ("nmin", "nmax", "sums", "rden"))
        m.consts = sb("consts", [P, 2 * D + EXPERTS])
        m.ident, m.centre, m.iota = m.consts[:, 0:D], m.consts[:, D:2 * D], m.consts[:, 2 * D:]
        m.ones = sb("ones", [P, D])
        m.one_row = sb("one_row", [1, 2 * D])
        m.m_w = sb("m_w", [P, D])
        m.wf, m.wc = sb("wf", [P, D]), sb("wc", [P, D])
        m.src_w, m.dst_w = sb("src_w", [P, D]), sb("dst_w", [P, D])
        m.gamma, m.beta = sb("gamma", [P, D]), sb("beta", [P, D])
        m.w12 = sb("w12", [P, 2 * D])
        m.wr = sb("wr", [P, EXPERTS])
        m.br_row = sb("br_row", [1, EXPERTS])
        m.bias_less = sb("bias_less", [1, D])
        m.b2_rows = sb("b2_rows", [EXPERTS, D])
        m.w1x = sb("w1x", [P, EXPERTS, FF])
        m.w2x = sb("w2x", [P, EXPERTS, FF // P, D])
        floats = m.MASK[:, :].bitcast(F32)
        m.raw = [floats[:, i * D:(i + 1) * D] for i in range(6)]
        m.w12_in = floats[:, D:3 * D]
        m.banks = ctx.enter_context(nc.psum_tensor("banks", [P, 8, W], F32))
        m.node_sums = sb("node_sums", [P, GRAPHS])
        m.x_copy = sb("x_copy", [P, 4, W])
        m.b1 = m.x_copy[:, :, :].rearrange("p q n -> p (q n)")
        m.for_rstd3 = Memory()
        m3 = m.for_rstd3
        m3.var, m3.nhv, m3.ra, m3.rb, m3.rt = (sb(name + "3", [P, 8]) for name in ("var", "nhv", "ra", "rb", "rt"))
        m3.stats, m3.seed = sb("stats3", [P, 8, 3]), sb("seed3", [P, 8], I32)
        m.held = {eng: ctx.enter_context(nc.semaphore(f"held{i}")) for i, eng in enumerate((nc.vector, nc.sync))}
        m.shift_beta = sb("shift_beta", [P, D])
        m.expert = sb("expert", [1, GRAPHS * TOPK], I32)
        m.weight = sb("weight", [P, GRAPHS * TOPK])
        m.d_expert = nc.dram_tensor("d_expert", (GRAPHS, TOPK), I32, kind="Internal").ap()
        m.d_weight = nc.dram_tensor("d_weight", (GRAPHS, TOPK), F32, kind="Internal").ap()
        m.d_b2 = nc.dram_tensor("d_b2", (GRAPHS, D), F32, kind="Internal").ap()
        m.z_lin = m.adj_in[:, :, :].bitcast(F32)
        m.zT_lin = [t[:, q, :] for t in (m.zT, m.pT) for q in range(2)]
        m.w1_top = floats[:, 0:2 * GRP * TOPK * FF].rearrange("p (q n f) -> p q n f", q=2, n=GRP * TOPK)
        m.g_s, m.b2_all = m.uT, m.e_s
        m.y_s = m.t_s[:, 0, :].rearrange("p (j d) -> p j d", j=GRP)
        m.o_s = floats[:, 2 * GRP * TOPK * FF:2 * GRP * TOPK * FF + 4 * W].rearrange("p (k w) -> p k w", k=4)
        xv = m.xv[:, :, :, :].rearrange("p a g n -> p (a g n)")
        m.r_s, m.f_s = (xv[:, i * 4 * W:(i + 1) * 4 * W].rearrange("p (k w) -> p k w", k=4) for i in range(2))
        m.xb_s = m.x_copy
        m.out_s = m.adj_in[:, :, :].bitcast(F32)
        m.four = Memory()
        m4 = m.four
        m4.var, m4.nhv, m4.ra, m4.rb, m4.rt = (sb(name + "4", [P, UN * GRP]) for name in ("var", "nhv", "ra", "rb", "rt"))
        m4.seed = sb("seed4", [P, UN * GRP], I32)
        m.all_stats = sb("all_stats", [P, GRAPHS, 3])
        m.small = ctx.enter_context(nc.semaphore("small"))
        m.f_stats_done, m.f_rstd_done = (ctx.enter_context(nc.semaphore("f_" + name))
                                         for name in ("stats_done", "rstd_done"))
        m.b_stats_done, m.b_rstd_done = (ctx.enter_context(nc.semaphore("b_" + name))
                                         for name in ("stats_done", "rstd_done"))
        m.experts_in = ctx.enter_context(nc.semaphore("experts_in"))
        m.x_in = [ctx.enter_context(nc.semaphore(f"x_in{i}")) for i in range(4)]
        make_weights(nc, m, a)
        layer0(nc, m, a)
        linear(nc, m)
        layer1(nc, m)
        route(nc, m)
        experts(nc, m, out)


def kernel(**inputs):
    import numpy as np
    import concourse.bacc as bacc
    from concourse.bass_utils import run_bass_kernel_spmd

    arrays = {name: np.ascontiguousarray(v) for name, v in inputs.items()}
    arrays["consts"] = np.concatenate([np.eye(D), np.eye(D) - 1 / D, np.tile(np.arange(EXPERTS), (P, 1))], 1)\
        .astype(np.float32)
    arrays["one_row"] = np.concatenate([np.full((1, D), 1 / D), np.ones((1, D))], 1).astype(np.float32)
    nc = bacc.Bacc("TRN2", target_bir_lowering=False, num_devices=1)
    a = {name: nc.dram_tensor(f"in_{name}", v.shape, mybir.dt.from_np(v.dtype), kind="ExternalInput").ap()
         for name, v in arrays.items()}
    out = nc.dram_tensor("out_x", (GRAPHS, P, D), F32, kind="ExternalOutput").ap()
    kernel_program(nc, a, out)
    r = run_bass_kernel_spmd(nc, [{f"in_{name}": v for name, v in arrays.items()}], core_ids=[0])
    return r.results[0]["out_x"]
```

```python
from contextlib import ExitStack

import concourse.bass as bass
from concourse import mybir

F32 = mybir.dt.float32
BF16 = mybir.dt.bfloat16
I32 = mybir.dt.int32
ALU = mybir.AluOpType
ACT = mybir.ActivationFunctionType
AX = mybir.AxisListType

GRAPHS, P, D = 128, 128, 128
GRP = 4
W = GRP * D
NG = GRAPHS // GRP
UN = 4
EXPERTS, FF, TOPK = 8, 256, 2
EPS = 1e-5
MASKED = 4.5e16
SLOPE = 0.2
CAPACITY = float(-(-(GRAPHS * P * 5 // 4) // EXPERTS))
RSQRT_SEED = float(0x5F375A86)


class Memory:
    pass


class Frames:

    def __init__(self, it, k, count, body):
        self.it, self.k, self.count, self.body = it, k, count, body

    def live(self, lag):
        return self.body or 0 <= self.it * UN + self.k - lag < self.count

    def group(self, lag=0):
        return self.it * UN + (self.k - lag)

    def pair(self, lag=0):
        return self.it * (UN // 2) + (self.k - lag) // 2

    def past(self, lag, n):
        return self.body or self.it * UN + self.k - lag >= n

    def slot(self, lag, n):
        return (self.k - lag) % n


def run_frames(eng, step, last_lag, history, ahead=0):
    first = -(-(last_lag + history) // UN)
    last = NG // UN - ahead
    assert first < last
    for t in range(first * UN):
        step(Frames(t // UN, t % UN, NG, False))
    with eng.Fori(first, last) as it:
        for k in range(UN):
            step(Frames(it, k, NG, True))
    for t in range(last * UN, NG + last_lag):
        step(Frames(t // UN, t % UN, NG, False))


def grp(t, s):
    return t[:, bass.ds(s * W, W)]


def by_graph(ap):
    return ap.rearrange("p (g d) -> p g d", g=GRP)


def each(v):
    return v.to_broadcast([P, GRP, D])


def hold(eng, m):
    eng.sem_inc(m.held[eng], 1)


class Rstd:

    STEPS = 14

    def __init__(self, nc, m, done):
        self.nc, self.m, self.done = nc, m, done

    def step(self, n, before, rstd, shift, stats=None, cols=slice(None)):
        v, m, done = self.nc.vector, self.m, self.done
        stats = m.stats if stats is None else stats
        mean, squares = stats[:, cols, 1], stats[:, cols, 2]
        var, nhv, seed, rt = m.var[:, cols], m.nhv[:, cols], m.seed[:, cols], m.rt[:, cols]
        if n:
            v.wait_ge(done, before * self.STEPS + n)
        if n == 0:
            i = v.tensor_scalar(var, squares, 1.0 / D, EPS, ALU.mult, ALU.add)
        elif n == 1:
            i = v.tensor_scalar(nhv, squares, -0.5 / D, -0.5 * EPS, ALU.mult, ALU.add)
        elif n == 2:
            i = v.tensor_scalar(seed, var.bitcast(I32), -0.5, RSQRT_SEED, ALU.mult, ALU.add)
        elif n < 12:
            y = [seed.bitcast(F32), m.ra[:, cols], m.rb[:, cols], rstd]
            a, b = y[n // 3 - 1], y[n // 3]
            if n % 3 == 0:
                i = v.tensor_tensor(rt, a, a, ALU.mult)
            elif n % 3 == 1:
                i = v.tensor_tensor(rt, rt, nhv, ALU.mult)
            else:
                i = v.scalar_tensor_tensor(b, rt, 1.5, a, ALU.add, ALU.mult)
        elif n == 12:
            i = v.tensor_tensor(rt, mean, rstd, ALU.mult)
        else:
            i = v.tensor_scalar(shift, rt, -1.0, 1.0, ALU.mult, ALU.add)
        i.then_inc(done, 1)


def load_group(sp, m, a, s, k):
    sp.dma_start(by_graph(grp(m.X, s)),
                 a["x"][bass.ds(s * GRP, GRP), :, :].rearrange("g n d -> n g d")).then_inc(m.x_in[k], 16)


def make_weights(nc, m, a):
    with ExitStack() as ctx:
        s_in = ctx.enter_context(nc.semaphore("w_in"))
        s_pe = ctx.enter_context(nc.semaphore("w_product"))
        s_dve = ctx.enter_context(nc.semaphore("w_copied"))
        block = ctx.enter_context(nc.Block())
        bk = m.banks
        raw = m.raw
        wcT, a12T, b_s, a2b, a1b, asb, adb, wfT = (m.h_s[:, 0, 0:D], m.h_s[:, 0, D:2 * D], m.h_s[:, 0, 2 * D:3 * D],
                                                   m.h_s[:, 0, 3 * D:], m.h_s[:, 1, 0:D], m.h_s[:, 1, D:2 * D],
                                                   m.h_s[:, 1, 2 * D:3 * D], m.h_s[:, 1, 3 * D:])
        zero = m.e_s[:, 0, 0:D]
        wc1T = m.e_s[:, 0, D:2 * D]
        wr_in = m.e_s[:, 0, 2 * D:2 * D + EXPERTS]
        bias_row = m.e_s[0:1, 0, 3 * D:4 * D]
        vecs = m.e_s[:, 1, 0:8]

        LOADS = [(m.consts[:, :], a["consts"]), (m.one_row[:, :], a["one_row"]),
                 (raw[0], a["L0_gnn_W"]), (raw[1], a["L0_gnn_W_1"]), (raw[2], a["L0_gnn_W_2"]),
                 (raw[3], a["L0_gnn_a_12"]), (raw[4], a["L0_ffn_weight"]), (raw[5], a["L1_gnn_W"]),
                 (vecs[:, 0:1], a["L0_gnn_a_1"]), (vecs[:, 1:2], a["L0_gnn_a_2"]),
                 (vecs[:, 2:3], a["L1_gnn_a"][0:D, :]), (vecs[:, 3:4], a["L1_gnn_a"][D:2 * D, :]),
                 (bias_row, a["L0_ffn_bias"].rearrange("(a d) -> a d", a=1)),
                 (wr_in, a["L1_ffn_Wr"]), (m.br_row[:, :], a["L1_ffn_br"].rearrange("(a e) -> a e", a=1)),
                 (m.b2_rows[:, :], a["L1_ffn_b2"]),
                 (m.gamma[:, :], a["L1_ffn_gamma"].partition_broadcast(P)),
                 (m.beta[:, :], a["L1_ffn_beta"].partition_broadcast(P))]
        N_IN = 16 * len(LOADS)

        @block.sync
        def _(sp):
            for to, of in LOADS[0::2]:
                sp.dma_start(to, of).then_inc(s_in, 16)
            for s in range(4):
                load_group(sp, m, a, s, s)
            sp.dma_start(m.w1x[:, :, :], a["L1_ffn_W1"].rearrange("e d f -> d e f")).then_inc(m.experts_in, 16)
            sp.dma_start(m.b1, a["L1_ffn_b1"].rearrange("e f -> (e f)").partition_broadcast(P))\
              .then_inc(m.experts_in, 16)

        @block.scalar
        def _(act):
            for to, of in LOADS[1::2]:
                act.dma_start(to, of).then_inc(s_in, 16)

        def bank(i, n):
            return bk[:, i, 0:n]

        @block.tensor
        def _(pe):
            pe.wait_ge(s_in, N_IN)
            pe.matmul(bank(0, D), raw[0], m.centre, start=True, stop=True)
            pe.transpose(bank(1, D), raw[3], m.ident)
            pe.transpose(bank(2, D), raw[4], m.ident)
            pe.matmul(bank(3, D), raw[5], m.centre, start=True, stop=True)
            pe.matmul(bk[:, 4, 0:2 * D], m.centre, m.w12_in, start=True, stop=True)
            pe.matmul(bank(5, D), m.centre, raw[5], start=True, stop=True)
            pe.matmul(bank(6, EXPERTS), m.centre, wr_in, start=True, stop=True).then_inc(s_pe, 1)
            pe.wait_ge(s_dve, 1)
            pe.matmul(bank(0, D), a12T, wcT, start=True, stop=True)
            pe.matmul(bank(1, D), m.centre, wfT, start=True, stop=False)
            pe.matmul(bank(1, D), m.one_row[:, 0:D], m.bias_less[:, :], start=False, stop=True)
            pe.matmul(bank(2, D), wc1T, asb, start=True, stop=True)
            pe.matmul(bank(3, D), wc1T, adb, start=True, stop=True).then_inc(s_pe, 1)
            pe.wait_ge(s_dve, 2)
            pe.matmul(bank(4, D), wcT, b_s, start=True, stop=False)
            pe.matmul(bank(4, D), a1b, wcT, start=False, stop=True).then_inc(s_pe, 1)

        @block.vector
        def _(v):
            chain = m.small
            n = [0]

            def mark(i):
                n[0] += 1
                i.then_inc(chain, 1)

            def settle():
                v.wait_ge(chain, n[0])

            v.wait_ge(s_in, N_IN)
            mark(v.memset(zero, 0.0))
            settle()
            for to, j, scale in ((a1b, 0, 1.0 / D), (a2b, 1, 1.0 / D), (asb, 2, -1.0), (adb, 3, -1.0)):
                mark(v.tensor_scalar(to, zero, vecs[:, j:j + 1], scale, ALU.add, ALU.mult))
            mark(v.tensor_scalar(m.bias_less[:, :], bias_row, 1.0, None, ALU.subtract))
            mark(v.memset(m.xv[:, :, :, 2 * D:], 1.0))
            mark(v.memset(m.ones[:, :], 1.0))
            v.wait_ge(s_pe, 1)
            mark(v.tensor_copy(wcT, bank(0, D)))
            mark(v.tensor_copy(a12T, bank(1, D)))
            mark(v.tensor_copy(wfT, bank(2, D)))
            mark(v.tensor_copy(wc1T, bank(3, D)))
            settle()
            v.sem_inc(s_dve, 1)
            mark(v.tensor_copy(m.w12[:, :], bk[:, 4, 0:2 * D]))
            mark(v.tensor_copy(m.wc[:, :], bank(5, D)))
            mark(v.tensor_scalar(m.wr[:, :], bank(6, EXPERTS), 1.0 / P, None, ALU.mult))
            v.wait_ge(s_pe, 2)
            mark(v.tensor_tensor(b_s, bank(0, D), a2b, ALU.add))
            settle()
            v.sem_inc(s_dve, 1)
            mark(v.tensor_copy(m.wf[:, :], bank(1, D)))
            mark(v.tensor_copy(m.src_w[:, :], bank(2, D)))
            mark(v.tensor_copy(m.dst_w[:, :], bank(3, D)))
            v.wait_ge(s_pe, 3)
            mark(v.tensor_scalar(m.m_w[:, :], bank(4, D), -1.0, None, ALU.mult))
            settle()


def two_statistics(v, stats, x, first, u, j, done):
    v.bn_stats(stats[:, GRP * u + j:GRP * u + j + 2, :].rearrange("p a b -> p (a b)"),
               x[:, bass.ds(first + j * D, 2 * D)].rearrange("p (g d) -> p d g", g=2)).then_inc(done, 1)


def statistics(v, stats, x, first, u, done):
    for j in range(0, GRP, 2):
        two_statistics(v, stats, x, first, u, j, done)


def transpose_graphs(pe, to, of, ident, done):
    for j in range(GRP):
        i = pe.transpose(to[:, j * D:(j + 1) * D], of[:, j * D:(j + 1) * D], ident)
    i.then_inc(done, 1)


def make_z(pool, m, s, z, rstd, shift, z_mul, z_ready, before=None):
    zq = by_graph(z)
    pool.tensor_tensor(zq, by_graph(grp(m.X, s)), each(rstd), ALU.mult).then_inc(z_mul, 1)
    pool.wait_ge(z_mul, (s if before is None else before) + 1)
    pool.tensor_tensor(zq, zq, each(shift), ALU.add).then_inc(z_ready, 1)


def softmax_rows(act, m, q, done, sums=None):
    for j in range(GRP):
        i = act.activation(m.p_s[:, q, j * D:(j + 1) * D], m.l_s[:, q, j * D:(j + 1) * D], ACT.Exp,
                           bias=m.nmax[:, q, j:j + 1], scale=-1.0,
                           accum_out=None if sums is None else sums[:, q, j:j + 1])
    i.then_inc(done, 1)


CHAIN = (0, 1, 2, 3), (4, 5, 6, 7), (8, 9, 10), (11, 12, 13)


def of_group(t, s):
    return t[:, bass.ds(s * GRP, GRP)]


def statistics_of(v, m, s, j, done):
    v.bn_stats(m.all_stats[:, bass.ds(s * GRP + j, 2), :].rearrange("p a b -> p (a b)"),
               m.X[:, bass.ds(s * W + j * D, 2 * D)].rearrange("p (g d) -> p d g", g=2)).then_inc(done, 1)


def rstd_of_body(v, m, rstd, done, f, ns):
    b = f.it - 1
    for n in ns:
        if n == 0 and f.past(4, UN):
            v.wait_ge(done, b * Rstd.STEPS)
        here = bass.ds(b * (UN * GRP), UN * GRP)
        rstd.step(n, b, m.rstd01[:, here], m.shift01[:, here], m.all_stats[:, here, :])


EARLY = 2 * UN


def early_statistics(v, m, rstd, t):
    f = Frames(t // UN, t % UN, NG, False)
    if t == UN:
        v.wait_ge(m.f_stats_done, 2 * UN)
    if f.live(UN):
        rstd_of_body(v, m, rstd, m.f_rstd_done, f, CHAIN[f.k])
    for j in range(0, GRP, 2):
        statistics_of(v, m, t, j, m.f_stats_done)


def layer0(nc, m, a):
    with ExitStack() as ctx:
        def sem(name):
            return ctx.enter_context(nc.semaphore("a_" + name))

        adj_in = [sem(f"adj_in{i}") for i in range(4)]
        mask_kept = [sem(f"mask_kept{i}") for i in range(4)]
        masked, stats_done, rstd_done = sem("masked"), sem("stats_done"), sem("rstd_done")
        z_mul, z_ready = sem("z_mul"), sem("z_ready")
        t_done, zT_copied = sem("t_done"), sem("zT_copied")
        u_done, uT_copied = sem("u_done"), sem("uT_copied")
        xv_done, xv_copied = sem("xv_done"), sem("xv_copied")
        s_done, s_read = sem("s_done"), sem("s_read")
        max_ready, l_ready = sem("max_ready"), sem("l_ready")
        p_ready = sem("p_ready")
        pt_done, pT_copied = sem("pt_done"), sem("pT_copied")
        o_done, rden_done, h_done = sem("o_done"), sem("rden_done"), sem("h_done")
        r_done, e_done, ex_done, x_done = sem("r_done"), sem("e_done"), sem("ex_done"), sem("x_done")
        w1_done, w1_copied = sem("w1_done"), sem("w1_copied")
        rstd = Rstd(nc, m.four, rstd_done)
        linear_rstd = Rstd(nc, m.four, m.f_rstd_done)
        bk = m.banks
        T_B, PT_B, U_B, S_B, XV_B, O_B = 0, 1, 2, 3, 4, 6
        block = ctx.enter_context(nc.Block())

        @block.sync
        def _(sp):
            def step(f):
                if f.live(0) and f.past(0, 4):
                    s, k = f.group(), f.slot(0, 4)
                    sp.wait_ge(stats_done, 2 * (s - 3))
                    load_group(sp, m, a, s, k)
                if f.live(8):
                    s, k = f.group(8), f.slot(8, 4)
                    if f.past(8, 4):
                        sp.wait_ge(masked, s - 3)
                    sp.dma_start(by_graph(m.adj_in[:, k, :]),
                                 a["adj"][bass.ds(s * GRP, GRP), :, :].rearrange("g n d -> n g d"))\
                      .then_inc(adj_in[k], 16)
                if f.live(12):
                    s, k = f.group(12), f.slot(12, 4)
                    sp.wait_ge(masked, s + 1)
                    sp.dma_start(grp(m.MASK, s), m.mask[:, k, :]).then_inc(mask_kept[k], 16)

            run_frames(sp, step, 12, 4)
            sp.dma_start(m.w2x[:, :, :, :], a["L1_ffn_W2"].rearrange("e (c p) d -> p e c d", p=P))\
              .then_inc(m.experts_in, 16)
            sp.wait_ge(m.experts_in, 48)
            for k in range(4):
                sp.wait_ge(mask_kept[k], 16 * (NG // 4))

        @block.gpsimd
        def _(pool):
            def step(f):
                if f.live(0):
                    s, q = f.group(), f.slot(0, 2)
                    pool.wait_ge(rstd_done, (f.it + 1) * Rstd.STEPS)
                    if f.past(0, 2):
                        pool.wait_ge(t_done, s - 1)
                    make_z(pool, m, s, m.z[:, q, :], of_group(m.rstd01, s), of_group(m.shift01, s), z_mul, z_ready)
                if f.live(6):
                    s, q = f.group(6), f.slot(6, 2)
                    pool.wait_ge(e_done, s + 1)
                    pool.tensor_tensor(grp(m.X, s), grp(m.X, s), m.e_s[:, q, :], ALU.add).then_inc(ex_done, 1)

            run_frames(pool, step, 6, 2)

        @block.tensor
        def _(pe):
            def step(f):
                if f.live(0):
                    s, q = f.group(), f.slot(0, 2)
                    pe.wait_ge(z_ready, s + 1)
                    if f.past(0, 1):
                        pe.wait_ge(zT_copied, s)
                    transpose_graphs(pe, bk[:, T_B, :], m.z[:, q, :], m.ident, t_done)
                if f.live(3):
                    s, q = f.group(3), f.slot(3, 2)
                    pe.wait_ge(p_ready, s + 1)
                    if f.past(3, 1):
                        pe.wait_ge(pT_copied, s)
                    transpose_graphs(pe, bk[:, PT_B, :], m.p_s[:, q, :], m.ident, pt_done)
                if f.live(1):
                    s, q = f.group(1), f.slot(1, 2)
                    pe.wait_ge(zT_copied, s + 1)
                    if f.past(1, 1):
                        pe.wait_ge(uT_copied, s)
                    pe.matmul(bk[:, U_B, :], m.m_w[:, :], m.zT[:, q, :], start=True, stop=True).then_inc(u_done, 1)
                    if f.past(1, 1):
                        pe.wait_ge(xv_copied, s)
                    for j in range(GRP):
                        i = pe.matmul(bk[:, XV_B + j // 2, (j % 2) * 2 * D:(j % 2 + 1) * 2 * D],
                                      m.zT[:, q, j * D:(j + 1) * D], m.w12[:, :], start=True, stop=True)
                    i.then_inc(xv_done, 1)
                if f.live(1):
                    s, q = f.group(1), f.slot(1, 2)
                    pe.wait_ge(uT_copied, s + 1)
                    if f.past(1, 1):
                        pe.wait_ge(s_read, GRP * s)
                    for j in range(GRP):
                        c = slice(j * D, (j + 1) * D)
                        i = pe.matmul(bk[:, S_B, c], m.uT[:, q, c], m.zT[:, q, c], start=True, stop=True)
                    i.then_inc(s_done, 1)
                if f.live(3):
                    s, q, k = f.group(3), f.slot(3, 2), f.slot(3, 4)
                    pe.wait_ge(pT_copied, s + 1)
                    if f.past(3, 1):
                        pe.wait_ge(h_done, s)
                    for j in range(GRP):
                        i = pe.matmul(bk[:, O_B + j // 2, (j % 2) * (D + 1):(j % 2 + 1) * (D + 1)],
                                      m.pT[:, q, j * D:(j + 1) * D], m.xv[:, k, j, D:], start=True, stop=True)
                    i.then_inc(o_done, 1)

            pe.wait_ge(m.experts_in, 32)
            for e in range(EXPERTS):
                pe.matmul(bk[:, e, 0:FF], m.centre, m.w1x[:, e, :], start=True, stop=True).then_inc(w1_done, 1)
            pe.wait_ge(w1_copied, EXPERTS)
            run_frames(pe, step, 3, 1)

        @block.scalar
        def _(act):
            def step(f):
                if f.live(0):
                    s, q = f.group(), f.slot(0, 2)
                    act.wait_ge(t_done, s + 1)
                    if f.past(0, 2):
                        act.wait_ge(s_done, s - 1)
                    act.copy(m.zT[:, q, :], bk[:, T_B, :]).then_inc(zT_copied, 1)
                if f.live(3):
                    s, q = f.group(3), f.slot(3, 2)
                    act.wait_ge(pt_done, s + 1)
                    if f.past(3, 2):
                        act.wait_ge(o_done, s - 1)
                    act.copy(m.pT[:, q, :], bk[:, PT_B, :]).then_inc(pT_copied, 1)
                if f.live(1):
                    s, q = f.group(1), f.slot(1, 2)
                    act.wait_ge(u_done, s + 1)
                    if f.past(1, 2):
                        act.wait_ge(s_done, s - 1)
                    act.copy(m.uT[:, q, :], bk[:, U_B, :]).then_inc(uT_copied, 1)
                if f.live(2):
                    s, q = f.group(2), f.slot(2, 2)
                    act.wait_ge(l_ready, s + 1)
                    if f.past(2, 2):
                        act.wait_ge(pt_done, s - 1)
                    softmax_rows(act, m, q, p_ready)
                if f.live(4):
                    s, q = f.group(4), f.slot(4, 2)
                    act.wait_ge(h_done, s + 1)
                    if f.past(4, 2):
                        act.wait_ge(ex_done, s - 1)
                    act.activation(m.e_s[:, q, :], m.h_s[:, q, :], ACT.Relu, scale=-1.0).then_inc(r_done, 1)
                if f.live(1):
                    s, k = f.group(1), f.slot(1, 4)
                    act.wait_ge(xv_done, s + 1)
                    if f.past(1, 4):
                        act.wait_ge(h_done, s - 3)
                    act.copy(m.xv[:, k, :, 0:2 * D].rearrange("p (b j) n -> p b j n", b=2),
                             bk[:, XV_B:XV_B + 2, :].rearrange("p b (j n) -> p b j n", j=2)).then_inc(xv_copied, 1)
                if f.live(4):
                    s, q = f.group(4), f.slot(4, 2)
                    act.wait_ge(r_done, s + 1)
                    act.activation(m.e_s[:, q, :], m.e_s[:, q, :], ACT.Exp, scale=-1.0).then_inc(e_done, 1)

            run_frames(act, step, 4, 4)

        @block.vector
        def _(v):
            def step(f):
                def chain(*ns):
                    if f.live(4):
                        rstd_of_body(v, m, rstd, rstd_done, f, ns)

                def measure(j):
                    if f.live(0):
                        if j == 0:
                            v.wait_ge(m.x_in[f.k], 16 * (f.it + 1))
                            hold(v, m)
                        statistics_of(v, m, f.group(), j, stats_done)

                ns = CHAIN[f.k]
                if f.k == 0 and f.live(4):
                    v.wait_ge(stats_done, 2 * UN * f.it)
                if not f.body and f.it == 1:
                    ns = ()
                    if f.k == 0:
                        for n in range(Rstd.STEPS):
                            chain(n)
                            if n < EXPERTS:
                                v.wait_ge(w1_done, n + 1)
                                v.scalar_tensor_tensor(m.w1x[:, n, :], m.b1[:, n * FF:(n + 1) * FF], 1.0 / P,
                                                       bk[:, n, 0:FF], ALU.mult, ALU.add).then_inc(w1_copied, 1)
                if f.live(11):
                    s, q, k = f.group(11), f.slot(11, 2), f.slot(11, 4)
                    v.wait_ge(s_done, s + 1)
                    v.wait_ge(masked, s + 1)
                    if f.past(11, 2):
                        v.wait_ge(l_ready, s - 1)
                    hold(v, m)
                    for j in range(GRP):
                        c = slice(j * D, (j + 1) * D)
                        v.tensor_tensor_reduce(m.t_s[:, q, c], bk[:, S_B, c], m.mask[:, k, c], 1.0, 3.0e38,
                                               ALU.add, ALU.min, m.nmin[:, q, j:j + 1]).then_inc(s_read, 1)
                        chain(*ns[j:j + 1])
                    v.wait_ge(s_read, GRP * (s + 1))
                    if f.past(11, 2):
                        v.wait_ge(p_ready, s - 1)
                    v.scalar_tensor_tensor(m.nmax[:, q, :], m.nmin[:, q, :], SLOPE, m.nmin[:, q, :], ALU.mult, ALU.min)\
                     .then_inc(max_ready, 1)
                    v.scalar_tensor_tensor(m.l_s[:, q, :], m.t_s[:, q, :], SLOPE, m.t_s[:, q, :], ALU.mult, ALU.min)\
                     .then_inc(l_ready, 1)
                else:
                    chain(*ns)
                if f.live(8):
                    s, k = f.group(8), f.slot(8, 4)
                    v.wait_ge(adj_in[k], 16 * (f.it - 1))
                    if f.past(8, 4):
                        v.wait_ge(mask_kept[k], 16 * (f.it - 2))
                        v.wait_ge(s_read, GRP * (s - 3))
                    v.tensor_scalar(m.mask[:, k, :], m.adj_in[:, k, :], 0, MASKED, ALU.is_le, ALU.mult)\
                     .then_inc(masked, 1)
                measure(0)
                if f.live(15):
                    s, q = f.group(15), f.slot(15, 2)
                    v.wait_ge(ex_done, s + 1)
                    v.scalar_tensor_tensor(grp(m.X, s), m.h_s[:, q, :], 0.0, grp(m.X, s), ALU.max, ALU.add)\
                     .then_inc(x_done, 1)
                if f.live(13):
                    s, q, k = f.group(13), f.slot(13, 2), f.slot(13, 4)
                    v.wait_ge(o_done, s + 1)
                    if f.past(13, 1):
                        v.wait_ge(h_done, s)
                    v.reciprocal(m.rden[:, q, :].rearrange("p (b j) -> p b j", b=2),
                                 bk[:, O_B:O_B + 2, D:2 * (D + 1):D + 1]).then_inc(rden_done, 1)
                    measure(2)
                    v.wait_ge(rden_done, s + 1)
                    if f.past(13, 2):
                        v.wait_ge(x_done, s - 1)
                    for j in range(GRP):
                        o = (j % 2) * (D + 1)
                        i = v.scalar_tensor_tensor(m.h_s[:, q, j * D:(j + 1) * D], bk[:, O_B + j // 2, o:o + D],
                                                   m.rden[:, q, j:j + 1], m.xv[:, k, j, 0:D], ALU.mult, ALU.add)
                    i.then_inc(h_done, 1)
                else:
                    measure(2)
                t = 0 if f.body else f.it * UN + f.k - NG
                if not f.body and 0 <= t < EARLY:
                    if t == 0:
                        v.wait_ge(z_ready, EARLY)
                    if t == UN:
                        v.wait_ge(rstd_done, NG // UN * Rstd.STEPS)
                    v.wait_ge(x_done, EARLY)
                    early_statistics(v, m, linear_rstd, t)

            run_frames(v, step, 15, 2)


def linear(nc, m):
    with ExitStack() as ctx:
        def sem(name):
            return ctx.enter_context(nc.semaphore("f_" + name))

        stats_done, rstd_done = m.f_stats_done, m.f_rstd_done
        z_act_ready, z_mul, z_pool_ready = sem("z_act_ready"), sem("z_mul"), sem("z_pool_ready")
        t_done, zT_copied = sem("t_done"), sem("zT_copied")
        y_done, x_done = sem("y_done"), sem("x_done")
        rstd = Rstd(nc, m.four, rstd_done)
        layer1_rstd = Rstd(nc, m.both, m.b_rstd_done)
        bk = m.banks
        z, zT = m.z_lin, m.zT_lin
        T_B, Y_B = 0, 2
        LAG = 12
        block = ctx.enter_context(nc.Block())

        @block.gpsimd
        def _(pool):
            def step(f):
                if f.k % 2:
                    s = f.group()
                    pool.wait_ge(rstd_done, (f.it + 1) * Rstd.STEPS)
                    if f.past(0, 4):
                        pool.wait_ge(t_done, s - 3)
                    make_z(pool, m, s, z[:, f.k, :], of_group(m.rstd01, s), of_group(m.shift01, s), z_mul,
                           z_pool_ready, f.pair(1))

            run_frames(pool, step, 0, 4)

        @block.tensor
        def _(pe):
            def step(f):
                if f.live(0):
                    s, q, k = f.group(), f.slot(0, 2), f.slot(0, 4)
                    if f.k % 2:
                        pe.wait_ge(z_pool_ready, f.pair(1) + 1)
                    else:
                        pe.wait_ge(z_act_ready, f.pair() + 1)
                    if f.past(0, 2):
                        pe.wait_ge(zT_copied, s - 1)
                    transpose_graphs(pe, bk[:, T_B + q, :], z[:, k, :], m.ident, t_done)
                if f.live(1):
                    s, k = f.group(1), f.slot(1, 4)
                    pe.wait_ge(zT_copied, s + 1)
                    if f.past(1, 4):
                        pe.wait_ge(x_done, s - 3)
                    for j in range(GRP):
                        c = slice(j * D, (j + 1) * D)
                        i = pe.matmul(bk[:, Y_B + k, c], zT[k][:, c], m.wf[:, :], start=True, stop=True)
                    i.then_inc(y_done, 1)

            run_frames(pe, step, 1, 4)

        @block.scalar
        def _(act):
            def step(f):
                if f.k % 2 == 0 and f.live(0):
                    s, k = f.group(), f.slot(0, 4)
                    act.wait_ge(rstd_done, (f.it + 1) * Rstd.STEPS)
                    if f.past(0, 4):
                        act.wait_ge(t_done, s - 3)
                    for j in range(GRP):
                        n = s * GRP + j
                        i = act.activation(z[:, k, j * D:(j + 1) * D], m.X[:, bass.ds(s * W + j * D, D)], ACT.Identity,
                                           bias=m.shift01[:, bass.ds(n, 1)], scale=m.rstd01[:, bass.ds(n, 1)])
                    i.then_inc(z_act_ready, 1)
                if f.live(1):
                    s, q, k = f.group(1), f.slot(1, 2), f.slot(1, 4)
                    act.wait_ge(t_done, s + 1)
                    if f.past(1, 4):
                        act.wait_ge(y_done, s - 3)
                    act.copy(zT[k], bk[:, T_B + q, :]).then_inc(zT_copied, 1)

            run_frames(act, step, 1, 4)

        @block.vector
        def _(v):
            def step(f):
                def chain(*ns):
                    if f.live(4) and f.past(0, EARLY):
                        rstd_of_body(v, m, rstd, rstd_done, f, ns)

                def add(half):
                    if f.live(LAG):
                        s, k = f.group(LAG), f.slot(LAG, 4)
                        if half == 0:
                            v.wait_ge(y_done, s + 1)
                        x = m.X[:, bass.ds(s * W + half * 2 * D, 2 * D)]
                        i = v.tensor_tensor(x, x, bk[:, Y_B + k, half * 2 * D:(half + 1) * 2 * D], ALU.add)
                        if half:
                            i.then_inc(x_done, 1)

                ns = CHAIN[f.k]
                if f.k == 0 and f.live(4) and f.past(0, EARLY):
                    v.wait_ge(stats_done, 2 * UN * f.it)
                chain(ns[0])
                if f.live(0) and f.past(0, EARLY):
                    statistics_of(v, m, f.group(), 0, stats_done)
                chain(ns[1])
                add(0)
                chain(ns[2])
                if f.live(0) and f.past(0, EARLY):
                    statistics_of(v, m, f.group(), 2, stats_done)
                chain(*ns[3:])
                add(1)

                t = 0 if f.body else f.it * UN + f.k - NG
                if t == 1:
                    v.wait_ge(x_done, 2)
                    for u in range(2):
                        statistics(v, m.both.stats, m.X, u * W, u, m.b_stats_done)
                    v.wait_ge(m.b_stats_done, 4)
                if 1 <= t <= Rstd.STEPS // 2:
                    for n in (2 * t - 2, 2 * t - 1):
                        layer1_rstd.step(n, 0, m.both.rstd[:, 0:2 * GRP], m.both.shift[:, 0:2 * GRP],
                                         cols=slice(0, 2 * GRP))

            run_frames(v, step, LAG, 4)


BEHIND = 5


def before_and_after(t, pair, half, first, n):
    return t[:, bass.ds((pair + half * BEHIND) * (4 * GRP) + half * 2 * GRP + first, n)]


def layer1(nc, m):
    with ExitStack() as ctx:
        def sem(name):
            return ctx.enter_context(nc.semaphore("b_" + name))

        mask_in = [sem(f"mask_in{i}") for i in range(4)]
        x_copied = [sem(f"x_copied{i}") for i in range(4)]
        stats_done, rstd_done = m.b_stats_done, m.b_rstd_done
        stats3_done = sem("stats3_done")
        z_mul, z_ready = sem("z_mul"), sem("z_ready")
        t_done, zT_copied = sem("t_done"), sem("zT_copied")
        wh_done, wh_copied = sem("wh_done"), sem("wh_copied")
        s_done, s_read = sem("s_done"), sem("s_read")
        max_ready, l_ready = sem("max_ready"), sem("l_ready")
        p_ready = sem("p_ready")
        pt_done, pT_copied = sem("pt_done"), sem("pT_copied")
        o_done, rden_done, h_done = sem("o_done"), sem("rden_done"), sem("h_done")
        x_done, mean_done = sem("x_done"), sem("mean_done")
        mean_copied = sem("mean_copied")
        both = m.both
        rstd = Rstd(nc, both, rstd_done)
        bk = m.banks
        T_B, PT_B, WH_B, S_B, MEAN_B, O_B = 0, 1, 2, 3, 5, 6
        block = ctx.enter_context(nc.Block())

        @block.sync
        def _(sp):
            def step(f):
                if f.live(0):
                    s, k = f.group(), f.slot(0, 4)
                    if f.past(0, 4):
                        sp.wait_ge(s_read, GRP * (s - 3))
                    sp.dma_start(m.mask[:, k, :], grp(m.MASK, s)).then_inc(mask_in[k], 16)
                if f.live(8):
                    s, k = f.group(8), f.slot(8, 4)
                    sp.wait_ge(x_done, s + 1)
                    hold(sp, m)
                    if f.past(8, 4):
                        sp.wait_ge(mean_done, s - 3)
                    sp.dma_start(m.x_copy[:, k, :], grp(m.X, s)).then_inc(x_copied[k], 16)

            run_frames(sp, step, 8, 4)

        @block.gpsimd
        def _(pool):
            def step(f):
                s, q = f.group(), f.slot(0, 2)
                p, first = f.pair(f.k % 2), GRP * (f.k % 2)
                pool.wait_ge(rstd_done, (p + 1) * Rstd.STEPS)
                if f.past(0, 2):
                    pool.wait_ge(t_done, s - 1)
                make_z(pool, m, s, m.z[:, q, :], before_and_after(both.rstd, p, 0, first, GRP),
                       before_and_after(both.shift, p, 0, first, GRP), z_mul, z_ready)

            run_frames(pool, step, 0, 2)

        @block.tensor
        def _(pe):
            def step(f):
                if f.live(0):
                    s, q = f.group(), f.slot(0, 2)
                    pe.wait_ge(z_ready, s + 1)
                    if f.past(0, 1):
                        pe.wait_ge(zT_copied, s)
                    transpose_graphs(pe, bk[:, T_B, :], m.z[:, q, :], m.ident, t_done)
                if f.live(3):
                    s, q = f.group(3), f.slot(3, 2)
                    pe.wait_ge(p_ready, s + 1)
                    if f.past(3, 1):
                        pe.wait_ge(pT_copied, s)
                    transpose_graphs(pe, bk[:, PT_B, :], m.p_s[:, q, :], m.ident, pt_done)
                if f.live(1):
                    s, q = f.group(1), f.slot(1, 2)
                    pe.wait_ge(zT_copied, s + 1)
                    if f.past(1, 2):
                        pe.wait_ge(s_read, GRP * (s - 1))
                    pe.matmul(bk[:, S_B + q, :], m.dst_w[:, :], m.zT[:, q, :], start=True, stop=False)
                    for j in range(GRP):
                        c = slice(j * D, (j + 1) * D)
                        i = pe.matmul(bk[:, S_B + q, c], m.zT[:, q, c], m.src_w[:, :], start=False, stop=j == GRP - 1)
                    i.then_inc(s_done, 1)
                    if f.past(1, 1):
                        pe.wait_ge(wh_copied, s)
                    for j in range(GRP):
                        c = slice(j * D, (j + 1) * D)
                        i = pe.matmul(bk[:, WH_B, c], m.zT[:, q, c], m.wc[:, :], start=True, stop=True)
                    i.then_inc(wh_done, 1)
                if f.live(3):
                    s, q, k = f.group(3), f.slot(3, 2), f.slot(3, 4)
                    pe.wait_ge(pT_copied, s + 1)
                    if f.past(3, 2):
                        pe.wait_ge(h_done, s - 1)
                    for j in range(GRP):
                        c = slice(j * D, (j + 1) * D)
                        i = pe.matmul(bk[:, O_B + q, c], m.pT[:, q, c], m.xv[:, k, j, D:2 * D],
                                      start=True, stop=True)
                    i.then_inc(o_done, 1)
                if f.live(8):
                    s, k = f.group(8), f.slot(8, 4)
                    pe.wait_ge(x_copied[k], 16 * (f.it - 1))
                    p = f.pair(8 + f.k % 2)
                    pe.wait_ge(rstd_done, (p + BEHIND + 1) * Rstd.STEPS)
                    for j in range(GRP):
                        i = pe.matmul(bk[:, MEAN_B, bass.ds(s * GRP + j, 1)], m.x_copy[:, k, j * D:(j + 1) * D],
                                      before_and_after(both.rstd, p, 1, GRP * (f.k % 2) + j, 1), start=True, stop=True)
                    i.then_inc(mean_done, 1)

            run_frames(pe, step, 8, 1)

        @block.scalar
        def _(act):
            def step(f):
                if f.live(0):
                    s, q = f.group(), f.slot(0, 2)
                    act.wait_ge(t_done, s + 1)
                    if f.past(0, 2):
                        act.wait_ge(wh_done, s - 1)
                    act.copy(m.zT[:, q, :], bk[:, T_B, :]).then_inc(zT_copied, 1)
                if f.live(4):
                    s, q = f.group(4), f.slot(4, 2)
                    act.wait_ge(o_done, s + 1)
                    act.wait_ge(rden_done, s + 1)
                    if f.past(4, 2):
                        act.wait_ge(x_done, s - 1)
                    for j in range(GRP):
                        c = slice(j * D, (j + 1) * D)
                        i = act.activation(m.h_s[:, q, c], bk[:, O_B + q, c], ACT.Relu,
                                           scale=m.rden[:, q, j:j + 1])
                    i.then_inc(h_done, 1)
                if f.live(3):
                    s, q = f.group(3), f.slot(3, 2)
                    act.wait_ge(pt_done, s + 1)
                    if f.past(3, 2):
                        act.wait_ge(o_done, s - 1)
                    act.copy(m.pT[:, q, :], bk[:, PT_B, :]).then_inc(pT_copied, 1)
                if f.live(2):
                    s, q = f.group(2), f.slot(2, 2)
                    act.wait_ge(l_ready, s + 1)
                    if f.past(2, 2):
                        act.wait_ge(pt_done, s - 1)
                    if f.past(2, 2):
                        act.wait_ge(rden_done, s - 1)
                    softmax_rows(act, m, q, p_ready, m.sums)
                if f.live(1):
                    s, k = f.group(1), f.slot(1, 4)
                    act.wait_ge(wh_done, s + 1)
                    if f.past(1, 4):
                        act.wait_ge(o_done, s - 3)
                    act.copy(m.xv[:, k, :, D:2 * D], by_graph(bk[:, WH_B, :])).then_inc(wh_copied, 1)

            run_frames(act, step, 4, 4)

        @block.vector
        def _(v):
            def step(f):
                def chain(*ns):
                    before = f.live(f.k % 2) and f.past(f.k % 2, 2)
                    after = f.live(2 * BEHIND + f.k % 2)
                    if before or after:
                        cols = slice(0 if before else 2 * GRP, 4 * GRP if after else 2 * GRP)
                        p = f.pair(f.k % 2)
                        here = bass.ds(p * (4 * GRP) + cols.start, cols.stop - cols.start)
                        for n in ns:
                            rstd.step(n, p, both.rstd[:, here], both.shift[:, here], cols=cols)

                if f.k % 2 == 0 and f.live(0) and f.past(0, 2):
                    p = f.pair()
                    v.wait_ge(rstd_done, p * Rstd.STEPS)
                    statistics(v, both.stats, m.X, f.group() * W, 0, stats_done)
                    statistics(v, both.stats, m.X, f.group() * W + W, 1, stats_done)
                    v.wait_ge(stats_done, 4 * (p + 1))
                if f.k % 2 == 0 and f.live(2 * BEHIND):
                    v.wait_ge(stats3_done, 4 * (f.pair(2 * BEHIND) + 1))
                    hold(v, m)
                if f.live(7):
                    s, q = f.group(7), f.slot(7, 2)
                    v.wait_ge(p_ready, s + 1)
                    if f.past(7, 2):
                        v.wait_ge(h_done, s - 1)
                    v.reciprocal(m.rden[:, q, :], m.sums[:, q, :]).then_inc(rden_done, 1)
                first = 7 * (f.k % 2)
                chain(first)
                if f.live(5):
                    s, q, k = f.group(5), f.slot(5, 2), f.slot(5, 4)
                    v.wait_ge(s_done, s + 1)
                    if f.past(5, 2):
                        v.wait_ge(l_ready, s - 1)
                    v.wait_ge(mask_in[k], 16 * (f.it - (f.k == 0)))
                    hold(v, m)
                    for j in range(GRP):
                        c = slice(j * D, (j + 1) * D)
                        v.tensor_tensor_reduce(m.t_s[:, q, c], bk[:, S_B + q, c], m.mask[:, k, c], 1.0, 3.0e38,
                                               ALU.add, ALU.min, m.nmin[:, q, j:j + 1]).then_inc(s_read, 1)
                        chain(first + 1 + j)
                    v.wait_ge(s_read, GRP * (s + 1))
                    if f.past(5, 2):
                        v.wait_ge(p_ready, s - 1)
                    v.scalar_tensor_tensor(m.nmax[:, q, :], m.nmin[:, q, :], SLOPE, m.nmin[:, q, :], ALU.mult, ALU.min)\
                     .then_inc(max_ready, 1)
                    v.scalar_tensor_tensor(m.l_s[:, q, :], m.t_s[:, q, :], SLOPE, m.t_s[:, q, :], ALU.mult, ALU.min)\
                     .then_inc(l_ready, 1)
                else:
                    chain(*range(first + 1, first + 5))
                chain(first + 5)
                if f.live(8):
                    s, q = f.group(8), f.slot(8, 2)
                    v.wait_ge(h_done, s + 1)
                    v.tensor_tensor(grp(m.X, s), grp(m.X, s), m.h_s[:, q, :], ALU.add).then_inc(x_done, 1)
                chain(first + 6)

                if f.k % 2 and f.live(2 * BEHIND - 1):
                    p = f.pair(2 * BEHIND - 1)
                    v.wait_ge(x_done, 2 * (p + 1))
                    v.wait_ge(rstd_done, (p + BEHIND) * Rstd.STEPS)
                    hold(v, m)
                    for u in range(2):
                        statistics(v, both.stats, m.X, f.group(2 * BEHIND - 1) * W + u * W, 2 + u, stats3_done)

            run_frames(v, step, 2 * BEHIND + 1, 4)
            v.wait_ge(mean_done, NG)
            v.tensor_copy(m.node_sums[:, :], bk[:, MEAN_B, 0:GRAPHS]).then_inc(mean_copied, 1)
            v.wait_ge(mean_copied, 1)


def expert_z(pool, m, s, pair, odd):
    rstd, shift = (before_and_after(t, pair, 1, GRP * odd, GRP) for t in (m.both.rstd, m.both.shift))
    make_z(pool, m, s, m.z[:, odd, :], rstd, shift, m.e_z_mul, m.e_z_ready)


def route(nc, m):
    with ExitStack() as ctx:
        s_pe = ctx.enter_context(nc.semaphore("r_product"))
        s_v = ctx.enter_context(nc.semaphore("r_vector"))
        s_act = ctx.enter_context(nc.semaphore("r_exp"))
        block = ctx.enter_context(nc.Block())
        bk = m.banks
        LG, LOAD, WT, B2 = bk[:, 0, 0:EXPERTS], bk[:, 1, 0:EXPERTS], bk[0:EXPERTS, 2, 0:D], bk[:, 3, 0:D]
        rows = m.l_s[:, 0, :].rearrange("p (r e) -> p r e", e=EXPERTS)
        ex, rw, scale, rw2, first, second, rest, dense, tmp = (rows[:, i, :] for i in range(9))
        cols = m.l_s[:, 1, :]
        nmax, total, rtotal, top1, top2, i1, i2, diff, e2, w_sum = (cols[:, i:i + 1] for i in range(10))
        i12, w12 = cols[:, 5:7], cols[:, 16:18]
        offsets = cols[:, 20:22]
        iota_less = rows[:, 10, :]
        OFFSETS, WEIGHTS = bk[0:1, 4, 0:TOPK * GRAPHS], bk[:, 5, 0:TOPK * GRAPHS]
        diagonals = m.h_s[:, 0, 0:TOPK * GRAPHS]
        dense_T = m.t_s[0:EXPERTS, 0, 0:D]
        b2_mix = m.t_s[:, 1, 0:D]

        @block.gpsimd
        def _(pool):
            for s in range(2):
                expert_z(pool, m, s, 0, s)

        @block.tensor
        def _(pe):
            pe.matmul(LG, m.node_sums[:, :], m.wr[:, :], start=True, stop=False)
            pe.matmul(LG, m.one_row[:, D:2 * D], m.br_row[:, :], start=False, stop=True).then_inc(s_pe, 1)
            pe.wait_ge(s_v, 4)
            pe.matmul(LOAD, m.ones[:, :], rw, start=True, stop=True).then_inc(s_pe, 1)
            pe.wait_ge(s_v, 23)
            for r in range(TOPK):
                pe.matmul(OFFSETS[:, r * GRAPHS:(r + 1) * GRAPHS], offsets[:, r:r + 1], m.ident, start=True, stop=True)
            pe.wait_ge(s_v, 28)
            pe.matmul(WEIGHTS, m.ones[:, :], diagonals, start=True, stop=True).then_inc(s_pe, 1)
            pe.wait_ge(s_v, 30)
            pe.transpose(WT, dense, m.ident).then_inc(s_pe, 1)
            pe.wait_ge(s_v, 33)
            pe.matmul(B2, dense_T, m.b2_rows[:, :], start=True, stop=True).then_inc(s_pe, 1)

        @block.scalar
        def _(act):
            act.wait_ge(s_v, 2)
            act.activation(ex, LG, ACT.Exp, bias=nmax, accum_out=total).then_inc(s_act, 1)
            act.wait_ge(s_v, 9)
            act.activation(ex, rw2, ACT.Exp, bias=nmax, accum_out=total).then_inc(s_act, 1)
            act.wait_ge(s_v, 18)
            act.activation(e2, diff, ACT.Exp).then_inc(s_act, 1)

        @block.vector
        def _(v):
            n = [0]

            def done(i):
                n[0] += 1
                i.then_inc(s_v, 1)
                v.wait_ge(s_v, n[0])

            done(v.tensor_scalar(iota_less, m.iota, float(EXPERTS), None, ALU.subtract))
            v.wait_ge(s_pe, 1)
            done(v.tensor_reduce(nmax, LG, AX.X, ALU.max, negate=True))
            v.wait_ge(s_act, 1)
            done(v.reciprocal(rtotal, total))
            done(v.tensor_scalar(rw, ex, rtotal, None, ALU.mult))
            v.wait_ge(s_pe, 2)
            done(v.tensor_scalar(scale, LOAD, float(P), None, ALU.mult))
            done(v.reciprocal(tmp, scale))
            done(v.tensor_scalar(scale, tmp, CAPACITY, 1.0, ALU.mult, ALU.min))
            done(v.tensor_tensor(rw2, rw, scale, ALU.mult))
            done(v.tensor_reduce(nmax, rw2, AX.X, ALU.max, negate=True))
            v.wait_ge(s_act, 2)
            done(v.reciprocal(rtotal, total))
            done(v.tensor_scalar(rw, ex, rtotal, None, ALU.mult))
            done(v.tensor_reduce(top1, rw, AX.X, ALU.max))
            done(v.scalar_tensor_tensor(tmp, rw, top1, iota_less, ALU.is_equal, ALU.mult))
            done(v.tensor_reduce(i1, tmp, AX.X, ALU.min))
            done(v.tensor_scalar(first, iota_less, i1, None, ALU.is_equal))
            done(v.scalar_tensor_tensor(rest, first, -4.0, rw, ALU.mult, ALU.add))
            done(v.tensor_reduce(top2, rest, AX.X, ALU.max))
            done(v.tensor_tensor(diff, top2, top1, ALU.subtract))
            assert n[0] == 18
            done(v.scalar_tensor_tensor(tmp, rest, top2, iota_less, ALU.is_equal, ALU.mult))
            done(v.tensor_reduce(i2, tmp, AX.X, ALU.min))
            done(v.tensor_scalar(second, iota_less, i2, None, ALU.is_equal))
            done(v.tensor_scalar(offsets, i12, float(EXPERTS), EXPERTS - 1.0, ALU.add, ALU.min))
            done(v.tensor_scalar(offsets, offsets, float(FF), None, ALU.mult))
            assert n[0] == 23
            v.wait_ge(s_act, 3)
            done(v.tensor_scalar(w_sum, e2, 1.0, None, ALU.add))
            done(v.reciprocal(w12[:, 0:1], w_sum))
            done(v.tensor_tensor(w12[:, 1:2], e2, w12[:, 0:1], ALU.mult))
            for r in range(TOPK):
                done(v.tensor_scalar(diagonals[:, r * GRAPHS:(r + 1) * GRAPHS], m.ident, w12[:, r:r + 1], None,
                                     ALU.mult))
            assert n[0] == 28
            done(v.tensor_scalar(tmp, first, w12[:, 0:1], None, ALU.mult))
            done(v.scalar_tensor_tensor(dense, second, w12[:, 1:2], tmp, ALU.mult, ALU.add))
            assert n[0] == 30
            v.wait_ge(s_pe, 3)
            done(v.tensor_copy(m.expert[:, :].rearrange("a (g r) -> a r g", r=TOPK),
                               OFFSETS.rearrange("a (r g) -> a r g", r=TOPK)))
            done(v.tensor_copy(m.weight[:, :].rearrange("p (g r) -> p r g", r=TOPK),
                               WEIGHTS.rearrange("p (r g) -> p r g", r=TOPK)))
            v.wait_ge(s_pe, 4)
            done(v.tensor_copy(dense_T, WT))
            v.wait_ge(s_pe, 5)
            done(v.tensor_copy(b2_mix, B2))
            done(v.tensor_tensor(m.shift_beta[:, :], m.beta[:, :], m.gamma[:, :], ALU.subtract))

        @block.sync
        def _(sp):
            sp.wait_ge(s_v, 34)
            sp.dma_start(m.d_b2, b2_mix).then_inc(m.b2_kept, 16)


def expert_columns(nc, m, eng, first, count):
    _, values = nc.values_load_multi_w_load_instructions(
        m.expert[0:1, bass.ds(first, count)], engines=[eng.engine], min_val=0, max_val=(EXPERTS - 1) * FF,
        skip_runtime_bounds_check_because="route() clamps the numbers of the experts")
    return values


def experts(nc, m, out):
    with ExitStack() as ctx:
        def sem(name):
            return ctx.enter_context(nc.semaphore("e_" + name))

        w1_in = [sem(f"w1_in{i}") for i in range(2)]
        b2_in = [sem(f"b2_in{i}") for i in range(2)]
        stored = [sem(f"stored{i}") for i in range(4)]
        z_ready, r_ready, xb_ready = m.e_z_ready, sem("r_ready"), sem("xb_ready")
        t_done, zT_copied, w1_copied = sem("t_done"), sem("zT_copied"), sem("w1_copied")
        h_done, g_ready = sem("h_done"), sem("g_ready")
        y_done, y_first, y_used = sem("y_done"), sem("y_first"), sem("y_used")
        stats_done, rstd_done = sem("stats_done"), sem("rstd_done")
        f_ready, fg_mul, out_ready = sem("f_ready"), sem("fg_mul"), sem("out_ready")
        rstd = Rstd(nc, m, rstd_done)
        bk = m.banks
        T_B, H_B, Y_B = 0, 1, 3
        w2 = m.w2x[:, :, :, :].rearrange("p e c d -> p (e c d)")
        w1 = m.w1x[:, :, :].rearrange("p e f -> p (e f)")
        CH = FF // P
        block = ctx.enter_context(nc.Block())

        @block.sync
        def _(sp):
            sp.wait_ge(m.b2_kept, 16)

            def step(f):
                if f.live(0):
                    s, q = f.group(), f.slot(0, 2)
                    if f.past(0, 2):
                        sp.wait_ge(h_done, GRP * (s - 1))
                        hold(sp, m)
                    if f.past(0, 1):
                        e = expert_columns(nc, m, sp, s * (GRP * TOPK), GRP * TOPK)
                        for n in range(1, GRP * TOPK, TOPK):
                            sp.dma_start(m.w1_top[:, q, n, :], w1[:, bass.ds(e[n], FF)]).then_inc(w1_in[q], 16)
                    if f.past(0, 2):
                        sp.wait_ge(r_ready, s - 1)
                    sp.dma_start(m.b2_all[:, q, :], m.d_b2[bass.ds(s * GRP, GRP), :].rearrange("g d -> (g d)")
                                 .partition_broadcast(P)).then_inc(b2_in[q], 16)
                if f.live(8):
                    s, k = f.group(8), f.slot(8, 4)
                    sp.wait_ge(out_ready, s + 1)
                    hold(sp, m)
                    sp.dma_start(out[bass.ds(s * GRP, GRP), :, :].rearrange("g n d -> n g d"),
                                 by_graph(m.out_s[:, k, :])).then_inc(stored[k], 16)

            run_frames(sp, step, 8, 2)
            for k in range(4):
                sp.wait_ge(stored[k], 16 * (NG // 4))

        @block.gpsimd
        def _(pool):
            def step(f):
                if f.live(0):
                    s, q = f.group(), f.slot(0, 2)
                    if f.past(0, 2):
                        pool.wait_ge(t_done, s - 1)
                        pool.wait_ge(r_ready, s - 1)
                        expert_z(pool, m, s, f.pair(f.k % 2), q)
                    pool.wait_ge(z_ready, s + 1)
                    pool.wait_ge(b2_in[q], 16 * (2 * f.it + f.k // 2 + 1))
                    if f.past(0, 4):
                        pool.wait_ge(y_used, GRP * (s - 3))
                    pool.tensor_tensor(m.r_s[:, f.slot(0, 4), :], m.z[:, q, :], m.b2_all[:, q, :], ALU.add)\
                        .then_inc(r_ready, 1)
                if f.live(5):
                    s, k = f.group(5), f.slot(5, 4)
                    if f.past(5, 4):
                        pool.wait_ge(out_ready, s - 3)
                    pool.tensor_tensor(by_graph(m.xb_s[:, k, :]), by_graph(grp(m.X, s)),
                                       m.shift_beta[:, :].unsqueeze(1).to_broadcast([P, GRP, D]), ALU.add)\
                        .then_inc(xb_ready, 1)

            run_frames(pool, step, 5, 4)

        @block.tensor
        def _(pe):
            def hidden(f, j):
                s, q = f.group(1), f.slot(1, 2)
                if j == 0:
                    pe.wait_ge(zT_copied, s + 1)
                    if f.past(1, 1):
                        pe.wait_ge(w1_in[q], 16 * GRP * (2 * f.it + (f.k - 1) // 2 + q))
                    pe.wait_ge(w1_copied, s + 1)
                if j >= 2 or f.past(1, 1):
                    pe.wait_ge(g_ready, GRP * s + j - 1)
                for n in range(TOPK * CH):
                    i = pe.matmul(bk[:, H_B + j % 2, n * P:(n + 1) * P],
                                  m.w1_top[:, q, TOPK * j + n // CH, (n % CH) * P:(n % CH + 1) * P],
                                  m.zT[:, q, j * D:(j + 1) * D], start=True, stop=True)
                i.then_inc(h_done, 1)

            def outputs(f, lag, j):
                s = f.group(lag)
                e = expert_columns(nc, m, pe, s * (GRP * TOPK) + TOPK * j, TOPK)
                pe.wait_ge(g_ready, GRP * s + j + 1)
                if f.past(lag, 1):
                    pe.wait_ge(y_used, GRP * (s - 1) + j + 1)
                for n in range(TOPK):
                    for c in range(CH):
                        i = pe.matmul(bk[:, Y_B + j, n * D:(n + 1) * D],
                                      m.g_s[:, j % 2, (n * CH + c) * P:(n * CH + c + 1) * P],
                                      w2[:, bass.ds(e[n] + c * D, D)], start=c == 0, stop=c == CH - 1)
                i.then_inc(y_done, 1)

            def step(f):
                if f.live(1):
                    hidden(f, 0)
                if f.live(2):
                    outputs(f, 2, 3)
                if f.live(1):
                    hidden(f, 1)
                    outputs(f, 1, 0)
                    hidden(f, 2)
                    outputs(f, 1, 1)
                if f.live(0):
                    s, q = f.group(), f.slot(0, 2)
                    pe.wait_ge(z_ready, s + 1)
                    if f.past(0, 1):
                        pe.wait_ge(zT_copied, s)
                    transpose_graphs(pe, bk[:, T_B, :], m.z[:, q, :], m.ident, t_done)
                if f.live(1):
                    hidden(f, 3)
                    outputs(f, 1, 2)

            run_frames(pe, step, 2, 2)

        @block.scalar
        def _(act):
            def step(f):
                def normalise(j):
                    if f.live(5):
                        s, k = f.group(5), f.slot(5, 4)
                        p, r, odd = f.pair(6 - f.k % 2), k // 2, k % 2
                        if j == 0:
                            act.wait_ge(rstd_done, (p + 1) * Rstd.STEPS)
                            if f.past(5, 4):
                                act.wait_ge(out_ready, s - 3)
                        c = slice(j * D, (j + 1) * D)
                        act.activation(m.f_s[:, k, c], m.o_s[:, k, c], ACT.Identity,
                                       bias=m.shift[:, r, GRP * odd + j:GRP * odd + j + 1],
                                       scale=m.rstd[:, r, GRP * odd + j:GRP * odd + j + 1]).then_inc(f_ready, 1)

                def copy_zT():
                    if f.live(0):
                        s, q = f.group(), f.slot(0, 2)
                        act.wait_ge(t_done, s + 1)
                        if f.past(0, 2):
                            act.wait_ge(h_done, GRP * (s - 1))
                        act.copy(m.zT[:, q, :], bk[:, T_B, :]).then_inc(zT_copied, 1)

                for j in range(GRP):
                    if j == GRP - 1:
                        copy_zT()
                    if f.live(1):
                        s = f.group(1)
                        act.wait_ge(h_done, GRP * s + j + 1)
                        if j >= 2 or f.past(1, 1):
                            act.wait_ge(y_done, GRP * s + j - 1)
                        act.activation(m.g_s[:, j % 2, :], bk[:, H_B + j % 2, :], ACT.Gelu).then_inc(g_ready, 1)
                    if j:
                        normalise(j - 1)
                    if j == GRP - 1:
                        normalise(j)

            run_frames(act, step, 5, 4)

        @block.vector
        def _(v):
            def first_experts(s, q, past, ranks=1):
                e = expert_columns(nc, m, v, s * (GRP * TOPK), GRP * TOPK)
                if past:
                    v.wait_ge(h_done, GRP * (s - 1))
                    hold(v, m)
                for j in range(GRP):
                    for n in range(TOPK * j, TOPK * j + ranks):
                        i = v.tensor_copy(m.w1_top[:, q, n, :], w1[:, bass.ds(e[n], FF)])
                i.then_inc(w1_copied, 1)

            def step(f):
                def chain(*ns):
                    lag = 2 + f.k % 2
                    if f.live(lag):
                        r = ((f.k - lag) // 2) % 2
                        for n in ns:
                            rstd.step(n, f.pair(lag), m.rstd[:, r, :], m.shift[:, r, :])

                if f.live(-1):
                    first_experts(f.group(-1), f.slot(-1, 2), f.past(-1, 2))
                if f.k % 2 == 0 and f.live(2):
                    p = f.pair(2)
                    if f.past(2, 2):
                        v.wait_ge(rstd_done, p * Rstd.STEPS)
                    v.wait_ge(y_used, 2 * GRP * (p + 1))
                    hold(v, m)
                    for u in range(2):
                        statistics(v, m.stats, m.o_s[:, f.slot(2 - u, 4), :], 0, u, stats_done)
                    v.wait_ge(stats_done, 4 * (p + 1))
                if f.k % 2 and f.past(3, 4):
                    v.wait_ge(f_ready, GRP * (2 * f.pair(3) - 2))
                first = 7 * (f.k % 2)
                chain(first)
                if f.live(0):
                    s, k = f.group(), f.slot(0, 4)
                    v.wait_ge(r_ready, s + 1)

                    def second(j):
                        c = slice(j * D, (j + 1) * D)
                        v.wait_ge(y_first, GRP * s + j + 1)
                        if f.past(0, 4):
                            v.wait_ge(f_ready, GRP * (s - 4) + j + 1)
                        v.scalar_tensor_tensor(m.o_s[:, k, c], bk[:, Y_B + j, D:2 * D],
                                               m.weight[:, bass.ds(s * (GRP * TOPK) + TOPK * j + 1, 1)], m.y_s[:, j, :],
                                               ALU.mult, ALU.add).then_inc(y_used, 1)

                    for j in range(GRP):
                        c = slice(j * D, (j + 1) * D)
                        v.wait_ge(y_done, GRP * s + j + 1)
                        if f.past(0, 1):
                            v.wait_ge(y_used, GRP * (s - 1) + j + 1)
                        v.scalar_tensor_tensor(m.y_s[:, j, :], bk[:, Y_B + j, 0:D],
                                               m.weight[:, bass.ds(s * (GRP * TOPK) + TOPK * j, 1)], m.r_s[:, k, c],
                                               ALU.mult, ALU.add).then_inc(y_first, 1)
                        chain(first + 1 + j)
                        if j:
                            second(j - 1)
                    second(GRP - 1)
                else:
                    chain(*range(first + 1, first + 5))
                chain(first + 5)
                if f.live(6):
                    s, q, k = f.group(6), f.slot(6, 4), f.slot(6, 4)
                    v.wait_ge(f_ready, GRP * (s + 1))
                    v.wait_ge(xb_ready, s + 1)
                    v.tensor_tensor(by_graph(m.f_s[:, q, :]), by_graph(m.f_s[:, q, :]),
                                    m.gamma[:, :].unsqueeze(1).to_broadcast([P, GRP, D]), ALU.mult).then_inc(fg_mul, 1)
                    chain(first + 6)
                    v.wait_ge(fg_mul, s + 1)
                    if f.past(6, 4):
                        v.wait_ge(stored[k], 16 * (f.it - 1 - (f.k < 2)))
                    v.tensor_tensor(m.out_s[:, k, :], m.f_s[:, q, :], m.xb_s[:, k, :], ALU.add)\
                     .then_inc(out_ready, 1)
                else:
                    chain(first + 6)

            first_experts(0, 0, False, ranks=TOPK)
            run_frames(v, step, 6, 4, ahead=1)


def kernel_program(nc, a, out):
    with ExitStack() as ctx:
        def sb(name, shape, dt=F32):
            return ctx.enter_context(nc.sbuf_tensor("sb_" + name, shape, dt))

        m = Memory()
        m.X = sb("X", [P, GRAPHS * D])
        m.MASK = sb("MASK", [P, GRAPHS * D], BF16)
        m.adj_in = sb("adj_in", [P, 4, W], I32)
        m.mask = sb("mask", [P, 4, W], BF16)
        m.z, m.zT, m.uT = (sb(name, [P, 2, W]) for name in ("z", "zT", "uT"))
        m.t_s = sb("t_s", [P, 2, W])
        m.l_s = sb("l_s", [P, 2, W])
        m.p_s = sb("p_s", [P, 2, W])
        m.pT = sb("pT", [P, 2, W])
        m.h_s, m.e_s = (sb(name, [P, 2, W]) for name in ("h_s", "e_s"))
        m.xv = sb("xv", [P, 4, GRP, 2 * D + 1])
        m.stats = sb("stats", [P, 8, 3])
        m.var, m.nhv, m.ra, m.rb, m.rt = (sb(name, [P, 8]) for name in ("var", "nhv", "ra", "rb", "rt"))
        m.seed = sb("seed", [P, 8], I32)
        m.rstd = sb("rstd", [P, 2, 8])
        m.shift = sb("shift", [P, 2, 8])
        m.rstd01 = sb("rstd01", [P, GRAPHS])
        m.shift01 = sb("shift01", [P, GRAPHS])
        m.nmin, m.nmax, m.sums, m.rden = (sb(name, [P, 2, GRP]) for name in ("nmin", "nmax", "sums", "rden"))
        m.consts = sb("consts", [P, 2 * D + EXPERTS])
        m.ident, m.centre, m.iota = m.consts[:, 0:D], m.consts[:, D:2 * D], m.consts[:, 2 * D:]
        m.ones = sb("ones", [P, D])
        m.one_row = sb("one_row", [1, 2 * D])
        m.m_w = sb("m_w", [P, D])
        m.wf, m.wc = sb("wf", [P, D]), sb("wc", [P, D])
        m.src_w, m.dst_w = sb("src_w", [P, D]), sb("dst_w", [P, D])
        m.gamma, m.beta = sb("gamma", [P, D]), sb("beta", [P, D])
        m.w12 = sb("w12", [P, 2 * D])
        m.wr = sb("wr", [P, EXPERTS])
        m.br_row = sb("br_row", [1, EXPERTS])
        m.bias_less = sb("bias_less", [1, D])
        m.b2_rows = sb("b2_rows", [EXPERTS, D])
        m.w1x = sb("w1x", [P, EXPERTS, FF])
        m.w2x = sb("w2x", [P, EXPERTS, FF // P, D])
        floats = m.MASK[:, :].bitcast(F32)
        m.raw = [floats[:, i * D:(i + 1) * D] for i in range(6)]
        m.w12_in = floats[:, D:3 * D]
        m.banks = ctx.enter_context(nc.psum_tensor("banks", [P, 8, W], F32))
        m.node_sums = sb("node_sums", [P, GRAPHS])
        m.x_copy = sb("x_copy", [P, 4, W])
        m.b1 = m.x_copy[:, :, :].rearrange("p q n -> p (q n)")
        m.both = Memory()
        mb, n_runs = m.both, NG // 2 + BEHIND
        mb.var, mb.nhv, mb.ra, mb.rb, mb.rt = (sb(name + "_both", [P, 4 * GRP])
                                               for name in ("var", "nhv", "ra", "rb", "rt"))
        mb.stats, mb.seed = sb("stats_both", [P, 4 * GRP, 3]), sb("seed_both", [P, 4 * GRP], I32)
        mb.rstd, mb.shift = sb("rstd_both", [P, n_runs * 4 * GRP]), sb("shift_both", [P, n_runs * 4 * GRP])
        m.held = {eng: ctx.enter_context(nc.semaphore(f"held{i}")) for i, eng in enumerate((nc.vector, nc.sync))}
        m.shift_beta = sb("shift_beta", [P, D])
        m.expert = sb("expert", [1, GRAPHS * TOPK], I32)
        m.weight = sb("weight", [P, GRAPHS * TOPK])
        m.d_b2 = nc.dram_tensor("d_b2", (GRAPHS, D), F32, kind="Internal").ap()
        m.z_lin = m.adj_in[:, :, :].bitcast(F32)
        m.zT_lin = [t[:, q, :] for t in (m.zT, m.pT) for q in range(2)]
        m.w1_top = floats[:, 0:2 * GRP * TOPK * FF].rearrange("p (q n f) -> p q n f", q=2, n=GRP * TOPK)
        m.g_s, m.b2_all = m.uT, m.e_s
        m.y_s = m.t_s[:, 0, :].rearrange("p (j d) -> p j d", j=GRP)
        m.o_s = floats[:, 2 * GRP * TOPK * FF:2 * GRP * TOPK * FF + 4 * W].rearrange("p (k w) -> p k w", k=4)
        xv = m.xv[:, :, :, :].rearrange("p a g n -> p (a g n)")
        m.r_s, m.f_s = (xv[:, i * 4 * W:(i + 1) * 4 * W].rearrange("p (k w) -> p k w", k=4) for i in range(2))
        m.xb_s = m.x_copy
        m.out_s = m.adj_in[:, :, :].bitcast(F32)
        m.four = Memory()
        m4 = m.four
        m4.var, m4.nhv, m4.ra, m4.rb, m4.rt = (sb(name + "4", [P, UN * GRP])
                                               for name in ("var", "nhv", "ra", "rb", "rt"))
        m4.seed = sb("seed4", [P, UN * GRP], I32)
        m.all_stats = sb("all_stats", [P, GRAPHS, 3])
        m.small = ctx.enter_context(nc.semaphore("small"))
        m.f_stats_done, m.f_rstd_done = (ctx.enter_context(nc.semaphore("f_" + name))
                                         for name in ("stats_done", "rstd_done"))
        m.b_stats_done, m.b_rstd_done = (ctx.enter_context(nc.semaphore("b_" + name))
                                         for name in ("stats_done", "rstd_done"))
        m.e_z_mul, m.e_z_ready = (ctx.enter_context(nc.semaphore("e_" + name)) for name in ("z_mul", "z_ready"))
        m.b2_kept = ctx.enter_context(nc.semaphore("b2_kept"))
        m.experts_in = ctx.enter_context(nc.semaphore("experts_in"))
        m.x_in = [ctx.enter_context(nc.semaphore(f"x_in{i}")) for i in range(4)]
        make_weights(nc, m, a)
        layer0(nc, m, a)
        linear(nc, m)
        layer1(nc, m)
        route(nc, m)
        experts(nc, m, out)


def kernel(**inputs):
    import numpy as np
    import concourse.bacc as bacc
    from concourse.bass_utils import run_bass_kernel_spmd

    arrays = {name: np.ascontiguousarray(v) for name, v in inputs.items()}
    arrays["consts"] = np.concatenate([np.eye(D), np.eye(D) - 1 / D, np.tile(np.arange(EXPERTS), (P, 1))], 1)\
        .astype(np.float32)
    arrays["one_row"] = np.concatenate([np.full((1, D), 1 / D), np.ones((1, D))], 1).astype(np.float32)
    nc = bacc.Bacc("TRN2", target_bir_lowering=False, num_devices=1)
    a = {name: nc.dram_tensor(f"in_{name}", v.shape, mybir.dt.from_np(v.dtype), kind="ExternalInput").ap()
         for name, v in arrays.items()}
    out = nc.dram_tensor("out_x", (GRAPHS, P, D), F32, kind="ExternalOutput").ap()
    kernel_program(nc, a, out)
    r = run_bass_kernel_spmd(nc, [{f"in_{name}": v for name, v in arrays.items()}], core_ids=[0])
    return r.results[0]["out_x"]
```
